# Optimizing a Trainium2 kernel written in Bass

```python
import numpy as np
import jax
import jax.numpy as jnp

def _softmax(x, axis=-1):
    return jax.nn.softmax(x, axis=axis)

def _gelu(x):
    return jax.nn.gelu(x, approximate=True)

def _silu(x):
    return jax.nn.silu(x)

def _sigmoid(x):
    return jax.nn.sigmoid(x)

def _layernorm(x, axis=-1, eps=1e-05):
    m = jnp.mean(x, axis=axis, keepdims=True)
    v = jnp.var(x, axis=axis, keepdims=True)
    return (x - m) / jnp.sqrt(v + eps)

def _scatter_add(tgt, idx, src, axis=0):
    return tgt.at[idx].add(src)

def _segment_sum(src, seg, n):
    return jax.ops.segment_sum(src, seg, n)
kernel_name = 'mk_gnn_resnorm_d2_gnn_r64_dd279e'

def setup_inputs(seed: int=0):
    np.random.seed(seed)
    _w = jnp.asarray

    def _rec_inputs():
        import jax
        import jax.numpy as jnp
        _gk = jax.random.key(seed)
        x = -0.0002117 + 1 * jax.random.normal(jax.random.fold_in(_gk, 1), (10000, 512), jnp.float32)
        src = jax.random.randint(jax.random.fold_in(_gk, 2), (5000,), 0, 10000, jnp.int32)
        dst = jnp.minimum((10000 * jax.random.uniform(jax.random.fold_in(_gk, 3), (5000,)) ** 2.0).astype(jnp.int32), 9999)
        _o = jnp.argsort(dst, stable=True)
        src = src[_o]
        dst = dst[_o]
        edge_type_2 = jax.random.randint(jax.random.fold_in(_gk, 12), (5000,), 0, 2, jnp.int32)
        return (x, src, dst, edge_type_2)
    x, src, dst, edge_type_2 = _rec_inputs()

    def _L0_gnn_setup():
        import jax, jax.numpy as jnp
        import numpy as np
        N_NODES = 50000
        N_EDGES = 150000
        D_IN = 512
        D_OUT = 512
        LN_EPS = 1e-05
        key = jax.random.key(seed)
        k_x, k_e, k_ws, k_wn = jax.random.split(key, 4)
        x = jax.random.normal(k_x, (N_NODES, D_IN), dtype=jnp.float32)
        edge_index = jax.random.randint(k_e, (2, N_EDGES), 0, N_NODES, dtype=jnp.int64)
        scale = 1.0 / np.sqrt(D_IN)
        w_self = jax.random.normal(k_ws, (D_OUT, D_IN), dtype=jnp.float32) * scale
        w_neigh = jax.random.normal(k_wn, (D_OUT, D_IN), dtype=jnp.float32) * scale
        bias = jnp.zeros((D_OUT,), dtype=jnp.float32)
        gamma = jnp.ones((D_OUT,), dtype=jnp.float32)
        beta = jnp.zeros((D_OUT,), dtype=jnp.float32)
        return {'x': x, 'edge_index': edge_index, 'w_self': w_self, 'w_neigh': w_neigh, 'bias': bias, 'gamma': gamma, 'beta': beta}
    _L0_gnn_all = _L0_gnn_setup()
    _L0_gnn_in = {k: v for k, v in _L0_gnn_all.items() if k in ('w_self', 'w_neigh', 'bias', 'gamma', 'beta')}
    del _L0_gnn_all

    def _L1_gnn_setup():
        import jax, jax.numpy as jnp
        import numpy as np
        NUM_RELATIONS = 2
        NUM_BASES = 30
        HIDDEN = 512
        N_NODES = 10000
        N_EDGES = 2500

        def rgcn_gate_layer(x, row, col, edge_type, basis, att, gate_w, root, bias):
            H = x.shape[1]
            w = jnp.einsum('rb,bio->rio', att, basis)
            x_j = x[col]
            msgs = []
            for r in range(NUM_RELATIONS):
                gate = jax.nn.sigmoid(x_j @ gate_w[r, :, 0])
                msgs.append(gate[:, None] * x_j @ w[r])
            msg = jnp.where((edge_type == 0)[:, None], msgs[0], msgs[1])
            agg = jax.ops.segment_sum(msg, row, num_segments=x.shape[0])
            return agg + x @ root + bias
        key = jax.random.key(seed)
        ks = jax.random.split(key, 16)
        H, R, B = (HIDDEN, NUM_RELATIONS, NUM_BASES)
        bound = 1.0 / np.sqrt(B * H)
        u = lambda k, shape: jax.random.uniform(k, shape, jnp.float32, -bound, bound)
        inp = {'x': jax.random.normal(ks[0], (N_NODES, H), jnp.float32), 'edge_index': jax.random.randint(ks[1], (2, N_EDGES), 0, N_NODES, jnp.int32), 'edge_type': jax.random.randint(ks[2], (N_EDGES,), 0, R, jnp.int32), 'basis1': u(ks[3], (B, H, H)), 'att1': u(ks[4], (R, B)), 'gate_w1': u(ks[5], (R, H, 1)), 'root1': u(ks[6], (H, H)), 'bias1': u(ks[7], (H,)), 'basis2': u(ks[8], (B, H, H)), 'att2': u(ks[9], (R, B)), 'gate_w2': u(ks[10], (R, H, 1)), 'root2': u(ks[11], (H, H)), 'bias2': u(ks[12], (H,))}
        return inp
    _L1_gnn_all = _L1_gnn_setup()
    _L1_gnn_in = {k: v for k, v in _L1_gnn_all.items() if k in ('basis1', 'att1', 'gate_w1', 'root1', 'bias1', 'basis2', 'att2', 'gate_w2', 'root2', 'bias2')}
    del _L1_gnn_all
    return {'x': x, 'src': src, 'dst': dst, 'edge_type_2': edge_type_2, 'L0_gnn_w_self': _L0_gnn_in['w_self'], 'L0_gnn_w_neigh': _L0_gnn_in['w_neigh'], 'L0_gnn_bias': _L0_gnn_in['bias'], 'L0_gnn_gamma': _L0_gnn_in['gamma'], 'L0_gnn_beta': _L0_gnn_in['beta'], 'L1_gnn_basis1': _L1_gnn_in['basis1'], 'L1_gnn_att1': _L1_gnn_in['att1'], 'L1_gnn_gate_w1': _L1_gnn_in['gate_w1'], 'L1_gnn_root1': _L1_gnn_in['root1'], 'L1_gnn_bias1': _L1_gnn_in['bias1'], 'L1_gnn_basis2': _L1_gnn_in['basis2'], 'L1_gnn_att2': _L1_gnn_in['att2'], 'L1_gnn_gate_w2': _L1_gnn_in['gate_w2'], 'L1_gnn_root2': _L1_gnn_in['root2'], 'L1_gnn_bias2': _L1_gnn_in['bias2']}

def reference(x, src, dst, edge_type_2, L0_gnn_w_self, L0_gnn_w_neigh, L0_gnn_bias, L0_gnn_gamma, L0_gnn_beta, L1_gnn_basis1, L1_gnn_att1, L1_gnn_gate_w1, L1_gnn_root1, L1_gnn_bias1, L1_gnn_basis2, L1_gnn_att2, L1_gnn_gate_w2, L1_gnn_root2, L1_gnn_bias2):
    import jax
    import jax.numpy as jnp

    def _L0_gnn_ref(x, edge_index, w_self, w_neigh, bias, gamma, beta):
        import jax, jax.numpy as jnp
        import numpy as np
        N_NODES = 50000
        N_EDGES = 150000
        D_IN = 512
        D_OUT = 512
        LN_EPS = 1e-05
        n = x.shape[0]
        s, d = (edge_index[0], edge_index[1])
        agg = jax.ops.segment_sum(x[s], d, num_segments=n)
        cnt = jax.ops.segment_sum(jnp.ones(s.shape[0], x.dtype), d, num_segments=n)
        agg = agg / jnp.maximum(cnt, 1.0)[:, None]
        h = x @ w_self.T + agg @ w_neigh.T + bias
        mu = jnp.mean(h, axis=-1, keepdims=True)
        var = jnp.mean(jnp.square(h - mu), axis=-1, keepdims=True)
        hn = (h - mu) * jax.lax.rsqrt(var + LN_EPS) * gamma + beta
        return jax.nn.relu(hn)

    def _L1_gnn_ref(x, edge_index, edge_type, basis1, att1, gate_w1, root1, bias1, basis2, att2, gate_w2, root2, bias2):
        import jax, jax.numpy as jnp
        import numpy as np
        NUM_RELATIONS = 2
        NUM_BASES = 30
        HIDDEN = 512
        N_NODES = 10000
        N_EDGES = 2500

        def rgcn_gate_layer(x, row, col, edge_type, basis, att, gate_w, root, bias):
            H = x.shape[1]
            w = jnp.einsum('rb,bio->rio', att, basis)
            x_j = x[col]
            msgs = []
            for r in range(NUM_RELATIONS):
                gate = jax.nn.sigmoid(x_j @ gate_w[r, :, 0])
                msgs.append(gate[:, None] * x_j @ w[r])
            msg = jnp.where((edge_type == 0)[:, None], msgs[0], msgs[1])
            agg = jax.ops.segment_sum(msg, row, num_segments=x.shape[0])
            return agg + x @ root + bias
        row, col = (edge_index[0], edge_index[1])
        h = jax.nn.relu(rgcn_gate_layer(x, row, col, edge_type, basis1, att1, gate_w1, root1, bias1))
        out = rgcn_gate_layer(h, row, col, edge_type, basis2, att2, gate_w2, root2, bias2)
        return out
    edge_index = jnp.stack([src, dst])
    x = _layernorm(x + _L0_gnn_ref(x, edge_index, L0_gnn_w_self, L0_gnn_w_neigh, L0_gnn_bias, L0_gnn_gamma, L0_gnn_beta), axis=-1)
    x = _layernorm(x + _L1_gnn_ref(x, edge_index, edge_type_2, L1_gnn_basis1, L1_gnn_att1, L1_gnn_gate_w1, L1_gnn_root1, L1_gnn_bias1, L1_gnn_basis2, L1_gnn_att2, L1_gnn_gate_w2, L1_gnn_root2, L1_gnn_bias2), axis=-1)
    return x

_drawn_inputs = setup_inputs


def setup_inputs(seed=0):
    import zlib

    import numpy as np

    out = dict(_drawn_inputs(seed))
    spreads = {'L0_gnn_bias': (0.0, 0.1), 'L0_gnn_gamma': (1.0, 0.2), 'L0_gnn_beta': (0.0, 0.1)}
    factors = {'L1_gnn_basis1': 8.0,
     'L1_gnn_att1': 8.0,
     'L1_gnn_gate_w1': 40.414,
     'L1_gnn_root1': 8.0,
     'L1_gnn_bias1': 24.339,
     'L1_gnn_basis2': 8.0,
     'L1_gnn_att2': 8.0,
     'L1_gnn_gate_w2': 64.0,
     'L1_gnn_root2': 7.26,
     'L1_gnn_bias2': 8.0}
    for name, (base, spread) in spreads.items():
        noise = np.random.default_rng([zlib.crc32(name.encode()), seed]).standard_normal(out[name].shape)
        drawn = base * np.exp(spread * noise) if base else spread * noise
        out[name] = jnp.asarray(drawn.astype(out[name].dtype))
    for name, factor in factors.items():
        out[name] = (out[name] * factor).astype(out[name].dtype)
    return out
```

```python
from contextlib import ExitStack

import numpy as np

import concourse.bass as bass
from concourse import mybir

F32 = mybir.dt.float32
F32R = mybir.dt.float32r
BF16 = mybir.dt.bfloat16
I32 = mybir.dt.int32
ALU = mybir.AluOpType
ACT = mybir.ActivationFunctionType

P = 128
D = 512
KC = D // P
PAIR = 2 * P
LN_EPS = 1e-5
RELATIONS = 2

NODES = 10000
NODE_TILES = -(-NODES // P)
NODE_STEPS = -(-NODES // PAIR)
LAST_ROWS = NODES - (NODE_TILES - 1) * P

EDGES = 5000
ET = 40
EP = EDGES // ET
EDGE_STEPS_0 = -(-EDGES // PAIR)
EDGE_STEPS = EDGE_STEPS_0 + 1
POS_TILES = 2 * EDGE_STEPS
POSITIONS = POS_TILES * P
NO_EDGE = float(1 << 20)

BASES = 30
QUARTERS = 4
BP = BASES * QUARTERS
CHUNK_Q = 8
CHUNKS = P // CHUNK_Q
SORT_ITER = CHUNKS // 2
SORT_TILES = ET // SORT_ITER
CLASSES = (NODE_TILES, RELATIONS * NODE_TILES)
RING = 4


def wide(ap, n):
    return ap.unsqueeze(2).to_broadcast([ap.shape[0], ap.shape[1], n])


class Shared:
    pass


def clear(nc, sems):
    nums = sorted(s.num for s in sems)
    first = nums[0]
    for n, after in zip(nums, nums[1:] + [None]):
        if after != n + 1:
            nc.gpsimd.sem_clear(range(first, n + 1))
            first = after


def deep(ap, n):
    return ap.unsqueeze(1).to_broadcast([ap.shape[0], n, ap.shape[1]])


def prologue(nc, m):
    with ExitStack() as ctx:
        inner = ctx.enter_context(ExitStack())

        def sb(name, shape, dt):
            return ctx.enter_context(nc.sbuf_tensor(name, shape, dt))

        mine = []

        def sem(name):
            mine.append(ctx.enter_context(nc.semaphore(name)))
            return mine[-1]

        iota_row = sb("iota_row", [P, 160], F32)
        iota_part = sb("iota_part", [P, 1], F32)
        part_int = sb("part_int", [P, 1], I32)
        quarter = sb("quarter", [P, 1], F32)
        before_edge = sb("before_edge", [EP, EP], F32)
        below = sb("below", [P, P], F32)
        ones = sb("ones", [P, 160], F32)
        dst_i = sb("dst_i", [EP, ET], I32)
        src_i = sb("src_i", [EP, ET], I32)
        type_i = sb("type_i", [EP, ET], I32)
        type_f = sb("type_f", [EP, ET], F32)
        low_i = sb("low_i", [EP, ET], I32)
        high_i = sb("high_i", [EP, ET], I32)
        low = sb("low", [EP, ET], F32)
        klass = sb("klass", [EP, ET], F32)
        low_b = sb("low_b", [EP, ET], BF16)
        key = sb("key", [EP, ET], F32)
        pay = sb("pay", [EP, ET], F32)
        one_low = sb("one_low", [EP, ET, P], BF16)
        one_class = sb("one_class", [EP, ET, CLASSES[1]], BF16)
        low_row = sb("low_row", [P, EDGES], BF16)
        by_tile = sb("by_tile", [P, ET, P], BF16)
        low_T = by_tile[:, :, 0:EP]
        key_row = sb("key_row", [P, EDGES], F32)
        rank = sb("rank", [EP, ET], F32)
        base = sb("base", [EP, ET], F32)
        junk = sb("junk", [EP, 2, 160], F32)
        count_hi = sb("count_hi", [P, SORT_TILES, CLASSES[1]], BF16)
        count_lo = sb("count_lo", [P, SORT_TILES, CLASSES[1]], BF16)
        pos = sb("pos", [EP, ET], F32)
        pos_i = sb("pos_i", [EP, ET], I32)
        tile_i = sb("tile_i", [EP, ET], I32)
        slot_i = sb("slot_i", [EP, ET], I32)
        tile_f = sb("tile_f", [EP, ET], F32)
        slot_f = sb("slot_f", [EP, ET], F32)
        one_slot = by_tile[0:EP]
        one_tile = sb("one_tile", [EP, ET, POS_TILES], BF16)
        vals = sb("vals", [EP, 2, ET], F32)
        vals_hi = sb("vals_hi", [EP, 2, ET], BF16)
        vals_lo = sb("vals_lo", [EP, 2, ET], BF16)
        put = key_row[0:EP, 0:2 * ET * POS_TILES].bitcast(BF16).rearrange(
            "p (h t k u) -> p h t k u", h=2, t=ET, k=2)
        hist = sb("hist", [P, CLASSES[1]], F32)
        upto = sb("upto", [P, CLASSES[1]], F32)
        start = sb("start", [P, CLASSES[1]], F32)
        last = sb("last", [P, CLASSES[1]], F32)
        empty = sb("empty", [P, CLASSES[1]], F32)
        split_i = sb("split_i", [P, 2], I32)
        split_f = sb("split_f", [P, 3], F32)
        keys_out = sb("keys_out", [P, P], F32)
        keys_T = sb("keys_T", [POS_TILES, P], F32)
        keys_row = sb("keys_row", [P, POSITIONS], F32)
        att = sb("att", [BP, 2, RELATIONS], F32)
        is_quarter = sb("is_quarter", [BP, QUARTERS], F32)
        mix = sb("mix", [BP, 2, 32], F32)
        chunk = sb("chunk", [BP, 2, CHUNK_Q * D], F32)
        made = sb("made", [P, 2, 2, D], F32)
        bias_f = sb("bias_f", [P, 3, D], F32)

        ps = m.psum
        ps_count = ps[:, 0, :]
        ps_sums = ps[:, 1, :]
        ps_put = ps[:, 4, 0:2 * POS_TILES]
        ps_keys = ps[:, 5, 0:P]

        def ps_look(s, classes):
            return ps[0:EP, 2 + s // 3, (s % 3) * 160:(s % 3) * 160 + classes]

        edges_in = sem("edges_in")
        const_ready = sem("const_ready")
        pool_step = sem("pool_step")
        dve_step = sem("dve_step")
        keys_ready = sem("keys_ready")
        keys_stored = sem("keys_stored")
        rows_in = sem("rows_in")
        onehot_ready = sem("onehot_ready")
        hist_ready = sem("hist_ready")
        hist_copied = sem("hist_copied")
        sums_ready = sem("sums_ready")
        start_ready = sem("start_ready")
        counted = sem("counted")
        count_hi_ready = sem("count_hi_ready")
        count_ready = sem("count_ready")
        looked = sem("looked")
        put_ready = sem("put_ready")
        put_done = sem("put_done")
        keys_out_ready = sem("keys_out_ready")
        keys_turned = sem("keys_turned")
        keys_T_ready = sem("keys_T_ready")
        keys_T_stored = sem("keys_T_stored")
        keys_row_in = sem("keys_row_in")
        mask_done = sem("mask_done")
        att_in = sem("att_in")
        mix_ready = sem("mix_ready")
        chunk_in = [sem(f"chunk_in{i}") for i in range(2)]
        mixed = sem("mixed")
        bank_copied = sem("bank_copied")
        made_ready = sem("made_ready")
        made_stored = [sem(f"made_stored{i}") for i in range(2)]
        bias_in = sem("bias_in")
        bias_step = sem("bias_step")

        basis_rows = [b.rearrange("b (i q) o -> (b i) (q o)", i=QUARTERS) for b in m.basis]
        w_rows = [w.rearrange("r (i q) o -> (r i) q o", i=QUARTERS) for w in m.w_made]
        block = inner.enter_context(nc.Block())

        @block.sync
        def _(sp):
            sp.dma_start(dst_i[:], m.dst.rearrange("(p t) -> p t", t=ET)).then_inc(edges_in, 16)
            sp.dma_start(src_i[:], m.src.rearrange("(p t) -> p t", t=ET)).then_inc(edges_in, 16)
            sp.dma_start(type_i[:], m.edge_type.rearrange("(p t) -> p t", t=ET)).then_inc(edges_in, 16)
            for layer in range(2):
                sp.dma_start(att[:, layer, :], m.att[layer]).then_inc(att_in, 16)
            sp.wait_ge(bias_step, 1)
            for n, vec in enumerate(m.biases):
                sp.dma_start(bias_f[0:1, n, :], vec.unsqueeze(0)).then_inc(bias_in, 16)
                sp.dma_start(bias_f[32:33, n, :], vec.unsqueeze(0)).then_inc(bias_in, 16)
            sp.dma_start(m.gamma_b[:], m.gamma.partition_broadcast(P)).then_inc(bias_in, 16)
            sp.dma_start(m.beta_b[:], m.beta.partition_broadcast(P)).then_inc(bias_in, 16)
            for layer in range(2):
                sp.dma_start(m.gate_b[layer][:], m.gate_w[layer].rearrange("r h o -> (r h o)").partition_broadcast(P)
                             ).then_inc(bias_in, 16)

            for s in range(2):
                sp.wait_ge(keys_ready, s + 1)
                sp.dma_start(m.key_d[s].rearrange("(p t) -> p t", t=ET), key[:]).then_inc(keys_stored, 16)
                sp.dma_start(m.low_d[s].rearrange("(p t) -> p t", t=ET), low_b[:]).then_inc(keys_stored, 16)
                sp.wait_ge(keys_stored, 32 * (s + 1))
                sp.dma_start(low_row[:], m.low_d[s].partition_broadcast(P)).then_inc(rows_in, 16)
                sp.dma_start(key_row[:], m.key_d[s].partition_broadcast(P)).then_inc(rows_in, 16)
                with sp.Fori(0, SORT_ITER) as i:
                    for c in range(2):
                        sp.wait_ge(mixed, 4 * i + (4 * SORT_ITER * s + 2 * c + 2))
                        sp.dma_start(chunk[:, c, :],
                                     basis_rows[s][:, bass.ds((2 * i + c) * (CHUNK_Q * D), CHUNK_Q * D)]
                                     ).then_inc(chunk_in[c], 16)
                sp.wait_ge(keys_T_ready, s + 1)
                sp.dma_start(m.sorted_d[s].rearrange("(u v) -> u v", v=P), keys_T[:]).then_inc(keys_T_stored, 16)
                sp.wait_ge(keys_T_stored, 16 * (s + 1))
                if s:
                    sp.wait_ge(mask_done, s)
                sp.dma_start(keys_row[:], m.sorted_d[s].partition_broadcast(P)).then_inc(keys_row_in, 16)
            sp.wait_ge(made_stored[0], 64 * (2 * SORT_ITER + 1))
            sp.wait_ge(made_stored[1], 64 * (2 * SORT_ITER + 1))

        @block.gpsimd
        def _(pool):
            def chain(ins, n=[0]):
                n[0] += 1
                ins.then_inc(pool_step, 1)
                pool.wait_ge(pool_step, n[0])

            pool.iota(iota_row[:], pattern=[[1, 160]], base=0, channel_multiplier=0,
                      allow_small_or_imprecise_dtypes=True)
            pool.iota(iota_part[:], pattern=[[0, 1]], base=0, channel_multiplier=1,
                      allow_small_or_imprecise_dtypes=True)
            pool.iota(part_int[:], pattern=[[0, 1]], base=0, channel_multiplier=1)
            pool.memset(ones[:], 1.0)
            pool.memset(keys_out[:], 0.0)
            pool.memset(mix[:], 0.0)
            pool.memset(bias_f[:], 0.0).then_inc(bias_step, 1)
            pool.memset(m.ident[:], 0.0)
            chain(pool.memset(m.row_pick_f[:], 0.0))
            pool.memset(m.row_pick_f[0:1, :], 1.0)
            chain(pool.memset(m.row_pick_f[32:33, :], 1.0))
            pool.affine_select(out=m.ident[:], in_=m.ident[:], compare_op=ALU.not_equal, fill=1.0, base=0,
                               pattern=[[-1, P]], channel_multiplier=1)
            pool.affine_select(out=before_edge[:], in_=ones[0:EP, 0:EP], compare_op=ALU.is_gt, fill=0.0, base=0,
                               pattern=[[-1, EP]], channel_multiplier=1)
            pool.affine_select(out=below[:], in_=ones[:, 0:P], compare_op=ALU.is_gt, fill=0.0, base=0,
                               pattern=[[1, P]], channel_multiplier=-1).then_inc(const_ready, 1)

        @block.tensor
        def _(pe):
            pe.sem_inc(mixed, 4)
            pe.sem_inc(bank_copied, 2)

            def basis_chunk(i, s, c):
                pe.wait_ge(chunk_in[c], 16 * i + 16 * (SORT_ITER * s + 1))
                for g in range(2):
                    pe.wait_ge(bank_copied, 4 * i + (4 * SORT_ITER * s + 2 * c + g + 1))
                    for j in range(4):
                        q = 4 * g + j
                        done = nc.tensor.matmul(ps[32 * j:32 * j + 32, 6 + g, :], mix[:, s, :],
                                                chunk[:, c, q * D:(q + 1) * D], start=True, stop=True)
                    done.then_inc(mixed, 1)

            def histogram_tile(s, t, first=False):
                n = CLASSES[s]
                return nc.tensor.matmul(ps_count[:, 0:n],
                                        one_low[:, bass.ds(t, 1), :].rearrange("p a b -> p (a b)"),
                                        one_class[:, bass.ds(t, 1), 0:n].rearrange("p a b -> p (a b)"),
                                        start=first, stop=False, skip_group_check=True)

            pe.wait_ge(const_ready, 1)
            pe.wait_ge(mix_ready, 1)
            for s in range(2):
                n = CLASSES[s]
                pe.wait_ge(onehot_ready, s + 1)
                for t in range(4):
                    histogram_tile(s, t, t == 0)
                with pe.Fori(1, ET // 4 - 1) as j:
                    for t in range(4):
                        histogram_tile(s, 4 * j + t)
                for t in range(ET - 4, ET):
                    done = histogram_tile(s, t)
                done.then_inc(hist_ready, 1)
                pe.wait_ge(hist_copied, s + 1)
                nc.tensor.matmul(ps_sums[:, 0:n], below[:], hist[:, 0:n], start=True, stop=True)
                nc.tensor.matmul(ps_sums[:, 160:160 + n], ones[:, 0:P], hist[:, 0:n], start=True,
                                 stop=True).then_inc(sums_ready, 1)
                pe.wait_ge(start_ready, s + 1)
                nc.tensor.matmul(ps_count[:, 0:n], m.ident[:], start[:, 0:n], start=True, stop=False,
                                 skip_group_check=True).then_inc(counted, 1)
                with pe.Fori(0, SORT_ITER) as i:
                    for k in range(SORT_TILES):
                        t = SORT_TILES * i + k
                        pe.wait_ge(count_ready, SORT_TILES * i + (ET * s + k + 1))
                        look = ps_look(k, n)
                        turned = low_T[:, bass.ds(t, 1), :].rearrange("p a b -> p (a b)")
                        nc.tensor.matmul(look, turned, count_hi[:, k, 0:n], start=True, stop=False,
                                         skip_group_check=True)
                        nc.tensor.matmul(look, turned, count_lo[:, k, 0:n], start=False, stop=True,
                                         skip_group_check=True).then_inc(looked, 1)
                        histogram_tile(s, t).then_inc(counted, 1)
                        if k in (1, 3):
                            basis_chunk(i, s, k // 2)
                pe.wait_ge(put_ready, s + 1)

                def put_of(part, t):
                    return put[:, part, bass.ds(t, 1)].rearrange("p a b c -> p (a b c)")

                def put_tile(t, first=False):
                    slot = one_slot[:, bass.ds(t, 1), :].rearrange("p a b -> p (a b)")
                    nc.tensor.matmul(ps_put, slot, put_of(0, t),
                                     start=first, stop=False, skip_group_check=True)
                    return nc.tensor.matmul(ps_put, slot, put_of(1, t),
                                            start=False, stop=False, skip_group_check=True)

                for t in range(4):
                    put_tile(t, t == 0)
                with pe.Fori(1, ET // 4 - 1) as j:
                    for t in range(4):
                        put_tile(4 * j + t)
                for t in range(ET - 4, ET):
                    done = put_tile(t)
                done.then_inc(put_done, 1)
                pe.wait_ge(keys_out_ready, s + 1)
                nc.tensor.transpose(ps_keys, keys_out[:], m.ident[:]).then_inc(keys_turned, 1)

        @block.scalar
        def _(act):
            for c in range(2):
                act.sem_inc(made_stored[c], 64)
            for s in range(2):
                with act.Fori(0, SORT_ITER) as i:
                    for c in range(2):
                        act.wait_ge(made_stored[c], 64 * i + 64 * (SORT_ITER * s + 1))
                        for g in range(2):
                            act.wait_ge(mixed, 4 * i + (4 * SORT_ITER * s + 2 * c + g + 1 + 4))
                            nc.scalar.copy(made[:, c, g, :], ps[:, 6 + g, :]).then_inc(bank_copied, 1)
                        act.wait_ge(bank_copied, 4 * i + (4 * SORT_ITER * s + 2 * c + 2 + 2))
                        for j in range(4):
                            rows = w_rows[s][:, bass.ds(CHUNK_Q * (2 * i + c) + j, 2, 4), :]
                            act.dma_start(rows, made[32 * j:32 * j + 8, c]).then_inc(made_stored[c], 16)

        @block.vector
        def _(dve):
            v = nc.vector
            steps = [0]

            def chain(ins):
                steps[0] += 1
                ins.then_inc(dve_step, 1)
                dve.wait_ge(dve_step, steps[0])

            def mask(s):
                dve.wait_ge(keys_row_in, 16 * (s + 1))
                v.memset(m.same[s][:, 0:1], 0.0)
                v.tensor_tensor(m.same[s][:, 1:POSITIONS], keys_row[:, 1:POSITIONS], keys_row[:, 0:POSITIONS - 1],
                                ALU.is_equal).then_inc(mask_done, 1)

            dve.wait_ge(const_ready, 1)
            chain(v.tensor_scalar(part_int[:], part_int[:], QUARTERS - 1, None, ALU.bitwise_and))
            chain(v.tensor_copy(quarter[:], part_int[:]))
            chain(v.tensor_scalar(is_quarter[:], iota_row[0:BP, 0:QUARTERS], quarter[0:BP, 0:1], None, ALU.is_equal))
            dve.wait_ge(att_in, 32)
            for layer in range(2):
                for r in range(RELATIONS):
                    done = v.tensor_scalar(mix[:, layer, QUARTERS * r:QUARTERS * (r + 1)], is_quarter[:],
                                           att[:, layer, r:r + 1], None, ALU.mult)
            done.then_inc(mix_ready, 1)
            dve.wait_ge(edges_in, 48)
            for s in range(2):
                n = CLASSES[s]
                target, source = (dst_i, src_i) if s == 0 else (src_i, dst_i)
                v.tensor_scalar(low_i[:], target[:], P - 1, None, ALU.bitwise_and)
                v.tensor_scalar(high_i[:], target[:], 7, None, ALU.logical_shift_right)
                v.tensor_copy(type_f[:], type_i[:])
                chain(v.tensor_copy(pay[:], source[:]))
                v.tensor_copy(low[:], low_i[:])
                chain(v.tensor_copy(klass[:], high_i[:]))
                if s:
                    chain(v.scalar_tensor_tensor(out=klass[:], in0=type_f[:], scalar=float(NODE_TILES), in1=klass[:],
                                                 op0=ALU.mult, op1=ALU.add))
                v.tensor_copy(low_b[:], low[:])
                v.scalar_tensor_tensor(out=key[:], in0=klass[:], scalar=float(P), in1=low[:],
                                       op0=ALU.mult, op1=ALU.add).then_inc(keys_ready, 1)
                v.tensor_tensor(one_low[:], deep(iota_row[0:EP, 0:P], ET), wide(low[:], P), ALU.is_equal)
                v.tensor_tensor(one_class[:, :, 0:n], deep(iota_row[0:EP, 0:n], ET), wide(klass[:], n),
                                ALU.is_equal).then_inc(onehot_ready, 1)
                if s:
                    mask(0)
                dve.wait_ge(hist_ready, s + 1)
                v.tensor_copy(hist[:, 0:n], ps_count[:, 0:n]).then_inc(hist_copied, 1)
                dve.wait_ge(sums_ready, s + 1)
                chain(v.tensor_tensor_scan(upto[:, 0:n], ones[:, 0:n], ps_sums[:, 160:160 + n], 0.0,
                                           ALU.mult, ALU.add))
                chain(v.tensor_tensor(start[:, 0:n], upto[:, 0:n], ps_sums[:, 160:160 + n], ALU.subtract))
                chain(v.tensor_tensor(start[:, 0:n], start[:, 0:n], ps_sums[:, 0:n], ALU.add))
                if s:
                    chain(v.tensor_scalar(split_f[:, 0:1], upto[:, NODE_TILES - 1:NODE_TILES], float(PAIR - 1), None,
                                          ALU.add))
                    chain(v.tensor_copy(split_i[:, 0:1], split_f[:, 0:1]))
                    chain(v.tensor_scalar(split_i[:, 0:1], split_i[:, 0:1], 8, None, ALU.logical_shift_right))
                    v.tensor_copy(m.pairs_0[:], split_i[:, 0:1])
                    chain(v.tensor_copy(split_f[:, 1:2], split_i[:, 0:1]))
                    chain(v.scalar_tensor_tensor(out=split_f[:, 2:3], in0=split_f[:, 1:2], scalar=float(PAIR),
                                                 in1=upto[:, NODE_TILES - 1:NODE_TILES], op0=ALU.mult,
                                                 op1=ALU.subtract))
                    chain(v.tensor_scalar(start[:, NODE_TILES:n], start[:, NODE_TILES:n], split_f[:, 2:3], None,
                                          ALU.add))
                dve.sem_inc(start_ready, 1)
                v.tensor_scalar(empty[:, 0:n], hist[:, 0:n], 0.0, NO_EDGE, ALU.is_equal, ALU.mult)
                chain(v.tensor_tensor(last[:, 0:n], start[:, 0:n], hist[:, 0:n], ALU.add))
                chain(v.scalar_tensor_tensor(out=last[:, 0:n], in0=last[:, 0:n], scalar=-1.0, in1=empty[:, 0:n],
                                             op0=ALU.add, op1=ALU.add))
                v.tensor_copy(m.last_edge[s][:, 0:n], last[:, 0:n])
                if s == 0:
                    chain(v.tensor_scalar(m.per_edge[:, 0:n], hist[:, 0:n], 1.0, None, ALU.max))
                    v.reciprocal(m.per_edge[:, 0:n], m.per_edge[:, 0:n])
                dve.wait_ge(rows_in, 32 * (s + 1))
                chain(v.tensor_scalar(low_T, low_row[:].rearrange("b (p t) -> b t p", t=ET), iota_part[:, 0:1],
                                      None, ALU.is_equal))
                key_of = key_row[0:EP, :].rearrange("b (p t) -> b t p", t=ET)
                with dve.Fori(0, SORT_ITER) as i:
                    for k in range(SORT_TILES):
                        t = SORT_TILES * i + k
                        before = SORT_TILES * i + (ET * s + k)
                        dve.wait_ge(counted, before + (s + 1))
                        v.tensor_copy(count_hi[:, k, 0:n], ps_count[:, 0:n]).then_inc(count_hi_ready, 1)
                        dve.wait_ge(count_hi_ready, before + 1)
                        v.tensor_tensor(count_lo[:, k, 0:n], ps_count[:, 0:n], count_hi[:, k, 0:n],
                                        ALU.subtract).then_inc(count_ready, 1)
                        v.scalar_tensor_tensor(out=junk[:, 0, 0:EP],
                                               in0=key_of[:, bass.ds(t, 1), :].rearrange("b a p -> b (a p)"),
                                               scalar=key[:, bass.ds(t, 1)], in1=before_edge[:],
                                               op0=ALU.is_equal, op1=ALU.mult, accum_out=rank[:, bass.ds(t, 1)])
                        dve.wait_ge(looked, before + 1)
                        v.scalar_tensor_tensor(out=junk[:, 1, 0:n],
                                               in0=one_class[:, bass.ds(t, 1), 0:n].rearrange("p a b -> p (a b)"),
                                               scalar=1.0, in1=ps_look(k, n),
                                               op0=ALU.mult, op1=ALU.mult, accum_out=base[:, bass.ds(t, 1)])
                chain(v.drain())
                chain(v.tensor_tensor(pos[:], base[:], rank[:], ALU.add))
                chain(v.tensor_copy(pos_i[:], pos[:]))
                v.tensor_scalar(tile_i[:], pos_i[:], 7, None, ALU.logical_shift_right)
                v.tensor_scalar(vals[:, 0, :], key[:], 1.0, None, ALU.add)
                v.tensor_copy(vals[:, 1, :], pay[:])
                chain(v.tensor_scalar(slot_i[:], pos_i[:], P - 1, None, ALU.bitwise_and))
                v.tensor_copy(vals_hi[:], vals[:])
                v.tensor_copy(tile_f[:], tile_i[:])
                chain(v.tensor_copy(slot_f[:], slot_i[:]))
                v.tensor_tensor(vals_lo[:], vals[:], vals_hi[:], ALU.subtract)
                v.tensor_tensor(one_slot, deep(iota_row[0:EP, 0:P], ET), wide(slot_f[:], P), ALU.is_equal)
                chain(v.tensor_tensor(one_tile[:], deep(iota_row[0:EP, 0:POS_TILES], ET), wide(tile_f[:], POS_TILES),
                                      ALU.is_equal))
                for h, part in enumerate((vals_hi, vals_lo)):
                    for k in range(2):
                        done = v.tensor_tensor(put[:, h, :, k, :], one_tile[:], wide(part[:, k, :], POS_TILES), ALU.mult)
                done.then_inc(put_ready, 1)
                dve.wait_ge(put_done, s + 1)
                v.tensor_copy(m.row_of[s][:], ps_put[:, POS_TILES:2 * POS_TILES])
                v.tensor_copy(keys_out[:, 0:POS_TILES], ps_put[:, 0:POS_TILES]).then_inc(keys_out_ready, 1)
                dve.wait_ge(keys_turned, s + 1)
                v.tensor_copy(keys_T[:], ps_keys[0:POS_TILES, :]).then_inc(keys_T_ready, 1)
            mask(1)
            dve.wait_ge(bias_in, 16 * (2 * len(m.biases) + 4))
            v.tensor_copy(m.row_pick[:], m.row_pick_f[:])
            chain(v.tensor_copy(m.bias_rows[:], bias_f[:]))
            v.tensor_tensor(m.bias_rows[32:33], bias_f[32:33], m.bias_rows[32:33].bitcast(F32), ALU.subtract)

        inner.close()
        clear(nc, mine)


def shared(nc, ctx, m):
    def sb(name, shape, dt):
        return ctx.enter_context(nc.sbuf_tensor(name, shape, dt))

    m.psum = ctx.enter_context(nc.psum_tensor("psum", [P, 8, 512], F32))
    m.ident = sb("ident", [P, P], F32)
    m.row_pick_f = sb("row_pick_f", [P, P], F32)
    m.row_pick = sb("row_pick", [P, P], F32R)
    m.bias_rows = sb("bias_rows", [P, 3, D], F32R)
    m.gamma_b = sb("gamma_b", [P, D], F32)
    m.beta_b = sb("beta_b", [P, D], F32)
    m.gate_b = [sb(f"gate_b{i}", [P, RELATIONS * D], F32) for i in range(2)]
    m.same = [sb(f"same{s}", [P, POSITIONS], BF16) for s in range(2)]
    m.row_of = [sb(f"row_of{s}", [P, POS_TILES], I32) for s in range(2)]
    m.last_edge = [sb(f"last_edge{s}", [P, CLASSES[s]], I32) for s in range(2)]
    m.per_edge = sb("per_edge", [P, NODE_TILES], F32)
    m.pairs_0 = sb("pairs_0", [P, 1], I32)
    m.key_d = [nc.dram_tensor(f"key_d{s}", [EDGES], F32).ap() for s in range(2)]
    m.low_d = [nc.dram_tensor(f"low_d{s}", [EDGES], BF16).ap() for s in range(2)]
    m.sorted_d = [nc.dram_tensor(f"sorted_d{s}", [POSITIONS], F32).ap() for s in range(2)]


class At:

    def __init__(self, ring, j, o):
        self.ring, self.j, self.o = ring, j, o

    def back(self, k):
        return At(self.ring, self.j, self.o - k)

    def count(self, per=1, more=0):
        return per * self.ring * self.j + (per * (self.o + 1) + more)

    def index(self, per=1, more=0):
        return per * self.ring * self.j + (per * self.o + more)

    def slot(self, n):
        return self.o % n

    def uses(self, n, per=1, more=0):
        return per * (self.ring // n) * self.j + (per * (self.o // n + 1) + more)

    def within(self, steps):
        return not isinstance(self.j, int) or 0 <= self.o < steps


def sweep(eng, ring, full, steps, skew, step):
    for o in range(ring):
        step(At(ring, 0, o))
    with eng.Fori(1, full // ring) as j:
        for o in range(ring):
            step(At(ring, j, o))
    for o in range(full // ring * ring, steps + skew):
        step(At(ring, 0, o))


def product(nc, m, out, slot, c, w_hi, w_lo, bias):
    if bias is not None:
        nc.tensor.matmul(out, m.row_pick[:], m.bias_rows[:, bias, :], start=True, stop=False)
    for k in range(KC):
        hi = m.x_hi[:, slot, k, c * P:(c + 1) * P]
        lo = m.x_lo[:, slot, k, c * P:(c + 1) * P]
        nc.tensor.matmul(out, hi, w_hi(k), start=(bias is None and k == 0), stop=False)
        nc.tensor.matmul(out, hi, w_lo(k), start=False, stop=False)
        done = nc.tensor.matmul(out, lo, w_hi(k), start=False, stop=(k == KC - 1))
    return done


def transposes(nc, m, source, slot, tiles):
    turned = m.turned(slot)
    for c in range(tiles):
        for k in range(KC):
            done = nc.tensor.transpose(turned[:, k, c * P:(c + 1) * P], source[:, c, k * P:(k + 1) * P], m.ident[:])
    return done



def load_weights(sp, m, load):
    for n, w in enumerate(load):
        sp.dma_start(m.w_stage[:, n * KC:(n + 1) * KC, :], w.rearrange("(c p) o -> p c o", p=P)
                     ).then_inc(m.stage_in, 16)
        m.staged += 16


def edge_phase(nc, m, name, steps, source, s, gate, table, next_weights, first_weights=()):
    ring = 4
    relations = 1 if gate is None else RELATIONS
    with ExitStack() as ctx:
        inner = ctx.enter_context(ExitStack())
        mine = []

        def sem(what):
            mine.append(ctx.enter_context(nc.semaphore(f"{name}_{what}")))
            return mine[-1]

        index_ready = sem("index_ready")
        index_seen = sem("index_seen")
        rows_in = [sem(f"rows_in{i}") for i in range(ring)]
        logits_ready = sem("logits_ready")
        gates_ready = sem("gates_ready")
        scaled = sem("scaled")
        turned = sem("turned")
        summed = sem("summed")
        hi_ready = sem("hi_ready")
        lo_ready = sem("lo_ready")
        multiplied = sem("multiplied")
        copied = sem("copied")
        stored = [sem(f"stored{i}") for i in range(ring)]
        split_hi = sem("split_hi")
        split_lo = sem("split_lo")
        zeroed = sem("zeroed")
        table_rows = table.rearrange("(q c p) o -> q p c o", c=2, p=P)
        staged = m.staged + 16 * len(first_weights)
        w_hi, w_lo, w_in = m.w_edge_hi[:, 0:relations * KC], m.w_edge_lo[:, 0:relations * KC], \
            m.w_stage[:, 0:relations * KC]
        block = inner.enter_context(nc.Block())

        @block.sync
        def _(sp):
            load_weights(sp, m, first_weights)
            sp.wait_ge(split_lo, 1)
            load_weights(sp, m, next_weights)

            def step(at):
                now = at
                if not now.within(steps):
                    return
                slot = now.slot(ring)
                sp.wait_ge(copied, now.count(1, 2))
                sp.dma_start(table_rows[bass.ds(now.index(), 1)].rearrange("a p c o -> (a p) c o"),
                             m.t[:, slot]).then_inc(stored[slot], 16)

            sweep(sp, ring, steps, steps, 0, step)
            for slot in range(ring):
                sp.wait_ge(stored[slot], 16 * len(range(slot, steps, ring)) + 16)

        @block.gpsimd
        def _(pool):
            def step(at):
                now = at
                if not now.within(steps):
                    return
                slot = now.slot(ring)
                pool.wait_ge(turned, now.count())
                nc.gpsimd.tensor_copy(m.index[:, 2 * slot:2 * slot + 2],
                                      m.row_of[s][:, bass.ds(now.index(2), 2)]).then_inc(index_ready, 1)
                pool.wait_ge(index_ready, now.count())
                pool.sem_inc(index_seen, 1)
                for c in range(2):
                    index = m.index[:, 2 * slot + c:2 * slot + c + 1]
                    pool.indirect_dma_start(out=m.x[:, slot, c, :], out_offset=None, in_=source,
                                            in_offset=bass.IndirectOffsetOnAxis(ap=index, axis=0),
                                            bounds_check=NODES - 1, oob_is_err=False).then_inc(rows_in[slot], 16)

            sweep(pool, ring, steps, steps, 0, step)

        @block.tensor
        def _(pe):
            pe.sem_inc(turned, ring)
            pe.sem_inc(multiplied, 2)
            if gate is not None:
                pairs_0 = pe.value_load(m.pairs_0[0:1, 0:1], min_val=0, max_val=EDGE_STEPS_0)
            pe.wait_ge(split_lo, 1)

            def step(at):
                now = at.back(1)
                if now.within(steps):
                    if gate is None:
                        pe.wait_ge(rows_in[now.slot(ring)], now.uses(ring, 32))
                    else:
                        pe.wait_ge(scaled, now.count())
                    pe.wait_ge(summed, now.count())
                    transposes(nc, m, m.x[:, now.slot(ring)], now.slot(2), 2).then_inc(turned, 1)
                now = at.back(3)
                if now.within(steps):
                    pe.wait_ge(lo_ready, now.count(1, 1))
                    pe.wait_ge(copied, now.count())
                    relation = 0 if gate is None else (now.index() >= pairs_0) * KC

                    def chunk_of(w, k):
                        if gate is None:
                            return w[:, k, :]
                        return w[:, bass.ds(relation + k, 1), :].rearrange("p a o -> p (a o)")

                    for c in range(2):
                        done = product(nc, m, m.product(now.slot(2))[:, c, :], now.slot(2), c,
                                       lambda k: chunk_of(w_hi, k), lambda k: chunk_of(w_lo, k), None)
                    done.then_inc(multiplied, 1)

            sweep(pe, ring, steps, steps, 3, step)

        @block.vector
        def _(dve):
            v = nc.vector
            dve.sem_inc(summed, 2)
            dve.sem_inc(lo_ready, 1)
            v.memset(m.sums[:, 1, :, PAIR - 1:PAIR], 0.0).then_inc(zeroed, 1)
            dve.wait_ge(split_hi, 1)
            v.tensor_tensor(w_lo, w_in, w_hi.bitcast(F32), ALU.subtract).then_inc(split_lo, 1)
            if gate is not None:
                pairs_0 = dve.value_load(m.pairs_0[0:1, 0:1], min_val=0, max_val=EDGE_STEPS_0)
            dve.wait_ge(zeroed, 1)

            def step(at):
                now = at.back(2)
                if now.within(steps):
                    slot = now.slot(2)
                    dve.wait_ge(turned, now.count(1, ring))
                    dve.wait_ge(lo_ready, now.count())
                    for k in range(KC):
                        done = v.tensor_tensor_scan(m.sums[:, slot, k, :],
                                                    m.same[s][:, bass.ds(now.index(PAIR), PAIR)],
                                                    m.turned(slot)[:, k, :], m.sums[:, 1 - slot, k, PAIR - 1:PAIR],
                                                    ALU.mult, ALU.add)
                    done.then_inc(summed, 1)
                now = at
                if gate is not None and now.within(steps):
                    slot = now.slot(ring)
                    relation = (now.index() >= pairs_0) * D
                    dve.wait_ge(rows_in[slot], now.uses(ring, 32))
                    for c in range(2):
                        done = v.scalar_tensor_tensor(out=m.g[:, slot // 2, slot % 2, c, :], in0=m.x[:, slot, c, :], scalar=1.0,
                                                      in1=gate[:, bass.ds(relation, D)], op0=ALU.mult, op1=ALU.mult,
                                                      accum_out=m.logits[:, slot, c:c + 1])
                    done.then_inc(logits_ready, 1)
                now = at.back(2)
                if now.within(steps):
                    slot = now.slot(2)
                    dve.wait_ge(hi_ready, now.count())
                    v.tensor_tensor(m.x_lo[:, slot], m.sums[:, slot], m.x_hi[:, slot].bitcast(F32),
                                    ALU.subtract).then_inc(lo_ready, 1)

            sweep(dve, ring, steps, steps, 2, step)

        @block.scalar
        def _(act):
            act.sem_inc(copied, 2)
            for slot in range(ring):
                act.sem_inc(stored[slot], 16)
            act.wait_ge(m.stage_in, staged)
            nc.scalar.copy(w_hi, w_in).then_inc(split_hi, 1)

            def step(at):
                now = at.back(2)
                if now.within(steps):
                    slot = now.slot(2)
                    act.wait_ge(summed, now.count(1, 2))
                    act.wait_ge(multiplied, now.count())
                    nc.scalar.copy(m.x_hi[:, slot], m.sums[:, slot]).then_inc(hi_ready, 1)
                now = at
                if gate is not None and now.within(steps):
                    slot = now.slot(ring)
                    act.wait_ge(logits_ready, now.count())
                    nc.scalar.activation(m.gates[:, slot, :], m.logits[:, slot, :], ACT.Sigmoid
                                         ).then_inc(gates_ready, 1)
                    act.wait_ge(gates_ready, now.count())
                    for c in range(2):
                        done = nc.scalar.activation(m.x[:, slot, c, :], m.x[:, slot, c, :], ACT.Copy,
                                                    scale=m.gates[:, slot, c:c + 1])
                    done.then_inc(scaled, 1)
                now = at.back(4)
                if now.within(steps):
                    slot = now.slot(ring)
                    act.wait_ge(multiplied, now.count(1, 2))
                    act.wait_ge(stored[slot], now.uses(ring, 16))
                    nc.scalar.copy(m.t[:, slot], m.product(now.slot(2))).then_inc(copied, 1)

            sweep(act, ring, steps, steps, 4, step)

        inner.close()
        clear(nc, mine)


def node_phase(nc, m, name, kind, source, s, table, bias, out, next_weights):
    ring = 6
    steps = NODE_STEPS
    full = NODES // PAIR
    relations = RELATIONS if kind else 1
    norm = kind != 1
    with ExitStack() as ctx:
        inner = ctx.enter_context(ExitStack())
        mine = []

        def sem(what):
            mine.append(ctx.enter_context(nc.semaphore(f"{name}_{what}")))
            return mine[-1]

        rows_in = [sem(f"rows_in{i}") for i in range(ring)]
        rows_free = sem("rows_free")
        extra_in = [sem(f"extra_in{i}") for i in range(2)]
        turned = sem("turned")
        hi_ready = sem("hi_ready")
        lo_ready = sem("lo_ready")
        multiplied = sem("multiplied")
        cleared = sem("cleared")
        index_ready = sem("index_ready")
        index_seen = sem("index_seen")
        edges_in = [sem(f"edges_in{i}") for i in range(2)]
        part_added = sem("part_added")
        added = sem("added")
        squared = sem("squared")
        stat_step = sem("stat_step")
        var_ready = sem("var_ready")
        std_ready = sem("std_ready")
        norm_ready = sem("norm_ready")
        normed = sem("normed")
        gained = sem("gained")
        shifted = sem("shifted")
        resid_ready = sem("resid_ready")
        resid_squared = sem("resid_squared")
        ready = sem("ready")
        stored = [sem(f"stored{i}") for i in range(6)]
        split_hi = sem("split_hi")
        split_lo = sem("split_lo")
        cleaned = sem("cleaned")
        staged = m.staged
        w_hi, w_lo, w_in = m.w_node_hi, m.w_node_lo, m.w_stage[:, 0:KC]
        positions = PAIR * (EDGE_STEPS if kind else EDGE_STEPS_0)
        result, result_ring = (m.y, 2) if kind == 0 else (m.t, 3)
        block = inner.enter_context(nc.Block())

        def tiles(now):
            return 1 if isinstance(now.j, int) and now.o == steps - 1 else 2

        def rows_of(ap, now):
            if tiles(now) == 1:
                return ap[full * PAIR:NODES, :].unsqueeze(1), LAST_ROWS, 1
            block_rows = ap[0:full * PAIR, :].rearrange("(q c p) o -> q p c o", c=2, p=P)
            return block_rows[bass.ds(now.index(), 1)].rearrange("a p c o -> (a p) c o"), P, 2

        def gathered(now):
            per = 16 * 2 * relations
            if tiles(now) == 1:
                return now.uses(2, per) - per // 2
            return now.uses(2, per)

        @block.sync
        def _(sp):
            def step(at):
                now = at
                if now.within(steps):
                    rows, p, c = rows_of(source, now)
                    sp.wait_ge(rows_free if kind == 0 else turned, now.count())
                    sp.dma_start(m.x[0:p, now.slot(ring), 0:c], rows).then_inc(rows_in[now.slot(ring)], 16)
                now = at.back(2)
                if kind == 2 and now.within(steps):
                    rows, p, c = rows_of(m.x1, now)
                    sp.wait_ge(added, now.count())
                    sp.dma_start(m.y[0:p, now.slot(2), 0:c], rows).then_inc(extra_in[now.slot(2)], 16)
                now = at.back(6)
                if now.within(steps):
                    rows, p, c = rows_of(out, now)
                    sp.wait_ge(ready, now.count())
                    sp.dma_start(rows, result[0:p, now.slot(result_ring), 0:c]
                                 ).then_inc(stored[now.slot(result_ring)], 16)

            for o in range(2):
                step(At(ring, 0, o))
            if next_weights:
                sp.wait_ge(split_lo, 1)
                load_weights(sp, m, next_weights)
            for o in range(2, ring):
                step(At(ring, 0, o))
            with sp.Fori(1, full // ring) as j:
                for o in range(ring):
                    step(At(ring, j, o))
            for o in range(full // ring * ring, steps + 6):
                step(At(ring, 0, o))
            for slot in range(result_ring):
                sp.wait_ge(stored[slot], 16 * len(range(slot, steps, result_ring)) + 16)

        @block.gpsimd
        def _(pool):
            if kind == 0:
                pool.wait_ge(cleaned, 1)

            def gathers(now):
                slot = now.slot(2)
                n = tiles(now)
                if kind == 0:
                    pool.wait_ge(added, now.count())
                else:
                    pool.wait_ge(cleared, now.count())
                for r in range(relations):
                    done = nc.gpsimd.tensor_copy(
                        m.index[:, 4 * slot + 2 * r:4 * slot + 2 * r + n],
                        m.last_edge[s][:, bass.ds(now.index(2, r * NODE_TILES), n)])
                if kind == 0:
                    done = nc.gpsimd.memset(m.g[:, 0, slot], 0.0)
                done.then_inc(index_ready, 1)
                pool.wait_ge(index_ready, now.count())
                pool.sem_inc(index_seen, 1)
                for r in range(relations):
                    for c in range(n):
                        at_index = 4 * slot + 2 * r + c
                        pool.indirect_dma_start(
                            out=m.g[:, r, slot, c, :], out_offset=None, in_=table[0:positions],
                            in_offset=bass.IndirectOffsetOnAxis(ap=m.index[:, at_index:at_index + 1], axis=0),
                            bounds_check=positions - 1, oob_is_err=False).then_inc(edges_in[slot], 16)

            def step(at):
                now = at
                if now.within(steps):
                    gathers(now)
                now = at.back(3)
                if kind == 0 and now.within(steps):
                    slot, n = now.slot(3), tiles(now)
                    pool.wait_ge(normed, now.count())
                    nc.gpsimd.tensor_tensor(m.t[:, slot, 0:n], m.t[:, slot, 0:n], deep(m.gamma_b[:], n), ALU.mult
                                            ).then_inc(gained, 1)

            sweep(pool, ring, full, steps, 3, step)

        @block.tensor
        def _(pe):
            pe.sem_inc(multiplied, 2)
            pe.sem_inc(turned, ring)
            pe.wait_ge(cleaned, 1)
            pe.wait_ge(split_lo, 1)

            def step(at):
                now = at
                if now.within(steps):
                    pe.wait_ge(rows_in[now.slot(ring)], now.uses(ring, 16))
                    pe.wait_ge(lo_ready, now.count())
                    done = transposes(nc, m, m.x[:, now.slot(ring)], now.slot(2), tiles(now))
                    done.then_inc(turned, 1)
                now = at.back(1)
                if now.within(steps):
                    pe.wait_ge(lo_ready, now.count(1, 2))
                    pe.wait_ge(added, now.count())
                    for c in range(tiles(now)):
                        done = product(nc, m, m.product(now.slot(2))[:, c, :], now.slot(2), c,
                                       lambda k: w_hi[:, k, :], lambda k: w_lo[:, k, :], bias)
                    done.then_inc(multiplied, 1)

            sweep(pe, ring, full, steps, 1, step)

        @block.vector
        def _(dve):
            v = nc.vector
            dve.sem_inc(lo_ready, 2)
            dve.sem_inc(added, 2)
            for slot in range(result_ring):
                dve.sem_inc(stored[slot], 16)
            dve.sem_inc(norm_ready, 1)
            if kind == 0:
                dve.sem_inc(rows_free, ring)
            v.memset(m.sum4[:], 0.0)
            v.memset(m.sq4[:], 0.0).then_inc(cleaned, 1)
            dve.wait_ge(split_hi, 1)
            v.tensor_tensor(w_lo[:], w_in, w_hi[:].bitcast(F32), ALU.subtract).then_inc(split_lo, 1)
            dve.wait_ge(cleaned, 1)

            def step(at):
                first, second = at.back(3), at.back(5)
                stats = norm and (first.within(steps) or (kind == 0 and second.within(steps)))
                if stats:
                    if first.within(steps):
                        dve.wait_ge(squared, first.count())
                    if kind == 0 and second.within(steps):
                        dve.wait_ge(resid_squared, second.count())
                    past = at.back(1).slot(2)
                    turn = first.index()
                    dve.wait_ge(norm_ready, turn + 1)
                    v.tensor_scalar(m.neg_mean[:], m.sum4[:, past], -1.0 / D, None, ALU.mult)
                    v.tensor_scalar(m.mean_sq[:], m.sq4[:, past], 1.0 / D, LN_EPS, ALU.mult, ALU.add
                                    ).then_inc(stat_step, 1)
                    dve.wait_ge(stat_step, 3 * turn + 1)
                    v.tensor_tensor(m.var[:], m.neg_mean[:], m.neg_mean[:], ALU.mult).then_inc(stat_step, 1)
                    dve.wait_ge(stat_step, 3 * turn + 2)
                    v.tensor_tensor(m.var[:], m.mean_sq[:], m.var[:], ALU.subtract).then_inc(var_ready, 1)
                now = at.back(2)
                if now.within(steps):
                    slot, n, t = now.slot(2), tiles(now), now.slot(3)
                    dve.wait_ge(multiplied, now.count(1, 2))
                    dve.wait_ge(edges_in[slot], gathered(now))
                    product_of, sums = m.product(slot), m.t[:, t]
                    if kind == 0:
                        for c in range(n):
                            done = v.scalar_tensor_tensor(
                                out=sums[:, c, :], in0=m.g[:, 0, slot, c, :],
                                scalar=m.per_edge[:, bass.ds(now.index(2, c), 1)], in1=product_of[:, c, :],
                                op0=ALU.mult, op1=ALU.add, accum_out=m.sum4[:, at.slot(2), c:c + 1])
                        done.then_inc(added, 1)
                    else:
                        dve.wait_ge(stored[t], now.uses(3, 16))
                        v.tensor_tensor(sums[:, 0:n], product_of[:, 0:n], m.g[:, 0, slot, 0:n], ALU.add
                                        ).then_inc(part_added, 1)
                        dve.wait_ge(part_added, now.count(kind, 1 - kind))
                        if kind == 1:
                            v.tensor_tensor(sums[:, 0:n], sums[:, 0:n], m.g[:, 1, slot, 0:n], ALU.add
                                            ).then_inc(added, 1)
                        else:
                            v.tensor_tensor(sums[:, 0:n], sums[:, 0:n], m.g[:, 1, slot, 0:n], ALU.add
                                            ).then_inc(part_added, 1)
                            dve.wait_ge(part_added, now.count(2))
                            dve.wait_ge(extra_in[slot], now.uses(2, 16))
                            for c in range(n):
                                done = v.scalar_tensor_tensor(
                                    out=sums[:, c, :], in0=sums[:, c, :], scalar=1.0, in1=m.y[:, slot, c, :],
                                    op0=ALU.mult, op1=ALU.add, accum_out=m.sum4[:, at.slot(2), c:c + 1])
                            done.then_inc(added, 1)
                now = at
                if kind and now.within(steps):
                    dve.wait_ge(added, now.count())
                    for r in range(RELATIONS):
                        done = v.memset(m.g[:, r, now.slot(2)], 0.0)
                    done.then_inc(cleared, 1)
                if stats:
                    dve.wait_ge(std_ready, first.count())
                    v.reciprocal(m.rstd[:, at.slot(2)], m.std[:]).then_inc(stat_step, 1)
                    dve.wait_ge(stat_step, 3 * turn + 3)
                    v.tensor_tensor(m.shift[:, at.slot(2)], m.neg_mean[:], m.rstd[:, at.slot(2)], ALU.mult
                                    ).then_inc(norm_ready, 1)
                now = at.back(4)
                if kind == 0 and now.within(steps):
                    slot, n = now.slot(3), tiles(now)
                    dve.wait_ge(gained, now.count())
                    v.tensor_tensor(m.t[:, slot, 0:n], m.t[:, slot, 0:n], deep(m.beta_b[:], n), ALU.add
                                    ).then_inc(shifted, 1)
                    dve.wait_ge(shifted, now.count())
                    dve.wait_ge(stored[now.slot(2)], now.uses(2, 16))
                    for c in range(n):
                        done = v.scalar_tensor_tensor(
                            out=m.y[:, now.slot(2), c, :], in0=m.t[:, slot, c, :], scalar=0.0,
                            in1=m.x[:, now.slot(ring), c, :], op0=ALU.max, op1=ALU.add,
                            accum_out=m.sum4[:, at.slot(2), 2 + c:3 + c])
                    done.then_inc(rows_free, 1)
                now = at
                if now.within(steps):
                    slot, n = now.slot(2), tiles(now)
                    dve.wait_ge(hi_ready, now.count())
                    v.tensor_tensor(m.x_lo[:, slot, :, 0:n * P], m.turned(slot)[:, :, 0:n * P],
                                    m.x_hi[:, slot, :, 0:n * P].bitcast(F32), ALU.subtract).then_inc(lo_ready, 1)

            sweep(dve, ring, full, steps, 5 if kind == 0 else 3, step)

        @block.scalar
        def _(act):
            act.wait_ge(m.stage_in, staged)
            nc.scalar.copy(w_hi[:], w_in).then_inc(split_hi, 1)
            act.wait_ge(cleaned, 1)

            def step(at):
                now = at
                if now.within(steps):
                    slot, n = now.slot(2), tiles(now)
                    act.wait_ge(turned, now.count(1, ring))
                    act.wait_ge(multiplied, now.count())
                    nc.scalar.copy(m.x_hi[:, slot, :, 0:n * P], m.turned(slot)[:, :, 0:n * P]).then_inc(hi_ready, 1)
                if kind == 1:
                    now = at.back(2)
                    if now.within(steps):
                        slot, n = now.slot(3), tiles(now)
                        act.wait_ge(added, now.count(1, 2))
                        nc.scalar.activation(m.t[:, slot, 0:n], m.t[:, slot, 0:n], ACT.Relu).then_inc(ready, 1)
                    return
                first, second = at.back(3), at.back(5)
                if first.within(steps) or (kind == 0 and second.within(steps)):
                    act.wait_ge(var_ready, first.count())
                    nc.scalar.activation(m.std[:], m.var[:], ACT.Sqrt).then_inc(std_ready, 1)
                now = at.back(2)
                if now.within(steps):
                    slot, n = now.slot(3), tiles(now)
                    act.wait_ge(added, now.count(1, 2))
                    for c in range(n):
                        done = nc.scalar.activation(m.junk[:, c, :], m.t[:, slot, c, :], ACT.Square,
                                                    accum_out=m.sq4[:, at.slot(2), c:c + 1])
                    done.then_inc(squared, 1)
                now = at.back(3)
                if now.within(steps):
                    slot, n = now.slot(3), tiles(now)
                    act.wait_ge(norm_ready, first.count(1, 1))
                    for c in range(n):
                        done = nc.scalar.activation(m.t[:, slot, c, :], m.t[:, slot, c, :], ACT.Identity,
                                                    bias=m.shift[:, at.slot(2), c:c + 1],
                                                    scale=m.rstd[:, at.slot(2), c:c + 1])
                    done.then_inc(normed if kind == 0 else ready, 1)
                now = at.back(5)
                if kind == 0 and now.within(steps):
                    slot, n = now.slot(2), tiles(now)
                    act.wait_ge(norm_ready, first.count(1, 1))
                    for c in range(n):
                        done = nc.scalar.activation(m.y[:, slot, c, :], m.y[:, slot, c, :], ACT.Identity,
                                                    bias=m.shift[:, at.slot(2), 2 + c:3 + c],
                                                    scale=m.rstd[:, at.slot(2), 2 + c:3 + c])
                    done.then_inc(ready, 1)
                now = at.back(4)
                if kind == 0 and now.within(steps):
                    slot, n = now.slot(2), tiles(now)
                    act.wait_ge(rows_free, now.count(1, ring))
                    for c in range(n):
                        done = nc.scalar.activation(m.junk[:, 2 + c, :], m.y[:, slot, c, :], ACT.Square,
                                                    accum_out=m.sq4[:, at.slot(2), 2 + c:3 + c])
                    done.then_inc(resid_squared, 1)

            sweep(act, ring, full, steps, 5 if kind == 0 else 3, step)

        inner.close()
        clear(nc, mine)


def main_buffers(nc, ctx, m):
    def sb(name, shape, dt):
        return ctx.enter_context(nc.sbuf_tensor(name, shape, dt))

    m.x = sb("x_rows", [P, 6, 2, D], F32)
    m.x_hi = sb("x_hi", [P, 2, KC, PAIR], F32R)
    m.x_lo = sb("x_lo", [P, 2, KC, PAIR], F32R)
    m.sums = sb("sums", [P, 2, KC, PAIR], F32)
    m.y = m.sums[:].rearrange("p s k r -> p (s k r)").rearrange("p (s c o) -> p s c o", s=2, c=2)
    m.t = sb("t_rows", [P, 4, 2, D], F32)
    m.g = sb("edge_rows", [P, RELATIONS, 2, 2, D], F32)
    m.index = sb("index", [P, 8], I32)
    m.w_stage = sb("w_stage", [P, RELATIONS * KC, D], F32)
    m.w_edge_hi = sb("w_edge_hi", [P, RELATIONS * KC, D], F32R)
    m.w_edge_lo = sb("w_edge_lo", [P, RELATIONS * KC, D], F32R)
    m.w_node_hi = sb("w_node_hi", [P, KC, D], F32R)
    m.w_node_lo = sb("w_node_lo", [P, KC, D], F32R)
    m.logits = sb("logits", [P, 4, 2], F32)
    m.gates = sb("gates", [P, 4, 2], F32)
    m.junk = sb("junk_squares", [P, 4, D], BF16)
    m.sum4, m.sq4, m.rstd, m.shift = (sb(f"stats{i}", [P, 2, 4], F32) for i in range(4))
    m.neg_mean, m.mean_sq, m.var, m.std = (sb(f"moments{i}", [P, 4], F32) for i in range(4))
    m.turned = lambda slot: m.psum[:, 2 * slot:2 * slot + 2, :].rearrange("p b (k r) -> p (b k) r", r=PAIR)
    m.product = lambda slot: m.psum[:, 4 + 2 * slot:6 + 2 * slot, :]
    m.stage_in = ctx.enter_context(nc.semaphore("stage_in"))
    m.staged = 0


def gnn_kernel(nc, x, src, dst, edge_type, w_self_T, w_neigh_T, bias, gamma, beta, basis1, att1, gate_w1, root1, bias1,
               basis2, att2, gate_w2, root2, bias2, out):
    m = Shared()
    with ExitStack() as ctx:
        shared(nc, ctx, m)
        m.src, m.dst, m.edge_type = src, dst, edge_type
        m.att, m.basis, m.gate_w = [att1, att2], [basis1, basis2], [gate_w1, gate_w2]
        m.biases, m.gamma, m.beta = [bias, bias1, bias2], gamma, beta
        m.w_made = [nc.dram_tensor(f"w_made{i}", [RELATIONS, D, D], F32).ap() for i in range(2)]
        m.x1 = nc.dram_tensor("x1", [NODES, D], F32).ap()
        m.h = nc.dram_tensor("h", [NODES, D], F32).ap()
        table = nc.dram_tensor("edge_table", [POSITIONS, D], F32).ap()
        prologue(nc, m)
        main_buffers(nc, ctx, m)
        made = [[w[0], w[1]] for w in m.w_made]
        edge_phase(nc, m, "e0", EDGE_STEPS_0, x, 0, None, table, [w_self_T], [w_neigh_T])
        node_phase(nc, m, "n0", 0, x, 0, table, 0, m.x1, made[0])
        edge_phase(nc, m, "e1", EDGE_STEPS, m.x1, 1, m.gate_b[0], table, [root1])
        node_phase(nc, m, "n1", 1, m.x1, 1, table, 1, m.h, made[1])
        edge_phase(nc, m, "e2", EDGE_STEPS, m.h, 1, m.gate_b[1], table, [root2])
        node_phase(nc, m, "n2", 2, m.h, 1, table, 2, out, [])


def kernel(x, src, dst, edge_type_2, L0_gnn_w_self, L0_gnn_w_neigh, L0_gnn_bias, L0_gnn_gamma, L0_gnn_beta,
           L1_gnn_basis1, L1_gnn_att1, L1_gnn_gate_w1, L1_gnn_root1, L1_gnn_bias1,
           L1_gnn_basis2, L1_gnn_att2, L1_gnn_gate_w2, L1_gnn_root2, L1_gnn_bias2):
    import concourse.bacc as bacc
    from concourse.bass_utils import run_bass_kernel_spmd

    def spread(att):
        return np.repeat(np.asarray(att).T, QUARTERS, axis=0)

    arrays = {
        "x": x, "src": src, "dst": dst, "edge_type": edge_type_2,
        "w_self_T": np.asarray(L0_gnn_w_self).T, "w_neigh_T": np.asarray(L0_gnn_w_neigh).T,
        "bias": L0_gnn_bias, "gamma": L0_gnn_gamma, "beta": L0_gnn_beta,
        "basis1": L1_gnn_basis1, "att1": spread(L1_gnn_att1), "gate_w1": L1_gnn_gate_w1, "root1": L1_gnn_root1,
        "bias1": L1_gnn_bias1,
        "basis2": L1_gnn_basis2, "att2": spread(L1_gnn_att2), "gate_w2": L1_gnn_gate_w2, "root2": L1_gnn_root2,
        "bias2": L1_gnn_bias2,
    }
    nc = bacc.Bacc("TRN2", target_bir_lowering=False, num_devices=1)
    launch, args = {}, {}
    for name, array in arrays.items():
        array = np.ascontiguousarray(array)
        launch[f"in_{name}"] = array
        args[name] = nc.dram_tensor(f"in_{name}", array.shape, mybir.dt.from_np(array.dtype), kind="ExternalInput").ap()
    out = nc.dram_tensor("out_rows", (NODES, D), F32, kind="ExternalOutput").ap()
    gnn_kernel(nc, out=out, **args)
    result = run_bass_kernel_spmd(nc, [launch], core_ids=[0])
    return result.results[0]["out_rows"]
```

```python
from contextlib import ExitStack

import numpy as np

import concourse.bass as bass
from concourse import mybir

F32 = mybir.dt.float32
F32R = mybir.dt.float32r
BF16 = mybir.dt.bfloat16
I32 = mybir.dt.int32
ALU = mybir.AluOpType
ACT = mybir.ActivationFunctionType

P = 128
D = 512
KC = D // P
PAIR = 2 * P
LN_EPS = 1e-5
RELATIONS = 2

NODES = 10000
NODE_TILES = -(-NODES // P)
NODE_STEPS = -(-NODES // PAIR)
LAST_ROWS = NODES - (NODE_TILES - 1) * P

EDGES = 5000
ET = 40
EP = EDGES // ET
EDGE_STEPS_0 = -(-EDGES // PAIR)
EDGE_STEPS = EDGE_STEPS_0 + 1
POS_TILES = 2 * EDGE_STEPS
POSITIONS = POS_TILES * P
NO_EDGE = float(1 << 20)

BASES = 30
QUARTERS = 4
BP = BASES * QUARTERS
CHUNK_Q = 4
CHUNKS = P // CHUNK_Q
SORT_ITER = 8
SORT_TILES = ET // SORT_ITER
CLASSES = (NODE_TILES, RELATIONS * NODE_TILES)
RING = 4


def wide(ap, n):
    return ap.unsqueeze(2).to_broadcast([ap.shape[0], ap.shape[1], n])


class Shared:
    pass


def clear(nc, sems):
    nums = sorted(s.num for s in sems)
    first = nums[0]
    for n, after in zip(nums, nums[1:] + [None]):
        if after != n + 1:
            nc.gpsimd.sem_clear(range(first, n + 1))
            first = after


def deep(ap, n):
    return ap.unsqueeze(1).to_broadcast([ap.shape[0], n, ap.shape[1]])


SORTS = range(2)
CHUNKS_BEFORE = 8
CHUNKS_AFTER = CHUNKS - CHUNKS_BEFORE - 2 * SORT_ITER
LOOK_SLOTS = 3


def prologue(nc, m):
    with ExitStack() as ctx:
        inner = ctx.enter_context(ExitStack())

        def sb(name, shape, dt):
            return ctx.enter_context(nc.sbuf_tensor(name, shape, dt))

        def two(name, shape, dt):
            return [sb(f"{name}{s}", shape, dt) for s in SORTS]

        mine = []

        def sem(name):
            mine.append(ctx.enter_context(nc.semaphore(name)))
            return mine[-1]

        iota_row = sb("iota_row", [P, 160], F32)
        iota_b = sb("iota_b", [P, 160], BF16)
        iota_part = sb("iota_part", [P, 1], F32)
        part_int = sb("part_int", [P, 1], I32)
        quarter = sb("quarter", [P, 1], F32)
        before_edge = sb("before_edge", [EP, EP], F32)
        below = sb("below", [P, P], F32)
        ones = sb("ones", [P, 160], F32)
        dst_i = sb("dst_i", [EP, ET], I32)
        src_i = sb("src_i", [EP, ET], I32)
        type_i = sb("type_i", [EP, ET], I32)
        type_f = sb("type_f", [EP, ET], F32)
        low_i = two("low_i", [EP, ET], I32)
        high_i = two("high_i", [EP, ET], I32)
        low = two("low", [EP, ET], F32)
        klass = two("klass", [EP, ET], F32)
        low_b = two("low_b", [EP, ET], BF16)
        klass_b = two("klass_b", [EP, ET], BF16)
        key = two("key", [EP, ET], F32)
        pay = two("pay", [EP, ET], F32)
        one_low = two("one_low", [EP, ET, P], BF16)
        one_class = [sb(f"one_class{s}", [EP, ET, CLASSES[s]], BF16) for s in SORTS]
        low_row = two("low_row", [P, EDGES], BF16)
        by_tile = two("by_tile", [P, ET, P], BF16)
        low_T = [b[:, :, 0:EP] for b in by_tile]
        rows = two("key_row", [P, POSITIONS], F32)
        key_row = [r[:, 0:EDGES] for r in rows]
        rank = two("rank", [EP, ET], F32)
        base = two("base", [EP, ET], F32)
        junk = sb("junk", [EP, 2, 2, 160], F32)
        count_hi = [sb(f"count_hi{s}", [P, SORT_TILES, CLASSES[s]], BF16) for s in SORTS]
        count_lo = [sb(f"count_lo{s}", [P, SORT_TILES, CLASSES[s]], BF16) for s in SORTS]
        pos = two("pos", [EP, ET], F32)
        pos_i = two("pos_i", [EP, ET], I32)
        tile_i = two("tile_i", [EP, ET], I32)
        slot_i = two("slot_i", [EP, ET], I32)
        tile_f = two("tile_f", [EP, ET], BF16)
        slot_f = two("slot_f", [EP, ET], BF16)
        one_slot = [b[0:EP] for b in by_tile]
        one_tile = [b[0:EP, 0:ET * POS_TILES].rearrange("p (t u) -> p t u", t=ET) for b in low_row]
        vals = two("vals", [EP, 2, ET], F32)
        vals_hi = two("vals_hi", [EP, 2, ET], BF16)
        vals_lo = two("vals_lo", [EP, 2, ET], BF16)
        put = [r[0:EP, 0:2 * ET * POS_TILES].bitcast(BF16).rearrange("p (h t k u) -> p h t k u", h=2, t=ET, k=2)
               for r in rows]
        hist = two("hist", [P, CLASSES[1]], F32)
        upto = two("upto", [P, CLASSES[1]], F32)
        start = two("start", [P, CLASSES[1]], F32)
        last = sb("last", [P, CLASSES[1]], F32)
        empty = sb("empty", [P, CLASSES[1]], F32)
        split_i = sb("split_i", [P, 2], I32)
        split_f = sb("split_f", [P, 3], F32)
        keys_out = two("keys_out", [P, P], F32)
        keys_T = two("keys_T", [POS_TILES, P], F32)
        sorted_row = rows
        att = sb("att", [BP, 2, RELATIONS], F32)
        is_quarter = sb("is_quarter", [BP, QUARTERS], F32)
        bias_f = m.same[1][:, 0:2 * 3 * D].bitcast(F32).rearrange("p (n o) -> p n o", n=3)

        ps = m.psum
        ps_count = [ps[:, s, 0:CLASSES[s]] for s in SORTS]
        ps_below = [ps[:, 4 + s, 0:CLASSES[s]] for s in SORTS]
        ps_all = [ps[:, 4 + s, 160:160 + CLASSES[s]] for s in SORTS]
        ps_put = [ps[:, 4 + s, 0:2 * POS_TILES] for s in SORTS]
        ps_keys = [ps[:, 4 + s, 384:384 + P] for s in SORTS]

        def ps_look(s, k):
            slot = 160 * (k % LOOK_SLOTS)
            return ps[0:EP, 2 + s, slot:slot + CLASSES[s]]

        def each(name):
            return [sem(f"{name}{s}") for s in SORTS]

        def for_pool(name):
            return [m.ctx.enter_context(nc.semaphore(f"{name}{s}")) for s in SORTS]

        edges_in = sem("edges_in")
        const_ready = sem("const_ready")
        pool_step = sem("pool_step")
        dve_step = sem("dve_step")
        keys_ready = each("keys_ready")
        keys_stored = for_pool("keys_stored")
        rows_in = for_pool("rows_in")
        onehot_ready = each("onehot_ready")
        hist_ready = each("hist_ready")
        hist_copied = each("hist_copied")
        sums_ready = each("sums_ready")
        start_ready = each("start_ready")
        counted = each("counted")
        count_hi_ready = each("count_hi_ready")
        count_ready = each("count_ready")
        looked = each("looked")
        put_ready = each("put_ready")
        put_done = each("put_done")
        keys_out_ready = each("keys_out_ready")
        keys_turned = each("keys_turned")
        keys_T_ready = each("keys_T_ready")
        keys_T_stored = for_pool("keys_T_stored")
        sorted_in = for_pool("sorted_in")
        att_in = sem("att_in")
        mix_ready = sem("mix_ready")
        chunk_in = [sem(f"chunk_in{i}") for i in range(2)]
        mixed = sem("mixed")
        bank_copied = sem("bank_copied")
        made_stored = [sem(f"made_stored{i}") for i in range(2)]
        bias_in = sem("bias_in")
        bias_step = sem("bias_step")

        block = inner.enter_context(nc.Block())

        @block.sync
        def _(sp):
            sp.dma_start(dst_i[:], m.dst.rearrange("(p t) -> p t", t=ET)).then_inc(edges_in, 16)
            sp.dma_start(src_i[:], m.src.rearrange("(p t) -> p t", t=ET)).then_inc(edges_in, 16)
            sp.dma_start(type_i[:], m.edge_type.rearrange("(p t) -> p t", t=ET)).then_inc(edges_in, 16)
            for n in range(2):
                sp.dma_start(att[:, n, :], m.att[n]).then_inc(att_in, 16)
            sp.wait_ge(bias_step, 1)
            for n, vec in enumerate(m.biases):
                sp.dma_start(bias_f[0:1, n, :], vec.unsqueeze(0)).then_inc(bias_in, 16)
                sp.dma_start(bias_f[32:33, n, :], vec.unsqueeze(0)).then_inc(bias_in, 16)
            sp.dma_start(m.gamma_b[:], m.gamma.partition_broadcast(P)).then_inc(bias_in, 16)
            sp.dma_start(m.beta_b[:], m.beta.partition_broadcast(P)).then_inc(bias_in, 16)
            def made_rows_out(n, c):
                sp.wait_ge(bank_copied, n + 3)
                store_made(sp, m, 0, c, n, made_stored)

            for c in range(2):
                load_chunk(sp, m, 0, c, c, chunk_in)
            with sp.Fori(1, CHUNKS // 2) as i:
                for c in range(2):
                    sp.wait_ge(mixed, 2 * i + (c - 1))
                    load_chunk(sp, m, 0, c, 2 * i + c, chunk_in)
                    made_rows_out(2 * i + (c - 2), c)
            for c in range(2):
                made_rows_out(CHUNKS - 2 + c, c)
            for c in range(2):
                sp.wait_ge(made_stored[c], 64 * (CHUNKS // 2 + 1))

        @block.gpsimd
        def _(pool):
            def chain(ins, n=[0]):
                n[0] += 1
                ins.then_inc(pool_step, 1)
                pool.wait_ge(pool_step, n[0])

            pool.iota(iota_row[:], pattern=[[1, 160]], base=0, channel_multiplier=0,
                      allow_small_or_imprecise_dtypes=True)
            pool.iota(iota_b[:], pattern=[[1, 160]], base=0, channel_multiplier=0,
                      allow_small_or_imprecise_dtypes=True)
            pool.iota(iota_part[:], pattern=[[0, 1]], base=0, channel_multiplier=1,
                      allow_small_or_imprecise_dtypes=True)
            pool.iota(part_int[:], pattern=[[0, 1]], base=0, channel_multiplier=1)
            pool.memset(ones[:], 1.0)
            for s in SORTS:
                pool.memset(keys_out[s][:], 0.0)
            pool.memset(m.zeros[:], 0.0)
            pool.memset(m.mix[:], 0.0)
            pool.memset(bias_f, 0.0).then_inc(bias_step, 1)
            pool.memset(m.ident[:], 0.0)
            chain(pool.memset(m.row_pick_f[:], 0.0))
            pool.memset(m.row_pick_f[0:1, :], 1.0)
            chain(pool.memset(m.row_pick_f[32:33, :], 1.0))
            pool.affine_select(out=m.ident[:], in_=m.ident[:], compare_op=ALU.not_equal, fill=1.0, base=0,
                               pattern=[[-1, P]], channel_multiplier=1)
            pool.affine_select(out=before_edge[:], in_=ones[0:EP, 0:EP], compare_op=ALU.is_gt, fill=0.0, base=0,
                               pattern=[[-1, EP]], channel_multiplier=1)
            pool.affine_select(out=below[:], in_=ones[:, 0:P], compare_op=ALU.is_gt, fill=0.0, base=0,
                               pattern=[[1, P]], channel_multiplier=-1).then_inc(const_ready, 1)
            for s in SORTS:
                pool.wait_ge(keys_ready[s], 1)
                pool.dma_start(m.key_d[s].rearrange("(p t) -> p t", t=ET), key[s][:]).then_inc(keys_stored[s], 16)
                pool.dma_start(m.low_d[s].rearrange("(p t) -> p t", t=ET), low_b[s][:]).then_inc(keys_stored[s], 16)
            for s in SORTS:
                pool.wait_ge(keys_stored[s], 32)
                pool.dma_start(low_row[s][:], m.low_d[s].partition_broadcast(P)).then_inc(rows_in[s], 16)
                pool.dma_start(key_row[s], m.key_d[s].partition_broadcast(P)).then_inc(rows_in[s], 16)
            for s in SORTS:
                pool.wait_ge(keys_T_ready[s], 1)
                pool.dma_start(m.sorted_d[s].rearrange("(u v) -> u v", v=P), keys_T[s][:]
                               ).then_inc(keys_T_stored[s], 16)
                pool.wait_ge(keys_T_stored[s], 16)
                pool.dma_start(sorted_row[s][:], m.sorted_d[s].partition_broadcast(P)).then_inc(sorted_in[s], 16)

        @block.tensor
        def _(pe):
            pe.sem_inc(bank_copied, 2)

            def basis_chunk(n, c):
                pe.wait_ge(chunk_in[c], 8 * (n - c) + 16)
                pe.wait_ge(bank_copied, n + 1)
                basis_group(nc, m, 0, c, 6 + c).then_inc(mixed, 1)

            def basis_chunks(first, end):
                with pe.Fori(first // 2, end // 2) as i:
                    for c in range(2):
                        basis_chunk(2 * i + c, c)

            def histogram_tile(s, t, first=False):
                return nc.tensor.matmul(ps_count[s],
                                        one_low[s][:, bass.ds(t, 1), :].rearrange("p a b -> p (a b)"),
                                        one_class[s][:, bass.ds(t, 1), :].rearrange("p a b -> p (a b)"),
                                        start=first, stop=False, skip_group_check=True)

            pe.wait_ge(const_ready, 1)
            pe.wait_ge(mix_ready, 1)
            basis_chunks(0, CHUNKS_BEFORE // 2)
            for s in SORTS:
                pe.wait_ge(onehot_ready[s], 1)
                for t in range(4):
                    histogram_tile(s, t, t == 0)
                with pe.Fori(1, ET // 4 - 1) as j:
                    for t in range(4):
                        histogram_tile(s, 4 * j + t)
                for t in range(ET - 4, ET):
                    done = histogram_tile(s, t)
                done.then_inc(hist_ready[s], 1)
                pe.wait_ge(hist_copied[s], 1)
                n = CLASSES[s]
                nc.tensor.matmul(ps_below[s], below[:], hist[s][:, 0:n], start=True, stop=True)
                nc.tensor.matmul(ps_all[s], ones[:, 0:P], hist[s][:, 0:n], start=True, stop=True
                                 ).then_inc(sums_ready[s], 1)
                if s == 0:
                    basis_chunks(CHUNKS_BEFORE // 2, CHUNKS_BEFORE)
                pe.wait_ge(start_ready[s], 1)
                nc.tensor.matmul(ps_count[s], m.ident[:], start[s][:, 0:n], start=True, stop=False,
                                 skip_group_check=True).then_inc(counted[s], 1)
            with pe.Fori(0, SORT_ITER) as i:
                for k in range(SORT_TILES):
                    t = SORT_TILES * i + k
                    for s in SORTS:
                        pe.wait_ge(count_ready[s], t + 1)
                        look = ps_look(s, k)
                        turned = low_T[s][:, bass.ds(t, 1), :].rearrange("p a b -> p (a b)")
                        nc.tensor.matmul(look, turned, count_hi[s][:, k, :], start=True, stop=False,
                                         skip_group_check=True)
                        nc.tensor.matmul(look, turned, count_lo[s][:, k, :], start=False, stop=True,
                                         skip_group_check=True).then_inc(looked[s], 1)
                        histogram_tile(s, t).then_inc(counted[s], 1)
                    if k in (1, 3):
                        basis_chunk(2 * i + (CHUNKS_BEFORE + k // 2), k // 2)
            for s in SORTS:
                if s == 0:
                    basis_chunks(CHUNKS - CHUNKS_AFTER, CHUNKS - 4)
                else:
                    basis_chunks(CHUNKS - 4, CHUNKS - 2)
                pe.wait_ge(put_ready[s], 1)

                def put_tile(t, first=False):
                    slot = one_slot[s][:, bass.ds(t, 1), :].rearrange("p a b -> p (a b)")
                    for h in range(2):
                        done = nc.tensor.matmul(ps_put[s], slot,
                                                put[s][:, h, bass.ds(t, 1)].rearrange("p a b c -> p (a b c)"),
                                                start=first and h == 0, stop=False, skip_group_check=True)
                    return done

                for t in range(4):
                    put_tile(t, t == 0)
                with pe.Fori(1, ET // 4 - 1) as j:
                    for t in range(4):
                        put_tile(4 * j + t)
                for t in range(ET - 4, ET):
                    done = put_tile(t)
                done.then_inc(put_done[s], 1)
                pe.wait_ge(keys_out_ready[s], 1)
                nc.tensor.transpose(ps_keys[s], keys_out[s][:], m.ident[:]).then_inc(keys_turned[s], 1)
            for c in range(2):
                basis_chunk(CHUNKS - 2 + c, c)

        @block.scalar
        def _(act):
            for c in range(2):
                act.sem_inc(made_stored[c], 64)

            def made_rows(n, c):
                act.wait_ge(made_stored[c], 32 * (n - c) + 64)
                act.wait_ge(mixed, n + 1)
                nc.scalar.copy(m.made[:, c], ps[:, 6 + c, :]).then_inc(bank_copied, 1)

            def all_made_rows(first, end):
                with act.Fori(first // 2, end // 2) as i:
                    for c in range(2):
                        made_rows(2 * i + c, c)

            all_made_rows(0, CHUNKS_BEFORE)
            with act.Fori(0, SORT_ITER) as i:
                for k in range(SORT_TILES):
                    for s in SORTS:
                        act.wait_ge(counted[s], SORT_TILES * i + (k + 1))
                        nc.scalar.copy(count_hi[s][:, k, :], ps_count[s]).then_inc(count_hi_ready[s], 1)
                    if k in (1, 3):
                        made_rows(2 * i + (CHUNKS_BEFORE + k // 2), k // 2)
            all_made_rows(CHUNKS - CHUNKS_AFTER, CHUNKS)

        @block.vector
        def _(dve):
            v = nc.vector
            steps = [0]

            def chain(ins):
                steps[0] += 1
                ins.then_inc(dve_step, 1)
                dve.wait_ge(dve_step, steps[0])

            dve.wait_ge(edges_in, 48)
            for s in SORTS:
                target, source = (dst_i, src_i) if s == 0 else (src_i, dst_i)
                v.tensor_scalar(low_i[s][:], target[:], P - 1, None, ALU.bitwise_and)
                v.tensor_scalar(high_i[s][:], target[:], 7, None, ALU.logical_shift_right)
                v.tensor_copy(type_f[:], type_i[:])
                chain(v.tensor_copy(pay[s][:], source[:]))
                v.tensor_copy(low[s][:], low_i[s][:])
                chain(v.tensor_copy(klass[s][:], high_i[s][:]))
                if s:
                    chain(v.scalar_tensor_tensor(out=klass[s][:], in0=type_f[:], scalar=float(NODE_TILES),
                                                 in1=klass[s][:], op0=ALU.mult, op1=ALU.add))
                v.tensor_copy(low_b[s][:], low[s][:])
                v.tensor_copy(klass_b[s][:], klass[s][:])
                v.scalar_tensor_tensor(out=key[s][:], in0=klass[s][:], scalar=float(P), in1=low[s][:],
                                       op0=ALU.mult, op1=ALU.add).then_inc(keys_ready[s], 1)
            dve.wait_ge(const_ready, 1)
            chain(v.tensor_scalar(part_int[:], part_int[:], QUARTERS - 1, None, ALU.bitwise_and))
            chain(v.tensor_copy(quarter[:], part_int[:]))
            chain(v.tensor_scalar(is_quarter[:], iota_row[0:BP, 0:QUARTERS], quarter[0:BP, 0:1], None, ALU.is_equal))
            dve.wait_ge(att_in, 32)
            for n in range(2):
                for r in range(RELATIONS):
                    done = v.tensor_scalar(m.mix[:, n, QUARTERS * r:QUARTERS * (r + 1)], is_quarter[:],
                                           att[:, n, r:r + 1], None, ALU.mult)
            done.then_inc(mix_ready, 1)
            for s in SORTS:
                n = CLASSES[s]
                v.tensor_tensor(one_low[s][:], deep(iota_b[0:EP, 0:P], ET), wide(low_b[s][:], P), ALU.is_equal)
                v.tensor_tensor(one_class[s][:], deep(iota_b[0:EP, 0:n], ET), wide(klass_b[s][:], n), ALU.is_equal
                                ).then_inc(onehot_ready[s], 1)
            for s in SORTS:
                dve.wait_ge(rows_in[s], 32)
                v.tensor_scalar(low_T[s], low_row[s][:].rearrange("b (p t) -> b t p", t=ET), iota_part[:, 0:1],
                                None, ALU.is_equal)
            for s in SORTS:
                n = CLASSES[s]
                dve.wait_ge(hist_ready[s], 1)
                v.tensor_copy(hist[s][:, 0:n], ps_count[s]).then_inc(hist_copied[s], 1)
                dve.wait_ge(sums_ready[s], 1)
                chain(v.tensor_tensor_scan(upto[s][:, 0:n], ones[:, 0:n], ps_all[s], 0.0, ALU.mult, ALU.add))
                chain(v.tensor_tensor(start[s][:, 0:n], upto[s][:, 0:n], ps_all[s], ALU.subtract))
                chain(v.tensor_tensor(start[s][:, 0:n], start[s][:, 0:n], ps_below[s], ALU.add))
                if s:
                    edges_0 = upto[s][:, NODE_TILES - 1:NODE_TILES]
                    chain(v.tensor_scalar(split_f[:, 0:1], edges_0, float(PAIR - 1), None, ALU.add))
                    chain(v.tensor_copy(split_i[:, 0:1], split_f[:, 0:1]))
                    chain(v.tensor_scalar(split_i[:, 0:1], split_i[:, 0:1], 8, None, ALU.logical_shift_right))
                    v.tensor_copy(m.pairs_0[:], split_i[:, 0:1])
                    chain(v.tensor_copy(split_f[:, 1:2], split_i[:, 0:1]))
                    chain(v.scalar_tensor_tensor(out=split_f[:, 2:3], in0=split_f[:, 1:2], scalar=float(PAIR),
                                                 in1=edges_0, op0=ALU.mult, op1=ALU.subtract))
                    chain(v.tensor_scalar(start[s][:, NODE_TILES:n], start[s][:, NODE_TILES:n], split_f[:, 2:3],
                                          None, ALU.add))
                dve.sem_inc(start_ready[s], 1)
            key_of = [key_row[s][0:EP, :].rearrange("b (p t) -> b t p", t=ET) for s in SORTS]
            with dve.Fori(0, SORT_ITER) as i:
                for k in range(SORT_TILES):
                    t = SORT_TILES * i + k
                    for s in SORTS:
                        dve.wait_ge(count_hi_ready[s], t + 1)
                        v.tensor_tensor(count_lo[s][:, k, :], ps_count[s], count_hi[s][:, k, :], ALU.subtract
                                        ).then_inc(count_ready[s], 1)
                    dve.wait_ge(count_ready[1], t + 1)
                    for s in SORTS:
                        v.scalar_tensor_tensor(out=junk[:, 0, s, 0:EP],
                                               in0=key_of[s][:, bass.ds(t, 1), :].rearrange("b a p -> b (a p)"),
                                               scalar=key[s][:, bass.ds(t, 1)], in1=before_edge[:],
                                               op0=ALU.is_equal, op1=ALU.mult, accum_out=rank[s][:, bass.ds(t, 1)])
                    for s in SORTS:
                        dve.wait_ge(looked[s], t + 1)
                        v.scalar_tensor_tensor(out=junk[:, 1, s, 0:CLASSES[s]],
                                               in0=one_class[s][:, bass.ds(t, 1), :].rearrange("p a b -> p (a b)"),
                                               scalar=1.0, in1=ps_look(s, k),
                                               op0=ALU.mult, op1=ALU.mult, accum_out=base[s][:, bass.ds(t, 1)])
            chain(v.drain())
            for s in SORTS:
                chain(v.tensor_tensor(pos[s][:], base[s][:], rank[s][:], ALU.add))
                chain(v.tensor_copy(pos_i[s][:], pos[s][:]))
                v.tensor_scalar(tile_i[s][:], pos_i[s][:], 7, None, ALU.logical_shift_right)
                v.tensor_scalar(vals[s][:, 0, :], key[s][:], 1.0, None, ALU.add)
                v.tensor_copy(vals[s][:, 1, :], pay[s][:])
                chain(v.tensor_scalar(slot_i[s][:], pos_i[s][:], P - 1, None, ALU.bitwise_and))
                v.tensor_copy(vals_hi[s][:], vals[s][:])
                v.tensor_copy(tile_f[s][:], tile_i[s][:])
                chain(v.tensor_copy(slot_f[s][:], slot_i[s][:]))
                v.tensor_tensor(vals_lo[s][:], vals[s][:], vals_hi[s][:], ALU.subtract)
                v.tensor_tensor(one_slot[s], deep(iota_b[0:EP, 0:P], ET), wide(slot_f[s][:], P), ALU.is_equal)
                chain(v.tensor_tensor(one_tile[s], deep(iota_b[0:EP, 0:POS_TILES], ET),
                                      wide(tile_f[s][:], POS_TILES), ALU.is_equal))
                for h, part in enumerate((vals_hi[s], vals_lo[s])):
                    for k in range(2):
                        done = v.tensor_tensor(put[s][:, h, :, k, :], one_tile[s], wide(part[:, k, :], POS_TILES),
                                               ALU.mult)
                done.then_inc(put_ready[s], 1)
            for s in SORTS:
                n = CLASSES[s]
                v.tensor_scalar(empty[:, 0:n], hist[s][:, 0:n], 0.0, NO_EDGE, ALU.is_equal, ALU.mult)
                chain(v.tensor_tensor(last[:, 0:n], start[s][:, 0:n], hist[s][:, 0:n], ALU.add))
                chain(v.scalar_tensor_tensor(out=last[:, 0:n], in0=last[:, 0:n], scalar=-1.0, in1=empty[:, 0:n],
                                             op0=ALU.add, op1=ALU.add))
                chain(v.tensor_copy(m.last_edge[s][:, 0:n], last[:, 0:n]))
            chain(v.tensor_scalar(m.per_edge[:], hist[0][:, 0:NODE_TILES], 1.0, None, ALU.max))
            v.reciprocal(m.per_edge[:], m.per_edge[:])
            dve.wait_ge(bias_in, 16 * (2 * len(m.biases) + 2))
            v.tensor_copy(m.row_pick[:], m.row_pick_f[:])
            chain(v.tensor_copy(m.bias_rows[:], bias_f))
            chain(v.tensor_tensor(m.bias_rows[32:33], bias_f[32:33], m.bias_rows[32:33].bitcast(F32), ALU.subtract))
            for s in SORTS:
                dve.wait_ge(put_done[s], 1)
                v.tensor_copy(m.row_of[s][:], ps_put[s][:, POS_TILES:2 * POS_TILES])
                v.tensor_copy(keys_out[s][:, 0:POS_TILES], ps_put[s][:, 0:POS_TILES]).then_inc(keys_out_ready[s], 1)
                dve.wait_ge(keys_turned[s], 1)
                v.tensor_copy(keys_T[s][:], ps_keys[s][0:POS_TILES, :]).then_inc(keys_T_ready[s], 1)
            for s in SORTS:
                dve.wait_ge(sorted_in[s], 16)
                v.memset(m.same[s][:, 0:1], 0.0)
                v.tensor_tensor(m.same[s][:, 1:POSITIONS], sorted_row[s][:, 1:POSITIONS],
                                sorted_row[s][:, 0:POSITIONS - 1], ALU.is_equal)

        inner.close()
        clear(nc, mine)


def shared(nc, ctx, m):
    def sb(name, shape, dt):
        return ctx.enter_context(nc.sbuf_tensor(name, shape, dt))

    m.psum = ctx.enter_context(nc.psum_tensor("psum", [P, 8, 512], F32))
    m.ident = sb("ident", [P, P], F32)
    m.row_pick_f = sb("row_pick_f", [P, P], F32)
    m.row_pick = sb("row_pick", [P, P], F32R)
    m.bias_rows = sb("bias_rows", [P, 3, D], F32R)
    m.gamma_b = sb("gamma_b", [P, D], F32)
    m.beta_b = sb("beta_b", [P, D], F32)
    m.gate_b = sb("gate_b", [P, RELATIONS * D], F32)
    m.same = [sb(f"same{s}", [P, POSITIONS], BF16) for s in range(2)]
    m.row_of = [sb(f"row_of{s}", [P, POS_TILES], I32) for s in range(2)]
    m.last_edge = [sb(f"last_edge{s}", [P, CLASSES[s]], I32) for s in range(2)]
    m.per_edge = sb("per_edge", [P, NODE_TILES], F32)
    m.pairs_0 = sb("pairs_0", [P, 1], I32)
    m.zeros = sb("zeros", [P, 1], F32)
    m.mix = sb("mix", [BP, 2, 32], F32)
    m.chunk = sb("chunk", [BP, 2, CHUNK_Q * D], F32)
    m.made = sb("made", [P, 2, D], F32)
    m.key_d = [nc.dram_tensor(f"key_d{s}", [EDGES], F32).ap() for s in range(2)]
    m.low_d = [nc.dram_tensor(f"low_d{s}", [EDGES], BF16).ap() for s in range(2)]
    m.sorted_d = [nc.dram_tensor(f"sorted_d{s}", [POSITIONS], F32).ap() for s in range(2)]


class At:

    def __init__(self, ring, j, o, early=False):
        self.ring, self.j, self.o, self.early = ring, j, o, early

    def back(self, k):
        return At(self.ring, self.j, self.o - k, self.early)

    def count(self, per=1, more=0):
        return per * self.ring * self.j + (per * (self.o + 1) + more)

    def index(self, per=1, more=0):
        return per * self.ring * self.j + (per * self.o + more)

    def slot(self, n):
        return self.o % n

    def uses(self, n, per=1, more=0):
        return per * (self.ring // n) * self.j + (per * (self.o // n + 1) + more)

    def within(self, steps):
        return not isinstance(self.j, int) or 0 <= self.ring * self.j + self.o < steps

    def is_step(self, n):
        return isinstance(self.j, int) and self.ring * self.j + self.o == n


def sweep(eng, ring, full, steps, skew, step, early=0, after_early=None):
    loops = full // ring
    for o in range(ring):
        step(At(ring, 0, o, ring * early > o))
    for lo, hi in ((1, min(early, loops)), (max(early, 1), loops)):
        if lo < hi:
            with eng.Fori(lo, hi) as j:
                for o in range(ring):
                    step(At(ring, j, o, lo < early))
        if lo < early and after_early:
            after_early()
    for o in range(loops * ring, steps + skew):
        step(At(ring, 0, o, ring * early > o))


def load_weights(sp, m, stage, load, loaded):
    for n, w in enumerate(load):
        sp.dma_start(stage[:, n * KC:(n + 1) * KC, :], w.rearrange("(c p) o -> p c o", p=P)).then_inc(loaded, 16)


def product(nc, m, out, slot, c, w_hi, w_lo, bias):
    if bias is not None:
        nc.tensor.matmul(out, m.row_pick[:], m.bias_rows[:, bias, :], start=True, stop=False)
    for k in range(KC):
        hi = m.x_hi[:, slot, k, c * P:(c + 1) * P]
        lo = m.x_lo[:, slot, k, c * P:(c + 1) * P]
        nc.tensor.matmul(out, hi, w_hi(k), start=(bias is None and k == 0), stop=False)
        nc.tensor.matmul(out, hi, w_lo(k), start=False, stop=False)
        done = nc.tensor.matmul(out, lo, w_hi(k), start=False, stop=(k == KC - 1))
    return done


def transposes(nc, m, source, slot, tiles):
    turned = m.turned(slot)
    for c in range(tiles):
        for k in range(KC):
            done = nc.tensor.transpose(turned[:, k, c * P:(c + 1) * P], source[:, c, k * P:(k + 1) * P], m.ident[:])
    return done


def basis_group(nc, m, layer, slot, bank):
    for j in range(4):
        done = nc.tensor.matmul(m.psum[32 * j:32 * j + 32, bank, :], m.mix[:, layer, :],
                                m.chunk[:, slot, j * D:(j + 1) * D], start=True, stop=True)
    return done


def load_chunk(eng, m, layer, slot, chunk, loaded):
    basis_rows = m.basis[layer].rearrange("b (i q) o -> (b i) (q o)", i=QUARTERS)
    eng.dma_start(m.chunk[:, slot, :], basis_rows[:, bass.ds(chunk * (CHUNK_Q * D), CHUNK_Q * D)]
                  ).then_inc(loaded[slot], 16)


def store_made(eng, m, layer, slot, chunk, stored):
    w_rows = m.w_made[layer].rearrange("r (i q) o -> (r i) q o", i=QUARTERS)
    for j in range(CHUNK_Q):
        rows = w_rows[:, bass.ds(CHUNK_Q * chunk + j, 1), :].rearrange("a q o -> a (q o)")
        eng.dma_start(rows, m.made[32 * j:32 * j + RELATIONS * QUARTERS, slot]).then_inc(stored[slot], 16)


def layer(nc, m, kind, source, out, table, edge_weights=None):
    s = 1 if kind else 0
    gated = kind > 0
    relations = RELATIONS if gated else 1
    e_ring, n_ring = 4, 6
    e_steps = EDGE_STEPS if gated else EDGE_STEPS_0
    steps, full = NODE_STEPS, NODES // PAIR
    norm = kind != 1
    store_lag = (6, 4, 5)[kind]
    positions = PAIR * e_steps
    n_early = (CHUNKS - EDGE_STEPS_0) // n_ring if kind == 0 else 0
    with ExitStack() as ctx:
        inner = ctx.enter_context(ExitStack())
        mine = []

        def sem(what):
            mine.append(ctx.enter_context(nc.semaphore(f"layer{kind}_{what}")))
            return mine[-1]

        e_index_ready = sem("e_index_ready")
        e_index_seen = sem("e_index_seen")
        e_rows_in = [sem(f"e_rows_in{i}") for i in range(e_ring)]
        e_logits_ready = sem("e_logits_ready")
        e_gates_ready = sem("e_gates_ready")
        e_scaled = sem("e_scaled")
        e_turned = sem("e_turned")
        e_summed = sem("e_summed")
        e_hi_ready = sem("e_hi_ready")
        e_lo_ready = sem("e_lo_ready")
        e_multiplied = sem("e_multiplied")
        e_copied = sem("e_copied")
        e_stored = [sem(f"e_stored{i}") for i in range(e_ring)]
        zeroed = sem("zeroed")
        rows_in = [sem(f"rows_in{i}") for i in range(n_ring)]
        rows_free = sem("rows_free")
        extra_in = [sem(f"extra_in{i}") for i in range(2)]
        turned = sem("turned")
        hi_ready = sem("hi_ready")
        lo_ready = sem("lo_ready")
        multiplied = sem("multiplied")
        cleared = sem("cleared")
        index_ready = sem("index_ready")
        index_seen = sem("index_seen")
        edges_in = [sem(f"edges_in{i}") for i in range(2)]
        part_added = sem("part_added")
        added = sem("added")
        squared = sem("squared")
        stat_step = sem("stat_step")
        var_ready = sem("var_ready")
        std_ready = sem("std_ready")
        norm_ready = sem("norm_ready")
        normed = sem("normed")
        gained = sem("gained")
        shifted = sem("shifted")
        resid_squared = sem("resid_squared")
        ready = sem("ready")
        result, result_ring = (m.y, 2) if kind == 0 else (m.t, 3)
        stored = [sem(f"stored{i}") for i in range(result_ring)]
        gate_in = sem("gate_in")
        edge_w_in = sem("edge_w_in")
        node_w_in = sem("node_w_in")
        edge_hi = sem("edge_hi")
        edge_lo = sem("edge_lo")
        node_hi = sem("node_hi")
        node_lo = sem("node_lo")
        basis_in = [sem(f"basis_in{i}") for i in range(2)]
        basis_done = sem("basis_done")
        basis_copied = sem("basis_copied")
        basis_stored = [sem(f"basis_stored{i}") for i in range(2)]

        table_rows = table.rearrange("(q c p) o -> q p c o", c=2, p=P)
        we_hi, we_lo, we_in = m.w_edge_hi, m.w_edge_lo, m.w_edge_stage
        next_edge = kind < 2
        NEXT_STEPS = range(1, 5)
        block = inner.enter_context(nc.Block())

        def tiles(now):
            return 1 if now.is_step(steps - 1) else 2

        def rows_of(ap, now):
            if tiles(now) == 1:
                return ap[full * PAIR:NODES, :].unsqueeze(1), LAST_ROWS, 1
            block_rows = ap[0:full * PAIR, :].rearrange("(q c p) o -> q p c o", c=2, p=P)
            return block_rows[bass.ds(now.index(), 1)].rearrange("a p c o -> (a p) c o"), P, 2

        def gathered(now):
            per = 16 * 2 * relations
            if tiles(now) == 1:
                return now.uses(2, per) - per // 2
            return now.uses(2, per)

        def all_edges_stored(eng):
            for slot in range(e_ring):
                eng.wait_ge(e_stored[slot], 16 * len(range(slot, e_steps, e_ring)) + 16)

        @block.sync
        def _(sp):
            if edge_weights:
                load_weights(sp, m, m.w_edge_stage, edge_weights, edge_w_in)
            if gated:
                sp.dma_start(m.gate_b[:], m.gate_w[kind - 1].rearrange("r h o -> (r h o)").partition_broadcast(P)
                             ).then_inc(gate_in, 16)
            load_weights(sp, m, m.w_node_stage, [m.node_weights[kind]], node_w_in)

            def edge_step(at):
                if at.within(e_steps):
                    sp.wait_ge(basis_done, at.count())
                    load_chunk(sp, m, 1, at.slot(2), at.index(), basis_in)
                now = at.back(1)
                if now.within(e_steps):
                    sp.wait_ge(basis_copied, now.count())
                    store_made(sp, m, 1, now.slot(2), now.index(), basis_stored)

            if kind == 0:
                sweep(sp, e_ring, e_steps, e_steps, 1, edge_step)
            sp.wait_ge(e_turned, e_steps + e_ring)

            def step(at):
                now = at
                if now.within(steps):
                    rows, p, c = rows_of(source, now)
                    sp.wait_ge(rows_free if kind == 0 else turned, now.count())
                    sp.dma_start(m.x[0:p, now.slot(n_ring), 0:c], rows).then_inc(rows_in[now.slot(n_ring)], 16)
                    if now.early:
                        sp.wait_ge(basis_done, now.count(1, e_steps))
                        load_chunk(sp, m, 1, now.slot(2), now.index(1, e_steps), basis_in)
                now = at.back(2)
                if kind == 2 and now.within(steps):
                    rows, p, c = rows_of(m.x1, now)
                    if now.is_step(0):
                        sp.wait_ge(e_lo_ready, e_steps + 1)
                    sp.wait_ge(added, now.count())
                    sp.dma_start(m.y[0:p, now.slot(2), 0:c], rows).then_inc(extra_in[now.slot(2)], 16)
                if at.early and not at.is_step(0):
                    made_rows_out(at.back(1))
                now = at.back(store_lag)
                if now.within(steps):
                    rows, p, c = rows_of(out, now)
                    sp.wait_ge(ready, now.count())
                    sp.dma_start(rows, result[0:p, now.slot(result_ring), 0:c]
                                 ).then_inc(stored[now.slot(result_ring)], 16)
                if next_edge and at.is_step(0):
                    sp.wait_ge(edge_lo, 1)
                    load_weights(sp, m, m.w_edge_stage, m.made_weights[kind], edge_w_in)

            def made_rows_out(now):
                sp.wait_ge(basis_copied, now.count(1, e_steps))
                store_made(sp, m, 1, now.slot(2), now.index(1, e_steps), basis_stored)

            sweep(sp, n_ring, full, steps, store_lag, step, n_early, lambda: made_rows_out(At(n_ring, n_early, -1)))
            for slot in range(result_ring):
                sp.wait_ge(stored[slot], 16 * len(range(slot, steps, result_ring)) + 16)
            if kind == 0:
                for slot in range(2):
                    sp.wait_ge(basis_stored[slot], 64 * (CHUNKS // 2 + 1))

        @block.gpsimd
        def _(pool):
            def edge_step(now):
                if not now.within(e_steps):
                    return
                slot = now.slot(e_ring)
                pool.wait_ge(e_turned, now.count())
                nc.gpsimd.tensor_copy(m.index[:, 2 * slot:2 * slot + 2],
                                      m.row_of[s][:, bass.ds(now.index(2), 2)]).then_inc(e_index_ready, 1)
                pool.wait_ge(e_index_ready, now.count())
                pool.sem_inc(e_index_seen, 1)
                for c in range(2):
                    index = m.index[:, 2 * slot + c:2 * slot + c + 1]
                    pool.indirect_dma_start(out=m.x[:, slot, c, :], out_offset=None, in_=source,
                                            in_offset=bass.IndirectOffsetOnAxis(ap=index, axis=0),
                                            bounds_check=NODES - 1, oob_is_err=False).then_inc(e_rows_in[slot], 16)

            sweep(pool, e_ring, e_steps, e_steps, 0, edge_step)
            all_edges_stored(pool)

            def gathers(now):
                slot = now.slot(2)
                n = tiles(now)
                pool.wait_ge(cleared if kind else added, now.count())
                for r in range(relations):
                    done = nc.gpsimd.tensor_copy(
                        m.index[:, 4 * slot + 2 * r:4 * slot + 2 * r + n],
                        m.last_edge[s][:, bass.ds(now.index(2, r * NODE_TILES), n)])
                if kind == 0:
                    done = nc.gpsimd.memset(m.g[:, 0, slot], 0.0)
                done.then_inc(index_ready, 1)
                pool.wait_ge(index_ready, now.count())
                pool.sem_inc(index_seen, 1)
                for r in range(relations):
                    for c in range(n):
                        at_index = 4 * slot + 2 * r + c
                        pool.indirect_dma_start(
                            out=m.g[:, r, slot, c, :], out_offset=None, in_=table[0:positions],
                            in_offset=bass.IndirectOffsetOnAxis(ap=m.index[:, at_index:at_index + 1], axis=0),
                            bounds_check=positions - 1, oob_is_err=False).then_inc(edges_in[slot], 16)

            def step(at):
                if at.within(steps):
                    gathers(at)
                now = at.back(3)
                if kind == 0 and now.within(steps):
                    slot, n = now.slot(3), tiles(now)
                    pool.wait_ge(normed, now.count())
                    nc.gpsimd.tensor_tensor(m.t[:, slot, 0:n], m.t[:, slot, 0:n], deep(m.gamma_b[:], n), ALU.mult
                                            ).then_inc(gained, 1)

            sweep(pool, n_ring, full, steps, 3, step)

        @block.tensor
        def _(pe):
            pe.sem_inc(e_turned, e_ring)
            pe.sem_inc(e_multiplied, 2)
            pe.sem_inc(basis_done, 2)
            if gated:
                pairs_0 = pe.value_load(m.pairs_0[0:1, 0:1], min_val=0, max_val=EDGE_STEPS_0)
            if edge_weights:
                pe.wait_ge(edge_lo, 1)

            def edge_step(at):
                now = at.back(1)
                if now.within(e_steps):
                    if gated:
                        pe.wait_ge(e_scaled, now.count())
                    else:
                        pe.wait_ge(e_rows_in[now.slot(e_ring)], now.uses(e_ring, 32))
                    pe.wait_ge(e_summed, now.count())
                    if kind == 0:
                        pe.wait_ge(basis_copied, now.count())
                    transposes(nc, m, m.x[:, now.slot(e_ring)], now.slot(2), 2).then_inc(e_turned, 1)
                relation = 0
                now = at.back(3)
                if now.within(e_steps):
                    pe.wait_ge(e_lo_ready, now.count(1, 1))
                    pe.wait_ge(e_copied, now.count())
                    if gated:
                        relation = (now.index() >= pairs_0) * KC

                def chunk_of(w, k):
                    if not gated:
                        return w[:, k, :]
                    return w[:, bass.ds(relation + k, 1), :].rearrange("p a o -> p (a o)")

                for c in range(2):
                    if now.within(e_steps):
                        done = product(nc, m, m.product(now.slot(2))[:, c, :], now.slot(2), c,
                                       lambda k: chunk_of(we_hi, k), lambda k: chunk_of(we_lo, k), None)
                    if kind == 0 and c == 0 and at.within(e_steps):
                        pe.wait_ge(basis_in[at.slot(2)], at.uses(2, 16))
                        pe.wait_ge(e_summed, at.count())
                        basis_group(nc, m, 1, at.slot(2), 2 * at.slot(2)).then_inc(basis_done, 1)
                if now.within(e_steps):
                    done.then_inc(e_multiplied, 1)

            sweep(pe, e_ring, e_steps, e_steps, 3, edge_step)

            pe.sem_inc(multiplied, 2)
            pe.sem_inc(turned, n_ring)
            pe.wait_ge(e_summed, e_steps + 2)

            def step(at):
                now = at
                if now.within(steps):
                    pe.wait_ge(rows_in[now.slot(n_ring)], now.uses(n_ring, 16))
                    pe.wait_ge(lo_ready, now.count())
                    if kind == 0:
                        pe.wait_ge(basis_copied, now.index(1, e_steps) if now.early else CHUNKS)
                    done = transposes(nc, m, m.x[:, now.slot(n_ring)], now.slot(2), tiles(now))
                    done.then_inc(turned, 1)
                now = at.back(1)
                if now.within(steps):
                    if now.is_step(0):
                        pe.wait_ge(node_lo, 1)
                        pe.wait_ge(e_copied, e_steps + 2)
                    pe.wait_ge(lo_ready, now.count(1, 2))
                    pe.wait_ge(added, now.count())
                for c in range(2):
                    if now.within(steps) and c < tiles(now):
                        done = product(nc, m, m.product(now.slot(2))[:, c, :], now.slot(2), c,
                                       lambda k: m.w_node_hi[:, k, :], lambda k: m.w_node_lo[:, k, :], kind)
                    if at.early and c == 0:
                        pe.wait_ge(basis_in[at.slot(2)], at.uses(2, 16, 16 * (e_steps // 2)))
                        pe.wait_ge(lo_ready, at.count(1, 1))
                        basis_group(nc, m, 1, at.slot(2), 2 * (1 - at.slot(2))).then_inc(basis_done, 1)
                if now.within(steps):
                    done.then_inc(multiplied, 1)

            sweep(pe, n_ring, full, steps, 1, step, n_early)

        @block.vector
        def _(dve):
            v = nc.vector
            dve.sem_inc(e_summed, 2)
            dve.sem_inc(e_lo_ready, 1)
            if kind == 0:
                v.memset(m.sum4[:], 0.0)
                v.memset(m.sq4[:], 0.0)
            v.memset(m.sums[:, 1, :, PAIR - 1:PAIR], 0.0).then_inc(zeroed, 1)
            if edge_weights:
                dve.wait_ge(edge_hi, 1)
                v.tensor_tensor(we_lo[:, 0:KC], we_in[:, 0:KC], we_hi[:, 0:KC].bitcast(F32), ALU.subtract
                                ).then_inc(edge_lo, 1)
            else:
                dve.sem_inc(edge_lo, 1)
            if gated:
                pairs_0 = dve.value_load(m.pairs_0[0:1, 0:1], min_val=0, max_val=EDGE_STEPS_0)
            dve.wait_ge(zeroed, 1)
            if gated:
                dve.wait_ge(gate_in, 16)

            def copy_made(at, more):
                slot = at.slot(2)
                dve.wait_ge(basis_done, at.count(1, 2 + more))
                dve.wait_ge(basis_stored[slot], at.uses(2, 64, 64 * (more // 2)))
                bank = 2 * (slot if more == 0 else 1 - slot)
                v.tensor_copy(m.made[:, slot], m.psum[:, bank, :]).then_inc(basis_copied, 1)

            def edge_step(at):
                now = at.back(2)
                if now.within(e_steps):
                    slot = now.slot(2)
                    dve.wait_ge(e_turned, now.count(1, e_ring))
                    dve.wait_ge(e_lo_ready, now.count())
                    for k in range(KC):
                        done = v.tensor_tensor_scan(m.sums[:, slot, k, :],
                                                    m.same[s][:, bass.ds(now.index(PAIR), PAIR)],
                                                    m.turned(slot)[:, k, :], m.sums[:, 1 - slot, k, PAIR - 1:PAIR],
                                                    ALU.mult, ALU.add)
                    done.then_inc(e_summed, 1)
                if gated and at.within(e_steps):
                    slot = at.slot(e_ring)
                    relation = (at.index() >= pairs_0) * D
                    dve.wait_ge(e_rows_in[slot], at.uses(e_ring, 32))
                    for c in range(2):
                        done = v.scalar_tensor_tensor(out=m.g[:, 0, slot % 2, c, :], in0=m.x[:, slot, c, :],
                                                      scalar=1.0, in1=m.gate_b[:, bass.ds(relation, D)],
                                                      op0=ALU.mult, op1=ALU.mult,
                                                      accum_out=m.logits[:, slot, c:c + 1])
                    done.then_inc(e_logits_ready, 1)
                if now.within(e_steps):
                    slot = now.slot(2)
                    dve.wait_ge(e_hi_ready, now.count())
                    v.tensor_tensor(m.x_lo[:, slot], m.sums[:, slot], m.x_hi[:, slot].bitcast(F32),
                                    ALU.subtract).then_inc(e_lo_ready, 1)
                if kind == 0 and at.within(e_steps):
                    copy_made(at, 0)
                if at.is_step(3):
                    dve.wait_ge(node_hi, 1)
                    v.tensor_tensor(m.w_node_lo[:], m.w_node_stage[:], m.w_node_hi[:].bitcast(F32), ALU.subtract
                                    ).then_inc(node_lo, 1)

            if kind == 0:
                for slot in range(2):
                    dve.sem_inc(basis_stored[slot], 64)
            sweep(dve, e_ring, e_steps, e_steps, 2, edge_step)

            dve.sem_inc(lo_ready, 2)
            dve.sem_inc(added, 2)
            for slot in range(result_ring):
                dve.sem_inc(stored[slot], 16)
            dve.sem_inc(norm_ready, 1)
            if kind == 0:
                dve.sem_inc(rows_free, n_ring)
            dve.wait_ge(e_lo_ready, e_steps + 1)

            def step(at):
                first, second = at.back(3), at.back(5)
                stats = norm and (first.within(steps) or (kind == 0 and second.within(steps)))
                if stats:
                    if first.within(steps):
                        dve.wait_ge(squared, first.count())
                    if kind == 0 and second.within(steps):
                        dve.wait_ge(resid_squared, second.count())
                    past = at.back(1).slot(2)
                    turn = first.index()
                    dve.wait_ge(norm_ready, turn + 1)
                    v.tensor_scalar(m.neg_mean[:], m.sum4[:, past], -1.0 / D, None, ALU.mult)
                    v.tensor_scalar(m.mean_sq[:], m.sq4[:, past], 1.0 / D, LN_EPS, ALU.mult, ALU.add
                                    ).then_inc(stat_step, 1)
                    dve.wait_ge(stat_step, 3 * turn + 1)
                    v.tensor_tensor(m.var[:], m.neg_mean[:], m.neg_mean[:], ALU.mult).then_inc(stat_step, 1)
                    dve.wait_ge(stat_step, 3 * turn + 2)
                    v.tensor_tensor(m.var[:], m.mean_sq[:], m.var[:], ALU.subtract).then_inc(var_ready, 1)
                now = at.back(2)
                if now.within(steps):
                    slot, n, t = now.slot(2), tiles(now), now.slot(3)
                    if now.is_step(0):
                        all_edges_stored(dve)
                    dve.wait_ge(multiplied, now.count(1, 2))
                    dve.wait_ge(edges_in[slot], gathered(now))
                    product_of, sums = m.product(slot), m.t[:, t]
                    if kind == 0:
                        for c in range(n):
                            done = v.scalar_tensor_tensor(
                                out=sums[:, c, :], in0=m.g[:, 0, slot, c, :],
                                scalar=m.per_edge[:, bass.ds(now.index(2, c), 1)], in1=product_of[:, c, :],
                                op0=ALU.mult, op1=ALU.add, accum_out=m.sum4[:, at.slot(2), c:c + 1])
                        done.then_inc(added, 1)
                    else:
                        dve.wait_ge(stored[t], now.uses(3, 16))
                        v.tensor_tensor(sums[:, 0:n], product_of[:, 0:n], m.g[:, 0, slot, 0:n], ALU.add
                                        ).then_inc(part_added, 1)
                        dve.wait_ge(part_added, now.count(kind, 1 - kind))
                        if kind == 1:
                            v.tensor_tensor(sums[:, 0:n], sums[:, 0:n], m.g[:, 1, slot, 0:n], ALU.add
                                            ).then_inc(added, 1)
                        else:
                            v.tensor_tensor(sums[:, 0:n], sums[:, 0:n], m.g[:, 1, slot, 0:n], ALU.add
                                            ).then_inc(part_added, 1)
                            dve.wait_ge(part_added, now.count(2))
                            dve.wait_ge(extra_in[slot], now.uses(2, 16))
                            for c in range(n):
                                done = v.scalar_tensor_tensor(
                                    out=sums[:, c, :], in0=sums[:, c, :], scalar=1.0, in1=m.y[:, slot, c, :],
                                    op0=ALU.mult, op1=ALU.add, accum_out=m.sum4[:, at.slot(2), c:c + 1])
                            done.then_inc(added, 1)
                if stats:
                    dve.wait_ge(std_ready, first.count())
                    v.reciprocal(m.rstd[:, at.slot(2)], m.std[:]).then_inc(stat_step, 1)
                    dve.wait_ge(stat_step, 3 * turn + 3)
                    v.tensor_tensor(m.shift[:, at.slot(2)], m.neg_mean[:], m.rstd[:, at.slot(2)], ALU.mult
                                    ).then_inc(norm_ready, 1)
                now = at.back(4)
                if kind == 0 and now.within(steps):
                    slot, n = now.slot(3), tiles(now)
                    dve.wait_ge(gained, now.count())
                    v.tensor_tensor(m.t[:, slot, 0:n], m.t[:, slot, 0:n], deep(m.beta_b[:], n), ALU.add
                                    ).then_inc(shifted, 1)
                    dve.wait_ge(shifted, now.count())
                    dve.wait_ge(stored[now.slot(2)], now.uses(2, 16))
                    for c in range(n):
                        done = v.scalar_tensor_tensor(
                            out=m.y[:, now.slot(2), c, :], in0=m.t[:, slot, c, :], scalar=0.0,
                            in1=m.x[:, now.slot(n_ring), c, :], op0=ALU.max, op1=ALU.add,
                            accum_out=m.sum4[:, at.slot(2), 2 + c:3 + c])
                    done.then_inc(rows_free, 1)
                if at.early:
                    copy_made(at, e_steps)
                now = at
                if now.within(steps):
                    slot, n = now.slot(2), tiles(now)
                    dve.wait_ge(hi_ready, now.count())
                    v.tensor_tensor(m.x_lo[:, slot, :, 0:n * P], m.turned(slot)[:, :, 0:n * P],
                                    m.x_hi[:, slot, :, 0:n * P].bitcast(F32), ALU.subtract).then_inc(lo_ready, 1)
                if next_edge and any(at.is_step(n) for n in NEXT_STEPS):
                    part = at.o - NEXT_STEPS[0]
                    k = slice(2 * part, 2 * part + 2)
                    dve.wait_ge(edge_hi, part + 1 + len(edge_weights or ()))
                    v.tensor_tensor(we_lo[:, k], we_in[:, k], we_hi[:, k].bitcast(F32), ALU.subtract
                                    ).then_inc(edge_lo, 1)

            sweep(dve, n_ring, full, steps, 5 if kind == 0 else 3, step, n_early)

        @block.scalar
        def _(act):
            act.sem_inc(e_copied, 2)
            for slot in range(e_ring):
                act.sem_inc(e_stored[slot], 16)
            if edge_weights:
                act.wait_ge(edge_w_in, 16)
                nc.scalar.copy(we_hi[:, 0:KC], we_in[:, 0:KC]).then_inc(edge_hi, 1)

            def edge_step(at):
                now = at.back(2)
                if now.within(e_steps):
                    slot = now.slot(2)
                    act.wait_ge(e_summed, now.count(1, 2))
                    act.wait_ge(e_multiplied, now.count())
                    nc.scalar.copy(m.x_hi[:, slot], m.sums[:, slot]).then_inc(e_hi_ready, 1)
                now = at
                if gated and now.within(e_steps):
                    slot = now.slot(e_ring)
                    act.wait_ge(e_logits_ready, now.count())
                    nc.scalar.activation(m.gates[:, slot, :], m.logits[:, slot, :], ACT.Sigmoid
                                         ).then_inc(e_gates_ready, 1)
                    act.wait_ge(e_gates_ready, now.count())
                    for c in range(2):
                        done = nc.scalar.activation(m.x[:, slot, c, :], m.x[:, slot, c, :], ACT.Copy,
                                                    scale=m.gates[:, slot, c:c + 1])
                    done.then_inc(e_scaled, 1)
                now = at.back(4)
                if now.within(e_steps):
                    slot = now.slot(e_ring)
                    act.wait_ge(e_multiplied, now.count(1, 2))
                    act.wait_ge(e_stored[slot], now.uses(e_ring, 16))
                    nc.scalar.copy(m.t[:, slot], m.product(now.slot(2))).then_inc(e_copied, 1)
                    act.wait_ge(e_copied, now.count(1, 2))
                    act.dma_start(table_rows[bass.ds(now.index(), 1)].rearrange("a p c o -> (a p) c o"),
                                  m.t[:, slot]).then_inc(e_stored[slot], 16)
                if at.is_step(3):
                    act.wait_ge(node_w_in, 16)
                    nc.scalar.copy(m.w_node_hi[:], m.w_node_stage[:]).then_inc(node_hi, 1)

            sweep(act, e_ring, e_steps, e_steps, 4, edge_step)
            act.wait_ge(e_multiplied, e_steps + 2)

            def step(at):
                now = at
                if now.within(steps):
                    slot, n = now.slot(2), tiles(now)
                    act.wait_ge(turned, now.count(1, n_ring))
                    act.wait_ge(multiplied, now.count())
                    nc.scalar.copy(m.x_hi[:, slot, :, 0:n * P], m.turned(slot)[:, :, 0:n * P]).then_inc(hi_ready, 1)
                if next_edge and any(at.is_step(n) for n in NEXT_STEPS):
                    part = at.o - NEXT_STEPS[0]
                    if part == 0:
                        act.wait_ge(edge_w_in, 16 * (RELATIONS + len(edge_weights or ())))
                        act.wait_ge(edge_lo, 1)
                    nc.scalar.copy(we_hi[:, 2 * part:2 * part + 2], we_in[:, 2 * part:2 * part + 2]
                                   ).then_inc(edge_hi, 1)
                first, second = at.back(3), at.back(5)
                if norm and (first.within(steps) or (kind == 0 and second.within(steps))):
                    act.wait_ge(var_ready, first.count())
                    nc.scalar.activation(m.std[:], m.var[:], ACT.Sqrt).then_inc(std_ready, 1)
                now = at.back(2)
                if now.within(steps):
                    slot, n = now.slot(3), tiles(now)
                    act.wait_ge(added, now.count(1, 2))
                    if now.is_step(0):
                        act.wait_ge(zeroed, 1)
                    if kind == 1:
                        nc.scalar.activation(m.t[:, slot, 0:n], m.t[:, slot, 0:n], ACT.Relu).then_inc(ready, 1)
                    else:
                        for c in range(n):
                            done = nc.scalar.activation(m.junk[:, c, :], m.t[:, slot, c, :], ACT.Square,
                                                        accum_out=m.sq4[:, at.slot(2), c:c + 1])
                        done.then_inc(squared, 1)
                if kind and at.within(steps):
                    act.wait_ge(added, at.count())
                    if at.is_step(0):
                        act.wait_ge(node_lo, 1)
                    nc.scalar.copy(m.g[:, :, at.slot(2)], m.zeros[:].unsqueeze(2).unsqueeze(3).to_broadcast(
                        [P, RELATIONS, 2, D])).then_inc(cleared, 1)
                now = at.back(3)
                if norm and now.within(steps):
                    slot, n = now.slot(3), tiles(now)
                    act.wait_ge(norm_ready, first.count(1, 1))
                    for c in range(n):
                        done = nc.scalar.activation(m.t[:, slot, c, :], m.t[:, slot, c, :], ACT.Identity,
                                                    bias=m.shift[:, at.slot(2), c:c + 1],
                                                    scale=m.rstd[:, at.slot(2), c:c + 1])
                    done.then_inc(normed if kind == 0 else ready, 1)
                now = at.back(5)
                if kind == 0 and now.within(steps):
                    slot, n = now.slot(2), tiles(now)
                    act.wait_ge(norm_ready, first.count(1, 1))
                    for c in range(n):
                        done = nc.scalar.activation(m.y[:, slot, c, :], m.y[:, slot, c, :], ACT.Identity,
                                                    bias=m.shift[:, at.slot(2), 2 + c:3 + c],
                                                    scale=m.rstd[:, at.slot(2), 2 + c:3 + c])
                    done.then_inc(ready, 1)
                now = at.back(4)
                if kind == 0 and now.within(steps):
                    slot, n = now.slot(2), tiles(now)
                    act.wait_ge(rows_free, now.count(1, n_ring))
                    for c in range(n):
                        done = nc.scalar.activation(m.junk[:, 2 + c, :], m.y[:, slot, c, :], ACT.Square,
                                                    accum_out=m.sq4[:, at.slot(2), 2 + c:3 + c])
                    done.then_inc(resid_squared, 1)

            sweep(act, n_ring, full, steps, 5 if kind == 0 else 3, step)

        inner.close()
        clear(nc, mine)


def main_buffers(nc, ctx, m):
    def sb(name, shape, dt):
        return ctx.enter_context(nc.sbuf_tensor(name, shape, dt))

    m.x = sb("x_rows", [P, 6, 2, D], F32)
    m.x_hi = sb("x_hi", [P, 2, KC, PAIR], F32R)
    m.x_lo = sb("x_lo", [P, 2, KC, PAIR], F32R)
    m.sums = sb("sums", [P, 2, KC, PAIR], F32)
    m.y = m.sums[:].rearrange("p s k r -> p (s k r)").rearrange("p (s c o) -> p s c o", s=2, c=2)
    m.t = sb("t_rows", [P, 4, 2, D], F32)
    m.g = sb("edge_rows", [P, RELATIONS, 2, 2, D], F32)
    m.index = sb("index", [P, 8], I32)
    m.w_edge_stage = sb("w_edge_stage", [P, RELATIONS * KC, D], F32)
    m.w_node_stage = m.g[:, 1].rearrange("p s c o -> p (s c) o")
    m.w_edge_hi = sb("w_edge_hi", [P, RELATIONS * KC, D], F32R)
    m.w_edge_lo = sb("w_edge_lo", [P, RELATIONS * KC, D], F32R)
    m.w_node_hi = sb("w_node_hi", [P, KC, D], F32R)
    m.w_node_lo = sb("w_node_lo", [P, KC, D], F32R)
    m.logits = sb("logits", [P, 4, 2], F32)
    m.gates = sb("gates", [P, 4, 2], F32)
    m.junk = sb("junk_squares", [P, 4, D], BF16)
    m.sum4, m.sq4, m.rstd, m.shift = (sb(f"stats{i}", [P, 2, 4], F32) for i in range(4))
    m.neg_mean, m.mean_sq, m.var, m.std = (sb(f"moments{i}", [P, 4], F32) for i in range(4))
    m.turned = lambda slot: m.psum[:, 2 * slot:2 * slot + 2, :].rearrange("p b (k r) -> p (b k) r", r=PAIR)
    m.product = lambda slot: m.psum[:, 4 + 2 * slot:6 + 2 * slot, :]


def gnn_kernel(nc, x, src, dst, edge_type, w_self_T, w_neigh_T, bias, gamma, beta, basis1, att1, gate_w1, root1, bias1,
               basis2, att2, gate_w2, root2, bias2, out):
    m = Shared()
    with ExitStack() as ctx:
        m.ctx = ctx
        shared(nc, ctx, m)
        m.src, m.dst, m.edge_type = src, dst, edge_type
        m.att, m.basis, m.gate_w = [att1, att2], [basis1, basis2], [gate_w1, gate_w2]
        m.biases, m.gamma, m.beta = [bias, bias1, bias2], gamma, beta
        m.w_made = [nc.dram_tensor(f"w_made{i}", [RELATIONS, D, D], F32).ap() for i in range(2)]
        m.x1 = nc.dram_tensor("x1", [NODES, D], F32).ap()
        m.h = nc.dram_tensor("h", [NODES, D], F32).ap()
        table = nc.dram_tensor("edge_table", [POSITIONS, D], F32).ap()
        prologue(nc, m)
        main_buffers(nc, ctx, m)
        m.node_weights = [w_self_T, root1, root2]
        m.made_weights = [[w[0], w[1]] for w in m.w_made]
        layer(nc, m, 0, x, m.x1, table, [w_neigh_T])
        layer(nc, m, 1, m.x1, m.h, table)
        layer(nc, m, 2, m.h, out, table)


def kernel(x, src, dst, edge_type_2, L0_gnn_w_self, L0_gnn_w_neigh, L0_gnn_bias, L0_gnn_gamma, L0_gnn_beta,
           L1_gnn_basis1, L1_gnn_att1, L1_gnn_gate_w1, L1_gnn_root1, L1_gnn_bias1,
           L1_gnn_basis2, L1_gnn_att2, L1_gnn_gate_w2, L1_gnn_root2, L1_gnn_bias2):
    import concourse.bacc as bacc
    from concourse.bass_utils import run_bass_kernel_spmd

    def spread(att):
        return np.repeat(np.asarray(att).T, QUARTERS, axis=0)

    arrays = {
        "x": x, "src": src, "dst": dst, "edge_type": edge_type_2,
        "w_self_T": np.asarray(L0_gnn_w_self).T, "w_neigh_T": np.asarray(L0_gnn_w_neigh).T,
        "bias": L0_gnn_bias, "gamma": L0_gnn_gamma, "beta": L0_gnn_beta,
        "basis1": L1_gnn_basis1, "att1": spread(L1_gnn_att1), "gate_w1": L1_gnn_gate_w1, "root1": L1_gnn_root1,
        "bias1": L1_gnn_bias1,
        "basis2": L1_gnn_basis2, "att2": spread(L1_gnn_att2), "gate_w2": L1_gnn_gate_w2, "root2": L1_gnn_root2,
        "bias2": L1_gnn_bias2,
    }
    nc = bacc.Bacc("TRN2", target_bir_lowering=False, num_devices=1)
    launch, args = {}, {}
    for name, array in arrays.items():
        array = np.ascontiguousarray(array)
        launch[f"in_{name}"] = array
        args[name] = nc.dram_tensor(f"in_{name}", array.shape, mybir.dt.from_np(array.dtype), kind="ExternalInput").ap()
    out = nc.dram_tensor("out_rows", (NODES, D), F32, kind="ExternalOutput").ap()
    gnn_kernel(nc, out=out, **args)
    result = run_bass_kernel_spmd(nc, [launch], core_ids=[0])
    return result.results[0]["out_rows"]
```

```python
from contextlib import ExitStack

import numpy as np

import concourse.bass as bass
from concourse import mybir

F32 = mybir.dt.float32
F32R = mybir.dt.float32r
BF16 = mybir.dt.bfloat16
I32 = mybir.dt.int32
ALU = mybir.AluOpType
ACT = mybir.ActivationFunctionType

P = 128
D = 512
KC = D // P
PAIR = 2 * P
LN_EPS = 1e-5
RELATIONS = 2

NODES = 10000
NODE_TILES = -(-NODES // P)
NODE_STEPS = -(-NODES // PAIR)
LAST_ROWS = NODES - (NODE_TILES - 1) * P

EDGES = 5000
ET = 40
EP = EDGES // ET
EDGE_STEPS_0 = -(-EDGES // PAIR)
EDGE_STEPS = EDGE_STEPS_0 + 1
POS_TILES = 2 * EDGE_STEPS
POSITIONS = POS_TILES * P
NO_EDGE = float(1 << 20)

BASES = 30
QUARTERS = 4
BP = BASES * QUARTERS
CHUNK_Q = 4
CHUNKS = P // CHUNK_Q
SORTS = range(2)
COUNT_SLOTS = 5
LOOK_SLOTS = 3
SORT_ITER = 4
SORT_TILES = ET // SORT_ITER
CLASSES = (NODE_TILES, RELATIONS * NODE_TILES)
PROLOGUE_CHUNKS = (12, 2)
CHUNKS_BEFORE = PROLOGUE_CHUNKS[0] - 2 * SORT_ITER
EDGE_CHUNKS = CHUNKS - PROLOGUE_CHUNKS[0]
NODE_CHUNKS = CHUNKS - PROLOGUE_CHUNKS[1]


def wide(ap, n):
    return ap.unsqueeze(2).to_broadcast([ap.shape[0], ap.shape[1], n])


class Shared:
    pass


def clear(nc, sems):
    nums = sorted(s.num for s in sems)
    first = nums[0]
    for n, after in zip(nums, nums[1:] + [None]):
        if after != n + 1:
            nc.gpsimd.sem_clear(range(first, n + 1))
            first = after


def deep(ap, n):
    return ap.unsqueeze(1).to_broadcast([ap.shape[0], n, ap.shape[1]])




def prologue(nc, m):
    with ExitStack() as ctx:
        inner = ctx.enter_context(ExitStack())

        def sb(name, shape, dt):
            return ctx.enter_context(nc.sbuf_tensor(name, shape, dt))

        def two(name, shape, dt):
            return [sb(f"{name}{s}", shape, dt) for s in SORTS]

        mine = []

        def sem(name):
            mine.append(ctx.enter_context(nc.semaphore(name)))
            return mine[-1]

        iota_row = sb("iota_row", [P, 160], F32)
        iota_b = sb("iota_b", [P, 160], BF16)
        iota_part = sb("iota_part", [P, 1], F32)
        part_int = sb("part_int", [P, 1], I32)
        quarter = sb("quarter", [P, 1], F32)
        before_edge = sb("before_edge", [EP, EP], F32)
        below = sb("below", [P, P], F32)
        ones = sb("ones", [P, 160], F32)
        dst_i = sb("dst_i", [EP, ET], I32)
        src_i = sb("src_i", [EP, ET], I32)
        type_i = sb("type_i", [EP, ET], I32)
        type_f = sb("type_f", [EP, ET], F32)
        low_i = two("low_i", [EP, ET], I32)
        high_i = two("high_i", [EP, ET], I32)
        low = two("low", [EP, ET], F32)
        klass = two("klass", [EP, ET], F32)
        low_b = two("low_b", [EP, ET], BF16)
        klass_b = two("klass_b", [EP, ET], BF16)
        key = two("key", [EP, ET], F32)
        pay = two("pay", [EP, ET], F32)
        one_low = two("one_low", [EP, ET, P], BF16)
        one_class = [sb(f"one_class{s}", [EP, ET, CLASSES[s]], BF16) for s in SORTS]
        low_row = two("low_row", [P, EDGES], BF16)
        by_tile = two("by_tile", [P, ET, P], BF16)
        low_T = [b[:, :, 0:EP] for b in by_tile]
        key_row = two("key_row", [P, EDGES], F32)
        rank = two("rank", [EP, ET], F32)
        base = two("base", [EP, ET], F32)
        junk = sb("junk", [EP, 2, 2, 160], F32)
        count_hi = [sb(f"count_hi{s}", [P, COUNT_SLOTS, CLASSES[s]], BF16) for s in SORTS]
        count_lo = [sb(f"count_lo{s}", [P, COUNT_SLOTS, CLASSES[s]], BF16) for s in SORTS]
        pos = two("pos", [EP, ET], F32)
        pos_i = two("pos_i", [EP, ET], I32)
        tile_i = two("tile_i", [EP, ET], I32)
        slot_i = two("slot_i", [EP, ET], I32)
        tile_f = two("tile_f", [EP, ET], BF16)
        slot_f = two("slot_f", [EP, ET], BF16)
        one_slot = [b[0:EP] for b in by_tile]
        one_tile = [b[0:EP, 0:ET * POS_TILES].rearrange("p (t u) -> p t u", t=ET) for b in low_row]
        vals = two("vals", [EP, 2, ET], F32)
        vals_hi = two("vals_hi", [EP, 2, ET], BF16)
        vals_lo = two("vals_lo", [EP, 2, ET], BF16)
        put = [r[0:EP, 0:2 * ET * POS_TILES].bitcast(BF16).rearrange("p (t h k u) -> p t h k u", h=2, t=ET, k=2)
               for r in key_row]
        hist = two("hist", [P, CLASSES[1]], F32)
        upto = two("upto", [P, CLASSES[1]], F32)
        start = two("start", [P, CLASSES[1]], F32)
        last = sb("last", [P, CLASSES[1]], F32)
        empty = sb("empty", [P, CLASSES[1]], F32)
        split_i = sb("split_i", [P, 2], I32)
        split_f = sb("split_f", [P, 3], F32)
        keys_out = two("keys_out", [P, 1 + POS_TILES], F32)
        payloads = two("payloads", [P, POS_TILES], F32)
        keys_T = two("keys_T", [POS_TILES, P], F32)
        same_T = two("same_T", [POS_TILES, P], BF16)
        one_before = sb("one_before", [P, P], F32)
        last_to_first = sb("last_to_first", [P, P], F32)
        att = sb("att", [BP, 2, RELATIONS], F32)
        is_quarter = sb("is_quarter", [BP, QUARTERS], F32)
        bias_f = m.same[1][:, 0:2 * 3 * D].bitcast(F32).rearrange("p (n o) -> p n o", n=3)

        ps = m.psum
        ps_count = [ps[:, s, 0:CLASSES[s]] for s in SORTS]
        ps_below = [ps[:, 4 + s, 0:CLASSES[s]] for s in SORTS]
        ps_all = [ps[:, 4 + s, 160:160 + CLASSES[s]] for s in SORTS]
        ps_put = [ps[:, 4 + s, 0:4 * POS_TILES] for s in SORTS]
        ps_keys = [ps[0:POS_TILES, 4 + s, 256:256 + P] for s in SORTS]
        ps_keys_before = [ps[0:POS_TILES, 4 + s, 384:384 + P] for s in SORTS]

        def ps_look(s, k):
            slot = 160 * (k % LOOK_SLOTS)
            return ps[0:EP, 2 + s, slot:slot + CLASSES[s]]

        def each(name):
            return [sem(f"{name}{s}") for s in SORTS]

        def lasting(name):
            return [m.ctx.enter_context(nc.semaphore(f"{name}{s}")) for s in SORTS]

        edges_in = sem("edges_in")
        const_ready = sem("const_ready")
        pool_step = sem("pool_step")
        dve_step = sem("dve_step")
        keys_ready = each("keys_ready")
        keys_stored = lasting("keys_stored")
        rows_in = lasting("rows_in")
        onehot_ready = each("onehot_ready")
        hist_ready = each("hist_ready")
        hist_copied = each("hist_copied")
        sums_ready = each("sums_ready")
        start_ready = each("start_ready")
        counted = each("counted")
        count_hi_ready = each("count_hi_ready")
        count_ready = each("count_ready")
        looked = each("looked")
        one_tile_ready = each("one_tile_ready")
        put_ready = each("put_ready")
        put_lo_ready = each("put_lo_ready")
        put_done = each("put_done")
        keys_out_ready = each("keys_out_ready")
        keys_turned = each("keys_turned")
        same_ready = each("same_ready")
        bias_split = sem("bias_split")
        same_stored = each("same_stored")
        m.same_in = lasting("same_in")
        att_in = sem("att_in")
        mix_ready = sem("mix_ready")
        chunk_in = [sem(f"chunk_in{i}") for i in range(2)]
        mixed = sem("mixed")
        bank_copied = sem("bank_copied")
        made_stored = [sem(f"made_stored{i}") for i in range(2)]
        bias_in = sem("bias_in")
        bias_step = sem("bias_step")

        block = inner.enter_context(nc.Block())

        @block.sync
        def _(sp):
            sp.dma_start(dst_i[:], m.dst.rearrange("(p t) -> p t", t=ET)).then_inc(edges_in, 16)
            sp.dma_start(src_i[:], m.src.rearrange("(p t) -> p t", t=ET)).then_inc(edges_in, 16)
            sp.dma_start(type_i[:], m.edge_type.rearrange("(p t) -> p t", t=ET)).then_inc(edges_in, 16)
            for n in range(2):
                sp.dma_start(att[:, n, :], m.att[n]).then_inc(att_in, 16)
            sp.wait_ge(bias_step, 1)
            for n, vec in enumerate(m.biases):
                sp.dma_start(bias_f[0:1, n, :], vec.unsqueeze(0)).then_inc(bias_in, 16)
                sp.dma_start(bias_f[32:33, n, :], vec.unsqueeze(0)).then_inc(bias_in, 16)
            sp.dma_start(m.gamma_b[:], m.gamma.partition_broadcast(P)).then_inc(bias_in, 16)
            sp.dma_start(m.beta_b[:], m.beta.partition_broadcast(P)).then_inc(bias_in, 16)
            def made_rows_out(n, c):
                sp.wait_ge(bank_copied, n + 3)
                store_made(sp, m, 0, c, n, made_stored)

            first = PROLOGUE_CHUNKS[0]
            for c in range(2):
                load_chunk(sp, m, 0, c, c, chunk_in)
            for s in SORTS:
                sp.wait_ge(rows_in[s], 32)
            with sp.Fori(1, first // 2) as i:
                for c in range(2):
                    sp.wait_ge(mixed, 2 * i + (c - 1))
                    load_chunk(sp, m, 0, c, 2 * i + c, chunk_in)
                    made_rows_out(2 * i + (c - 2), c)
            for c in range(2):
                sp.wait_ge(mixed, first + c - 1)
                load_chunk(sp, m, 1, c, c, chunk_in)
                made_rows_out(first - 2 + c, c)
            for s in SORTS:
                sp.wait_ge(same_ready[s], 1)
                sp.dma_start(m.same_d[s].rearrange("(u v) -> u v", v=P), same_T[s][:]).then_inc(same_stored[s], 16)
                sp.wait_ge(same_stored[s], 16)
                if s:
                    sp.wait_ge(bias_split, 1)
                sp.dma_start(m.same[s][:], m.same_d[s].partition_broadcast(P)).then_inc(m.same_in[s], 16)
            for c in range(2):
                sp.wait_ge(bank_copied, first + c + 3)
                store_made(sp, m, 1, c, c, made_stored)
            for c in range(2):
                sp.wait_ge(made_stored[c], 64 * (sum(PROLOGUE_CHUNKS) // 2 + 1))

        @block.gpsimd
        def _(pool):
            def chain(ins, n=[0]):
                n[0] += 1
                ins.then_inc(pool_step, 1)
                pool.wait_ge(pool_step, n[0])

            pool.iota(iota_row[:], pattern=[[1, 160]], base=0, channel_multiplier=0,
                      allow_small_or_imprecise_dtypes=True)
            pool.iota(iota_b[:], pattern=[[1, 160]], base=0, channel_multiplier=0,
                      allow_small_or_imprecise_dtypes=True)
            pool.iota(iota_part[:], pattern=[[0, 1]], base=0, channel_multiplier=1,
                      allow_small_or_imprecise_dtypes=True)
            pool.iota(part_int[:], pattern=[[0, 1]], base=0, channel_multiplier=1)
            pool.memset(ones[:], 1.0)
            for s in SORTS:
                pool.memset(keys_out[s][:], 0.0)
            pool.memset(m.zeros[:], 0.0)
            pool.memset(m.mix[:], 0.0)
            pool.memset(bias_f, 0.0).then_inc(bias_step, 1)
            pool.memset(m.ident[:], 0.0)
            chain(pool.memset(m.row_pick_f[:], 0.0))
            pool.memset(m.row_pick_f[0:1, :], 1.0)
            chain(pool.memset(m.row_pick_f[32:33, :], 1.0))
            pool.affine_select(out=one_before[:], in_=ones[:, 0:P], compare_op=ALU.is_equal, fill=0.0, base=1,
                               pattern=[[-1, P]], channel_multiplier=1)
            pool.affine_select(out=last_to_first[:], in_=ones[:, 0:P], compare_op=ALU.is_equal, fill=0.0,
                               base=1 - P, pattern=[[-1, P]], channel_multiplier=1)
            pool.affine_select(out=m.ident[:], in_=m.ident[:], compare_op=ALU.not_equal, fill=1.0, base=0,
                               pattern=[[-1, P]], channel_multiplier=1)
            pool.affine_select(out=before_edge[:], in_=ones[0:EP, 0:EP], compare_op=ALU.is_gt, fill=0.0, base=0,
                               pattern=[[-1, EP]], channel_multiplier=1)
            pool.affine_select(out=below[:], in_=ones[:, 0:P], compare_op=ALU.is_gt, fill=0.0, base=0,
                               pattern=[[1, P]], channel_multiplier=-1).then_inc(const_ready, 1)
            for s in SORTS:
                pool.wait_ge(keys_ready[s], 1)
                pool.dma_start(m.key_d[s].rearrange("(p t) -> p t", t=ET), key[s][:]).then_inc(keys_stored[s], 16)
                pool.dma_start(m.low_d[s].rearrange("(p t) -> p t", t=ET), low_b[s][:]).then_inc(keys_stored[s], 16)
            for s in SORTS:
                pool.wait_ge(keys_stored[s], 32)
                pool.dma_start(low_row[s][:], m.low_d[s].partition_broadcast(P)).then_inc(rows_in[s], 16)
                pool.dma_start(key_row[s][:], m.key_d[s].partition_broadcast(P)).then_inc(rows_in[s], 16)
            for s in SORTS:
                pool.wait_ge(one_tile_ready[s], 1)
                for k in range(2):
                    done = pool.tensor_tensor(put[s][:, :, 1, k, :], one_tile[s],
                                              wide(vals_lo[s][:, k, :], POS_TILES), ALU.mult)
                done.then_inc(put_lo_ready[s], 1)

        @block.tensor
        def _(pe):
            pe.sem_inc(bank_copied, 2)

            def basis_chunk(n, c, basis=0):
                pe.wait_ge(chunk_in[c], 8 * (n - c) + 16)
                pe.wait_ge(bank_copied, n + 1)
                basis_group(nc, m, basis, c, 6 + c).then_inc(mixed, 1)

            def histogram_tile(s, t, first=False):
                return nc.tensor.matmul(ps_count[s],
                                        one_low[s][:, bass.ds(t, 1), :].rearrange("p a b -> p (a b)"),
                                        one_class[s][:, bass.ds(t, 1), :].rearrange("p a b -> p (a b)"),
                                        start=first, stop=False, skip_group_check=True)

            pe.wait_ge(const_ready, 1)
            pe.wait_ge(mix_ready, 1)
            for c in range(2):
                basis_chunk(c, c)
            for s in SORTS:
                pe.wait_ge(onehot_ready[s], 1)
                for t in range(4):
                    histogram_tile(s, t, t == 0)
                with pe.Fori(1, ET // 4 - 1) as j:
                    for t in range(4):
                        histogram_tile(s, 4 * j + t)
                for t in range(ET - 4, ET):
                    done = histogram_tile(s, t)
                done.then_inc(hist_ready[s], 1)
            for s in SORTS:
                pe.wait_ge(hist_copied[s], 1)
                n = CLASSES[s]
                nc.tensor.matmul(ps_below[s], below[:], hist[s][:, 0:n], start=True, stop=True)
                nc.tensor.matmul(ps_all[s], ones[:, 0:P], hist[s][:, 0:n], start=True, stop=True
                                 ).then_inc(sums_ready[s], 1)
            for c in range(2):
                basis_chunk(2 + c, c)
            for s in SORTS:
                n = CLASSES[s]
                pe.wait_ge(start_ready[s], 1)
                nc.tensor.matmul(ps_count[s], m.ident[:], start[s][:, 0:n], start=True, stop=False,
                                 skip_group_check=True).then_inc(counted[s], 1)
            with pe.Fori(0, SORT_ITER) as i:
                for k in range(SORT_TILES):
                    t = SORT_TILES * i + k
                    for s in SORTS:
                        pe.wait_ge(count_ready[s], t + 1)
                        look = ps_look(s, k)
                        turned = low_T[s][:, bass.ds(t, 1), :].rearrange("p a b -> p (a b)")
                        nc.tensor.matmul(look, turned, count_hi[s][:, k % COUNT_SLOTS, :], start=True, stop=False,
                                         skip_group_check=True)
                        nc.tensor.matmul(look, turned, count_lo[s][:, k % COUNT_SLOTS, :], start=False, stop=True,
                                         skip_group_check=True).then_inc(looked[s], 1)
                        histogram_tile(s, t).then_inc(counted[s], 1)
                    if k in (3, 8):
                        basis_chunk(2 * i + (CHUNKS_BEFORE + k // 5), k // 5)
            for s in SORTS:
                if s == 0:
                    basis_chunk(PROLOGUE_CHUNKS[0], 0, 1)
                pe.wait_ge(put_ready[s], 1)
                pe.wait_ge(put_lo_ready[s], 1)

                def put_tile(t, first=False):
                    slot = one_slot[s][:, bass.ds(t, 1), :].rearrange("p a b -> p (a b)")
                    return nc.tensor.matmul(ps_put[s], slot,
                                            put[s][:, bass.ds(t, 1)].rearrange("p a h k u -> p (a h k u)"),
                                            start=first, stop=False, skip_group_check=True)

                for t in range(4):
                    put_tile(t, t == 0)
                with pe.Fori(1, ET // 4 - 1) as j:
                    for t in range(4):
                        put_tile(4 * j + t)
                for t in range(ET - 4, ET):
                    done = put_tile(t)
                done.then_inc(put_done[s], 1)
                pe.wait_ge(keys_out_ready[s], 1)
                nc.tensor.matmul(ps_keys[s], keys_out[s][:, 1:], m.ident[:], start=True, stop=True)
                nc.tensor.matmul(ps_keys_before[s], keys_out[s][:, 1:], one_before[:], start=True, stop=False,
                                 skip_group_check=True)
                nc.tensor.matmul(ps_keys_before[s], keys_out[s][:, 0:POS_TILES], last_to_first[:], start=False,
                                 stop=True, skip_group_check=True).then_inc(keys_turned[s], 1)
            basis_chunk(PROLOGUE_CHUNKS[0] + 1, 1, 1)

        @block.scalar
        def _(act):
            for c in range(2):
                act.sem_inc(made_stored[c], 64)

            def made_rows(n, c):
                act.wait_ge(made_stored[c], 32 * (n - c) + 64)
                act.wait_ge(mixed, n + 1)
                nc.scalar.copy(m.made[:, c], ps[:, 6 + c, :]).then_inc(bank_copied, 1)

            for n in range(CHUNKS_BEFORE):
                made_rows(n, n % 2)
            with act.Fori(0, SORT_ITER) as i:
                for k in range(SORT_TILES):
                    for s in SORTS:
                        act.wait_ge(counted[s], SORT_TILES * i + (k + 1))
                        nc.scalar.copy(count_hi[s][:, k % COUNT_SLOTS, :], ps_count[s]).then_inc(count_hi_ready[s], 1)
                    if k in (3, 8):
                        made_rows(2 * i + (CHUNKS_BEFORE + k // 5), k // 5)
            for c in range(2):
                made_rows(PROLOGUE_CHUNKS[0] + c, c)

        @block.vector
        def _(dve):
            v = nc.vector
            steps = [0]

            def chain(ins):
                steps[0] += 1
                ins.then_inc(dve_step, 1)
                dve.wait_ge(dve_step, steps[0])

            dve.wait_ge(edges_in, 48)
            for s in SORTS:
                target, source = (dst_i, src_i) if s == 0 else (src_i, dst_i)
                v.tensor_scalar(low_i[s][:], target[:], P - 1, None, ALU.bitwise_and)
                v.tensor_scalar(high_i[s][:], target[:], 7, None, ALU.logical_shift_right)
                v.tensor_copy(type_f[:], type_i[:])
                chain(v.tensor_copy(pay[s][:], source[:]))
                v.tensor_copy(low[s][:], low_i[s][:])
                chain(v.tensor_copy(klass[s][:], high_i[s][:]))
                if s:
                    chain(v.scalar_tensor_tensor(out=klass[s][:], in0=type_f[:], scalar=float(NODE_TILES),
                                                 in1=klass[s][:], op0=ALU.mult, op1=ALU.add))
                v.tensor_copy(low_b[s][:], low[s][:])
                v.tensor_copy(klass_b[s][:], klass[s][:])
                v.scalar_tensor_tensor(out=key[s][:], in0=klass[s][:], scalar=float(P), in1=low[s][:],
                                       op0=ALU.mult, op1=ALU.add).then_inc(keys_ready[s], 1)
            dve.wait_ge(const_ready, 1)
            chain(v.tensor_scalar(part_int[:], part_int[:], QUARTERS - 1, None, ALU.bitwise_and))
            chain(v.tensor_copy(quarter[:], part_int[:]))
            chain(v.tensor_scalar(is_quarter[:], iota_row[0:BP, 0:QUARTERS], quarter[0:BP, 0:1], None, ALU.is_equal))
            dve.wait_ge(att_in, 32)
            for n in range(2):
                for r in range(RELATIONS):
                    done = v.tensor_scalar(m.mix[:, n, QUARTERS * r:QUARTERS * (r + 1)], is_quarter[:],
                                           att[:, n, r:r + 1], None, ALU.mult)
            done.then_inc(mix_ready, 1)
            for s in SORTS:
                n = CLASSES[s]
                v.tensor_tensor(one_low[s][:], deep(iota_b[0:EP, 0:P], ET), wide(low_b[s][:], P), ALU.is_equal)
                v.tensor_tensor(one_class[s][:], deep(iota_b[0:EP, 0:n], ET), wide(klass_b[s][:], n), ALU.is_equal
                                ).then_inc(onehot_ready[s], 1)
            for s in SORTS:
                dve.wait_ge(rows_in[s], 32)
                v.tensor_scalar(low_T[s], low_row[s][:].rearrange("b (p t) -> b t p", t=ET), iota_part[:, 0:1],
                                None, ALU.is_equal)
                n = CLASSES[s]
                dve.wait_ge(hist_ready[s], 1)
                v.tensor_copy(hist[s][:, 0:n], ps_count[s]).then_inc(hist_copied[s], 1)
            for s in SORTS:
                n = CLASSES[s]
                dve.wait_ge(sums_ready[s], 1)
                chain(v.tensor_tensor_scan(upto[s][:, 0:n], ones[:, 0:n], ps_all[s], 0.0, ALU.mult, ALU.add))
                chain(v.tensor_tensor(start[s][:, 0:n], upto[s][:, 0:n], ps_all[s], ALU.subtract))
                chain(v.tensor_tensor(start[s][:, 0:n], start[s][:, 0:n], ps_below[s], ALU.add))
                if s:
                    edges_0 = upto[s][:, NODE_TILES - 1:NODE_TILES]
                    chain(v.tensor_scalar(split_f[:, 0:1], edges_0, float(PAIR - 1), None, ALU.add))
                    chain(v.tensor_copy(split_i[:, 0:1], split_f[:, 0:1]))
                    chain(v.tensor_scalar(split_i[:, 0:1], split_i[:, 0:1], 8, None, ALU.logical_shift_right))
                    v.tensor_copy(m.pairs_0[:], split_i[:, 0:1])
                    chain(v.tensor_copy(split_f[:, 1:2], split_i[:, 0:1]))
                    chain(v.scalar_tensor_tensor(out=split_f[:, 2:3], in0=split_f[:, 1:2], scalar=float(PAIR),
                                                 in1=edges_0, op0=ALU.mult, op1=ALU.subtract))
                    chain(v.tensor_scalar(start[s][:, NODE_TILES:n], start[s][:, NODE_TILES:n], split_f[:, 2:3],
                                          None, ALU.add))
                dve.sem_inc(start_ready[s], 1)
            key_of = [key_row[s][0:EP, :].rearrange("b (p t) -> b t p", t=ET) for s in SORTS]
            with dve.Fori(0, SORT_ITER) as i:
                for k in range(SORT_TILES):
                    t = SORT_TILES * i + k
                    for s in SORTS:
                        dve.wait_ge(count_hi_ready[s], t + 1)
                        v.tensor_tensor(count_lo[s][:, k % COUNT_SLOTS, :], ps_count[s],
                                        count_hi[s][:, k % COUNT_SLOTS, :], ALU.subtract
                                        ).then_inc(count_ready[s], 1)
                    dve.wait_ge(count_ready[1], t + 1)
                    for s in SORTS:
                        v.scalar_tensor_tensor(out=junk[:, 0, s, 0:EP],
                                               in0=key_of[s][:, bass.ds(t, 1), :].rearrange("b a p -> b (a p)"),
                                               scalar=key[s][:, bass.ds(t, 1)], in1=before_edge[:],
                                               op0=ALU.is_equal, op1=ALU.mult, accum_out=rank[s][:, bass.ds(t, 1)])
                    for s in SORTS:
                        dve.wait_ge(looked[s], t + 1)
                        v.scalar_tensor_tensor(out=junk[:, 1, s, 0:CLASSES[s]],
                                               in0=one_class[s][:, bass.ds(t, 1), :].rearrange("p a b -> p (a b)"),
                                               scalar=1.0, in1=ps_look(s, k),
                                               op0=ALU.mult, op1=ALU.mult, accum_out=base[s][:, bass.ds(t, 1)])
            chain(v.drain())
            for s in SORTS:
                chain(v.tensor_tensor(pos[s][:], base[s][:], rank[s][:], ALU.add))
                chain(v.tensor_copy(pos_i[s][:], pos[s][:]))
                v.tensor_scalar(tile_i[s][:], pos_i[s][:], 7, None, ALU.logical_shift_right)
                v.tensor_scalar(vals[s][:, 0, :], key[s][:], 1.0, None, ALU.add)
                v.tensor_copy(vals[s][:, 1, :], pay[s][:])
                chain(v.tensor_scalar(slot_i[s][:], pos_i[s][:], P - 1, None, ALU.bitwise_and))
                v.tensor_copy(vals_hi[s][:], vals[s][:])
                v.tensor_copy(tile_f[s][:], tile_i[s][:])
                chain(v.tensor_copy(slot_f[s][:], slot_i[s][:]))
                v.tensor_tensor(vals_lo[s][:], vals[s][:], vals_hi[s][:], ALU.subtract)
                v.tensor_tensor(one_tile[s], deep(iota_b[0:EP, 0:POS_TILES], ET), wide(tile_f[s][:], POS_TILES),
                                ALU.is_equal).then_inc(one_tile_ready[s], 1)
                v.tensor_tensor(one_slot[s], deep(iota_b[0:EP, 0:P], ET), wide(slot_f[s][:], P), ALU.is_equal)
                dve.wait_ge(one_tile_ready[s], 1)
                for k in range(2):
                    done = v.tensor_tensor(put[s][:, :, 0, k, :], one_tile[s], wide(vals_hi[s][:, k, :], POS_TILES),
                                           ALU.mult)
                done.then_inc(put_ready[s], 1)
            def masks(s):
                dve.wait_ge(put_done[s], 1)
                v.tensor_copy(keys_out[s][:, 1:], ps_put[s][:, 2 * POS_TILES:3 * POS_TILES])
                chain(v.tensor_copy(payloads[s][:], ps_put[s][:, 3 * POS_TILES:]))
                v.tensor_tensor(m.row_of[s][:], ps_put[s][:, POS_TILES:2 * POS_TILES], payloads[s][:], ALU.add)
                v.tensor_tensor(keys_out[s][:, 1:], ps_put[s][:, 0:POS_TILES], keys_out[s][:, 1:], ALU.add
                                ).then_inc(keys_out_ready[s], 1)
                dve.wait_ge(keys_turned[s], 1)
                chain(v.tensor_copy(keys_T[s][:], ps_keys[s]))
                v.tensor_tensor(same_T[s][:], ps_keys_before[s], keys_T[s][:], ALU.is_equal
                                ).then_inc(same_ready[s], 1)

            masks(0)
            for s in SORTS:
                n = CLASSES[s]
                v.tensor_scalar(empty[:, 0:n], hist[s][:, 0:n], 0.0, NO_EDGE, ALU.is_equal, ALU.mult)
                chain(v.tensor_tensor(last[:, 0:n], start[s][:, 0:n], hist[s][:, 0:n], ALU.add))
                chain(v.scalar_tensor_tensor(out=last[:, 0:n], in0=last[:, 0:n], scalar=-1.0, in1=empty[:, 0:n],
                                             op0=ALU.add, op1=ALU.add))
                chain(v.tensor_copy(m.last_edge[s][:, 0:n], last[:, 0:n]))
            chain(v.tensor_scalar(m.per_edge[:], hist[0][:, 0:NODE_TILES], 1.0, None, ALU.max))
            v.reciprocal(m.per_edge[:], m.per_edge[:])
            dve.wait_ge(bias_in, 16 * (2 * len(m.biases) + 2))
            v.tensor_copy(m.row_pick[:], m.row_pick_f[:])
            chain(v.tensor_copy(m.bias_rows[:], bias_f))
            v.tensor_tensor(m.bias_rows[32:33], bias_f[32:33], m.bias_rows[32:33].bitcast(F32), ALU.subtract
                            ).then_inc(bias_split, 1)
            masks(1)

        inner.close()
        clear(nc, mine)


def shared(nc, ctx, m):
    def sb(name, shape, dt):
        return ctx.enter_context(nc.sbuf_tensor(name, shape, dt))

    m.psum = ctx.enter_context(nc.psum_tensor("psum", [P, 8, 512], F32))
    m.ident = sb("ident", [P, P], F32)
    m.row_pick_f = sb("row_pick_f", [P, P], F32)
    m.row_pick = sb("row_pick", [P, P], F32R)
    m.bias_rows = sb("bias_rows", [P, 3, D], F32R)
    m.gamma_b = sb("gamma_b", [P, D], F32)
    m.beta_b = sb("beta_b", [P, D], F32)
    m.bias_b = m.gamma_b
    m.gate_b = sb("gate_b", [P, RELATIONS * D], F32)
    m.same = [sb(f"same{s}", [P, POSITIONS], BF16) for s in range(2)]
    m.row_of = [sb(f"row_of{s}", [P, POS_TILES], I32) for s in range(2)]
    m.last_edge = [sb(f"last_edge{s}", [P, CLASSES[s]], I32) for s in range(2)]
    m.per_edge = sb("per_edge", [P, NODE_TILES], F32)
    m.pairs_0 = sb("pairs_0", [P, 1], I32)
    m.zeros = sb("zeros", [P, 1], F32)
    m.mix = sb("mix", [BP, 2, 32], F32)
    m.chunk = sb("chunk", [BP, 2, CHUNK_Q * D], F32)
    m.made = sb("made", [P, 2, D], F32)
    m.e_rows_in, m.edges_in = [[[ctx.enter_context(nc.semaphore(f"{name}{kind}_{i}")) for i in range(ring)]
                                for kind, ring in enumerate(rings)]
                               for name, rings in (("e_rows_in", (4, 4, 4)), ("edges_in", (2, 3, 3)))]
    m.key_d = [nc.dram_tensor(f"key_d{s}", [EDGES], F32).ap() for s in range(2)]
    m.low_d = [nc.dram_tensor(f"low_d{s}", [EDGES], BF16).ap() for s in range(2)]
    m.same_d = [nc.dram_tensor(f"same_d{s}", [POSITIONS], BF16).ap() for s in range(2)]


class At:

    def __init__(self, ring, j, o, early=False):
        self.ring, self.j, self.o, self.early = ring, j, o, early

    def back(self, k):
        return At(self.ring, self.j, self.o - k, self.early)

    def count(self, per=1, more=0):
        return per * self.ring * self.j + (per * (self.o + 1) + more)

    def index(self, per=1, more=0):
        return per * self.ring * self.j + (per * self.o + more)

    def slot(self, n):
        return self.o % n

    def uses(self, n, per=1, more=0):
        return per * (self.ring // n) * self.j + (per * (self.o // n + 1) + more)

    def within(self, steps):
        return not isinstance(self.j, int) or 0 <= self.ring * self.j + self.o < steps

    def is_step(self, n):
        return isinstance(self.j, int) and self.ring * self.j + self.o == n


def sweep(eng, ring, full, steps, skew, step, early=0, after_early=None):
    loops = full // ring
    for o in range(ring):
        step(At(ring, 0, o, ring * early > o))
    for lo, hi in ((1, min(early, loops)), (max(early, 1), loops)):
        if lo < hi:
            with eng.Fori(lo, hi) as j:
                for o in range(ring):
                    step(At(ring, j, o, lo < early))
        if lo < early and after_early:
            after_early()
    for o in range(loops * ring, steps + skew):
        step(At(ring, 0, o, ring * early > o))


def load_weights(sp, m, stage, load, loaded):
    for n, w in enumerate(load):
        sp.dma_start(stage[:, n * KC:(n + 1) * KC, :], w.rearrange("(c p) o -> p c o", p=P)).then_inc(loaded, 16)


def product(nc, m, out, slot, c, w_hi, w_lo, bias):
    if bias is not None:
        nc.tensor.matmul(out, m.row_pick[:], m.bias_rows[:, bias, :], start=True, stop=False)
    for k in range(KC):
        hi = m.x_hi[:, slot, k, c * P:(c + 1) * P]
        lo = m.x_lo[:, slot, k, c * P:(c + 1) * P]
        nc.tensor.matmul(out, hi, w_hi(k), start=(bias is None and k == 0), stop=False)
        nc.tensor.matmul(out, hi, w_lo(k), start=False, stop=False)
        done = nc.tensor.matmul(out, lo, w_hi(k), start=False, stop=(k == KC - 1))
    return done


def transposes(nc, m, source, slot, tiles):
    turned = m.turned(slot)
    for c in range(tiles):
        for k in range(KC):
            done = nc.tensor.transpose(turned[:, k, c * P:(c + 1) * P], source[:, c, k * P:(k + 1) * P], m.ident[:])
    return done


def basis_group(nc, m, layer, slot, bank):
    for j in range(4):
        done = nc.tensor.matmul(m.psum[32 * j:32 * j + 32, bank, :], m.mix[:, layer, :],
                                m.chunk[:, slot, j * D:(j + 1) * D], start=True, stop=True)
    return done


def load_chunk(eng, m, layer, slot, chunk, loaded):
    basis_rows = m.basis[layer].rearrange("b (i q) o -> (b i) (q o)", i=QUARTERS)
    eng.dma_start(m.chunk[:, slot, :], basis_rows[:, bass.ds(chunk * (CHUNK_Q * D), CHUNK_Q * D)]
                  ).then_inc(loaded[slot], 16)


def store_made(eng, m, layer, slot, chunk, stored):
    w_rows = m.w_made[layer].rearrange("r (i q) o -> (r i) q o", i=QUARTERS)
    for j in range(CHUNK_Q):
        rows = w_rows[:, bass.ds(CHUNK_Q * chunk + j, 1), :].rearrange("a q o -> a (q o)")
        eng.dma_start(rows, m.made[32 * j:32 * j + RELATIONS * QUARTERS, slot]).then_inc(stored[slot], 16)


def layer(nc, m, kind, source, out, table, edge_weights=None):
    s = 1 if kind else 0
    gated = kind > 0
    relations = RELATIONS if gated else 1
    e_ring, n_ring = 4, 6
    e_steps = EDGE_STEPS if gated else EDGE_STEPS_0
    steps, full = NODE_STEPS, NODES // PAIR
    norm = kind != 1
    x_ring, g_ring = (6, 2) if kind == 0 else (3, 3)
    store_lag = (6, 4, 5)[kind]
    positions = PAIR * e_steps
    e_early, n_early = (EDGE_CHUNKS // e_ring, NODE_CHUNKS // n_ring) if kind == 0 else (0, 0)
    with ExitStack() as ctx:
        inner = ctx.enter_context(ExitStack())
        mine = []

        def sem(what):
            mine.append(ctx.enter_context(nc.semaphore(f"layer{kind}_{what}")))
            return mine[-1]

        e_index_ready = sem("e_index_ready")
        e_index_seen = sem("e_index_seen")
        e_rows_in = m.e_rows_in[kind]
        e_logits_ready = sem("e_logits_ready")
        e_gates_ready = sem("e_gates_ready")
        e_scaled = sem("e_scaled")
        e_turned = sem("e_turned")
        e_summed = sem("e_summed")
        e_hi_ready = sem("e_hi_ready")
        e_lo_ready = sem("e_lo_ready")
        e_multiplied = sem("e_multiplied")
        e_copied = sem("e_copied")
        e_stored = [sem(f"e_stored{i}") for i in range(e_ring)]
        zeroed = sem("zeroed")
        rows_in = [sem(f"rows_in{i}") for i in range(x_ring)]
        rows_free = sem("rows_free")
        extra_in = [sem(f"extra_in{i}") for i in range(2)]
        turned = sem("turned")
        hi_ready = sem("hi_ready")
        lo_ready = sem("lo_ready")
        multiplied = sem("multiplied")
        cleared = sem("cleared")
        index_ready = sem("index_ready")
        index_seen = sem("index_seen")
        edges_in = m.edges_in[kind]
        part_added = sem("part_added")
        added = sem("added")
        squared = sem("squared")
        stat_step = sem("stat_step")
        var_ready = sem("var_ready")
        std_ready = sem("std_ready")
        norm_ready = sem("norm_ready")
        normed = sem("normed")
        gained = sem("gained")
        shifted = sem("shifted")
        resid_squared = sem("resid_squared")
        ready = sem("ready")
        result, result_ring = (m.y, 2) if kind == 0 else (m.t, 3)
        stored = [sem(f"stored{i}") for i in range(result_ring)]
        gate_in = sem("gate_in")
        bias_in = sem("bias_in")
        edge_w_in = sem("edge_w_in")
        node_w_in = sem("node_w_in")
        edge_hi = sem("edge_hi")
        edge_lo = sem("edge_lo")
        node_hi = sem("node_hi")
        node_lo = sem("node_lo")
        basis_in = [sem(f"basis_in{i}") for i in range(2)]
        basis_done = sem("basis_done")
        basis_copied = sem("basis_copied")
        basis_stored = [sem(f"basis_stored{i}") for i in range(2)]

        table_rows = table.rearrange("(q c p) o -> q p c o", c=2, p=P)
        we_hi, we_lo, we_in = m.w_edge_hi, m.w_edge_lo, m.w_edge_stage
        next_edge = kind < 2
        NEXT_STEPS = (4, 5)
        part_chunks = RELATIONS * KC // len(NEXT_STEPS)
        block = inner.enter_context(nc.Block())

        def tiles(now):
            return 1 if now.is_step(steps - 1) else 2

        def rows_of(ap, now):
            if tiles(now) == 1:
                return ap[full * PAIR:NODES, :].unsqueeze(1), LAST_ROWS, 1
            block_rows = ap[0:full * PAIR, :].rearrange("(q c p) o -> q p c o", c=2, p=P)
            return block_rows[bass.ds(now.index(), 1)].rearrange("a p c o -> (a p) c o"), P, 2

        def gathered(now):
            per = 16 * 2 * relations
            if tiles(now) == 1:
                return now.uses(g_ring, per) - per // 2
            return now.uses(g_ring, per)

        def edge_sums(slot):
            return m.x[:, 4:6] if slot == 2 else m.g[:, :, slot]

        def all_edges_stored(eng):
            for slot in range(e_ring):
                eng.wait_ge(e_stored[slot], 16 * len(range(slot, e_steps, e_ring)) + 16)

        @block.sync
        def _(sp):
            if edge_weights:
                load_weights(sp, m, m.w_edge_stage, edge_weights, edge_w_in)
            if gated:
                sp.dma_start(m.gate_b[:], m.gate_w[kind - 1].rearrange("r h o -> (r h o)").partition_broadcast(P)
                             ).then_inc(gate_in, 16)
            if gated:
                sp.wait_ge(e_rows_in[1], 32)
                if kind == 1:
                    sp.dma_start(m.bias_b[:], m.biases[1].partition_broadcast(P)).then_inc(bias_in, 16)
                load_weights(sp, m, m.w_node_stage, [m.node_weights[kind]], node_w_in)

            def edge_step(at):
                if at.within(EDGE_CHUNKS):
                    sp.wait_ge(basis_done, at.count())
                    load_chunk(sp, m, 0, at.slot(2), at.index(1, PROLOGUE_CHUNKS[0]), basis_in)
                if at.is_step(2):
                    load_weights(sp, m, m.w_node_stage, [m.node_weights[kind]], node_w_in)
                now = at.back(1)
                if now.within(EDGE_CHUNKS):
                    sp.wait_ge(basis_copied, now.count())
                    store_made(sp, m, 0, now.slot(2), now.index(1, PROLOGUE_CHUNKS[0]), basis_stored)

            if kind == 0:
                sweep(sp, e_ring, EDGE_CHUNKS, EDGE_CHUNKS, 1, edge_step)
            sp.wait_ge(e_turned, e_steps + e_ring)

            def step(at):
                now = at
                if now.within(steps):
                    rows, p, c = rows_of(source, now)
                    sp.wait_ge(rows_free if kind == 0 else turned, now.count())
                    sp.dma_start(m.x[0:p, now.slot(x_ring), 0:c], rows).then_inc(rows_in[now.slot(x_ring)], 16)
                    if now.early:
                        sp.wait_ge(basis_done, now.count(1, EDGE_CHUNKS))
                        load_chunk(sp, m, 1, now.slot(2), now.index(1, PROLOGUE_CHUNKS[1]), basis_in)
                now = at.back(2)
                if kind == 2 and now.within(steps):
                    rows, p, c = rows_of(m.x1, now)
                    if now.is_step(0):
                        sp.wait_ge(e_lo_ready, e_steps + 1)
                    sp.wait_ge(added, now.count())
                    sp.dma_start(m.y[0:p, now.slot(2), 0:c], rows).then_inc(extra_in[now.slot(2)], 16)
                if at.early and not at.is_step(0):
                    made_rows_out(at.back(1))
                now = at.back(store_lag)
                if now.within(steps):
                    rows, p, c = rows_of(out, now)
                    sp.wait_ge(ready, now.count())
                    sp.dma_start(rows, result[0:p, now.slot(result_ring), 0:c]
                                 ).then_inc(stored[now.slot(result_ring)], 16)
                if next_edge and at.is_step(2):
                    sp.wait_ge(edge_lo, 1)
                    if kind == 0:
                        for slot in range(2):
                            sp.wait_ge(basis_stored[slot], 64 * (EDGE_CHUNKS // 2 + 1))
                    load_weights(sp, m, m.w_edge_stage, m.made_weights[kind], edge_w_in)

            def made_rows_out(now):
                sp.wait_ge(basis_copied, now.count(1, EDGE_CHUNKS))
                store_made(sp, m, 1, now.slot(2), now.index(1, PROLOGUE_CHUNKS[1]), basis_stored)

            sweep(sp, n_ring, full, steps, store_lag, step, n_early, lambda: made_rows_out(At(n_ring, n_early, -1)))
            for slot in range(result_ring):
                sp.wait_ge(stored[slot], 16 * len(range(slot, steps, result_ring)) + 16)
            if kind == 0:
                for slot in range(2):
                    sp.wait_ge(basis_stored[slot], 64 * ((EDGE_CHUNKS + NODE_CHUNKS) // 2 + 1))

        @block.gpsimd
        def _(pool):
            def edge_step(now):
                if not now.within(e_steps):
                    return
                slot = now.slot(e_ring)
                pool.wait_ge(e_turned, now.count())
                nc.gpsimd.tensor_copy(m.index[:, 2 * slot:2 * slot + 2],
                                      m.row_of[s][:, bass.ds(now.index(2), 2)]).then_inc(e_index_ready, 1)
                pool.wait_ge(e_index_ready, now.count())
                pool.sem_inc(e_index_seen, 1)
                for c in range(2):
                    index = m.index[:, 2 * slot + c:2 * slot + c + 1]
                    pool.indirect_dma_start(out=m.x[:, slot, c, :], out_offset=None, in_=source,
                                            in_offset=bass.IndirectOffsetOnAxis(ap=index, axis=0),
                                            bounds_check=NODES - 1, oob_is_err=False).then_inc(e_rows_in[slot], 16)

            sweep(pool, e_ring, e_steps, e_steps, 0, edge_step)
            all_edges_stored(pool)

            def gathers(now):
                slot = now.slot(g_ring)
                n = tiles(now)
                pool.wait_ge(cleared if kind else added, now.count())
                for r in range(relations):
                    done = nc.gpsimd.tensor_copy(
                        m.index[:, 4 * slot + 2 * r:4 * slot + 2 * r + n],
                        m.last_edge[s][:, bass.ds(now.index(2, r * NODE_TILES), n)])
                if kind == 0:
                    done = nc.gpsimd.memset(m.g[:, 0, slot], 0.0)
                done.then_inc(index_ready, 1)
                pool.wait_ge(index_ready, now.count())
                pool.sem_inc(index_seen, 1)
                for r in range(relations):
                    for c in range(n):
                        at_index = 4 * slot + 2 * r + c
                        pool.indirect_dma_start(
                            out=edge_sums(slot)[:, r, c, :], out_offset=None, in_=table[0:positions],
                            in_offset=bass.IndirectOffsetOnAxis(ap=m.index[:, at_index:at_index + 1], axis=0),
                            bounds_check=positions - 1, oob_is_err=False).then_inc(edges_in[slot], 16)

            def step(at):
                if at.within(steps):
                    gathers(at)
                now = at.back(3)
                if kind == 0 and now.within(steps):
                    slot, n = now.slot(3), tiles(now)
                    pool.wait_ge(normed, now.count())
                    nc.gpsimd.tensor_tensor(m.t[:, slot, 0:n], m.t[:, slot, 0:n], deep(m.gamma_b[:], n), ALU.mult
                                            ).then_inc(gained, 1)

            sweep(pool, n_ring, full, steps, 3, step)

        @block.tensor
        def _(pe):
            pe.sem_inc(e_turned, e_ring)
            pe.sem_inc(e_multiplied, 2)
            pe.sem_inc(basis_done, 2)
            if gated:
                pairs_0 = pe.value_load(m.pairs_0[0:1, 0:1], min_val=0, max_val=EDGE_STEPS_0)
            if edge_weights:
                pe.wait_ge(edge_lo, 1)

            def edge_step(at):
                now = at.back(1)
                if now.within(e_steps):
                    if gated:
                        pe.wait_ge(e_scaled, now.count())
                    else:
                        pe.wait_ge(e_rows_in[now.slot(e_ring)], now.uses(e_ring, 32))
                    pe.wait_ge(e_summed, now.count())
                    if kind == 0:
                        pe.wait_ge(basis_copied, now.count() if at.early else EDGE_CHUNKS)
                    transposes(nc, m, m.x[:, now.slot(e_ring)], now.slot(2), 2).then_inc(e_turned, 1)
                relation = 0
                now = at.back(3)
                if now.within(e_steps):
                    pe.wait_ge(e_lo_ready, now.count(1, 1))
                    pe.wait_ge(e_copied, now.count())
                    if gated:
                        relation = (now.index() >= pairs_0) * KC

                def chunk_of(w, k):
                    if not gated:
                        return w[:, k, :]
                    return w[:, bass.ds(relation + k, 1), :].rearrange("p a o -> p (a o)")

                for c in range(2):
                    if now.within(e_steps):
                        done = product(nc, m, m.product(now.slot(2))[:, c, :], now.slot(2), c,
                                       lambda k: chunk_of(we_hi, k), lambda k: chunk_of(we_lo, k), None)
                    if at.early and c == 0:
                        pe.wait_ge(basis_in[at.slot(2)], at.uses(2, 16))
                        pe.wait_ge(e_summed, at.count())
                        basis_group(nc, m, 0, at.slot(2), 2 * at.slot(2)).then_inc(basis_done, 1)
                if now.within(e_steps):
                    done.then_inc(e_multiplied, 1)

            sweep(pe, e_ring, e_steps, e_steps, 3, edge_step, e_early)

            pe.sem_inc(multiplied, 2)
            pe.sem_inc(turned, x_ring)
            pe.wait_ge(e_summed, e_steps + 2)

            def step(at):
                now = at
                if now.within(steps):
                    pe.wait_ge(rows_in[now.slot(x_ring)], now.uses(x_ring, 16))
                    pe.wait_ge(lo_ready, now.count())
                    if kind == 0:
                        pe.wait_ge(basis_copied,
                                   now.index(1, EDGE_CHUNKS) if now.early else EDGE_CHUNKS + NODE_CHUNKS)
                    done = transposes(nc, m, m.x[:, now.slot(x_ring)], now.slot(2), tiles(now))
                    done.then_inc(turned, 1)
                now = at.back(1)
                if now.within(steps):
                    if now.is_step(0):
                        pe.wait_ge(node_lo, 1)
                        pe.wait_ge(e_copied, e_steps + 2)
                    pe.wait_ge(lo_ready, now.count(1, 2))
                    pe.wait_ge(added, now.count())
                for c in range(2):
                    if now.within(steps) and c < tiles(now):
                        done = product(nc, m, m.product(now.slot(2))[:, c, :], now.slot(2), c,
                                       lambda k: m.w_node_hi[:, k, :], lambda k: m.w_node_lo[:, k, :],
                                       None if kind == 1 else kind)
                    if at.early and c == 0:
                        pe.wait_ge(basis_in[at.slot(2)], at.uses(2, 16, 16 * (EDGE_CHUNKS // 2)))
                        pe.wait_ge(lo_ready, at.count(1, 1))
                        basis_group(nc, m, 1, at.slot(2), 2 * (1 - at.slot(2))).then_inc(basis_done, 1)
                if now.within(steps):
                    done.then_inc(multiplied, 1)

            sweep(pe, n_ring, full, steps, 1, step, n_early)

        @block.vector
        def _(dve):
            v = nc.vector
            dve.sem_inc(e_summed, 2)
            dve.sem_inc(e_lo_ready, 1)
            if kind == 0:
                v.memset(m.sum4[:], 0.0)
                v.memset(m.sq4[:], 0.0)
            v.memset(m.sums[:, 1, :, PAIR - 1:PAIR], 0.0).then_inc(zeroed, 1)
            if edge_weights:
                dve.wait_ge(edge_hi, 1)
                v.tensor_tensor(we_lo[:, 0:KC], we_in[:, 0:KC], we_hi[:, 0:KC].bitcast(F32), ALU.subtract
                                ).then_inc(edge_lo, 1)
            else:
                dve.sem_inc(edge_lo, 1)
            if gated:
                pairs_0 = dve.value_load(m.pairs_0[0:1, 0:1], min_val=0, max_val=EDGE_STEPS_0)
            dve.wait_ge(zeroed, 1)
            dve.wait_ge(m.same_in[s], 16)
            if gated:
                dve.wait_ge(gate_in, 16)

            def copy_made(at, more):
                slot = at.slot(2)
                dve.wait_ge(basis_done, at.count(1, 2 + more))
                dve.wait_ge(basis_stored[slot], at.uses(2, 64, 64 * (more // 2)))
                bank = 2 * (slot if more == 0 else 1 - slot)
                v.tensor_copy(m.made[:, slot], m.psum[:, bank, :]).then_inc(basis_copied, 1)

            def edge_step(at):
                now = at.back(2)
                if now.within(e_steps):
                    slot = now.slot(2)
                    dve.wait_ge(e_turned, now.count(1, e_ring))
                    dve.wait_ge(e_lo_ready, now.count())
                    for k in range(KC):
                        done = v.tensor_tensor_scan(m.sums[:, slot, k, :],
                                                    m.same[s][:, bass.ds(now.index(PAIR), PAIR)],
                                                    m.turned(slot)[:, k, :], m.sums[:, 1 - slot, k, PAIR - 1:PAIR],
                                                    ALU.mult, ALU.add)
                    done.then_inc(e_summed, 1)
                if gated and at.within(e_steps):
                    slot = at.slot(e_ring)
                    relation = (at.index() >= pairs_0) * D
                    dve.wait_ge(e_rows_in[slot], at.uses(e_ring, 32))
                    for c in range(2):
                        done = v.scalar_tensor_tensor(out=m.g[:, 0, slot % 2, c, :], in0=m.x[:, slot, c, :],
                                                      scalar=1.0, in1=m.gate_b[:, bass.ds(relation, D)],
                                                      op0=ALU.mult, op1=ALU.mult,
                                                      accum_out=m.logits[:, slot, c:c + 1])
                    done.then_inc(e_logits_ready, 1)
                if now.within(e_steps):
                    slot = now.slot(2)
                    dve.wait_ge(e_hi_ready, now.count())
                    v.tensor_tensor(m.x_lo[:, slot], m.sums[:, slot], m.x_hi[:, slot].bitcast(F32),
                                    ALU.subtract).then_inc(e_lo_ready, 1)
                if at.early:
                    copy_made(at, 0)
                if at.is_step(3):
                    dve.wait_ge(node_hi, 1)
                    v.tensor_tensor(m.w_node_lo[:], m.w_node_stage[:], m.w_node_hi[:].bitcast(F32), ALU.subtract
                                    ).then_inc(node_lo, 1)

            if kind == 0:
                for slot in range(2):
                    dve.sem_inc(basis_stored[slot], 64)
            sweep(dve, e_ring, e_steps, e_steps, 2, edge_step, e_early)

            dve.sem_inc(lo_ready, 2)
            dve.sem_inc(added, 2)
            for slot in range(result_ring):
                dve.sem_inc(stored[slot], 16)
            dve.sem_inc(norm_ready, 1)
            if kind == 0:
                dve.sem_inc(rows_free, n_ring)
            dve.wait_ge(e_lo_ready, e_steps + 1)
            if kind == 1:
                dve.wait_ge(bias_in, 16)

            def moments(at):
                if at.back(3).within(steps):
                    dve.wait_ge(squared, at.back(3).count())
                if kind == 0 and at.back(5).within(steps):
                    dve.wait_ge(resid_squared, at.back(5).count())
                past = at.back(1).slot(2)
                turn = at.back(3).index()
                dve.wait_ge(norm_ready, turn + 1)
                v.tensor_scalar(m.neg_mean[:], m.sum4[:, past], -1.0 / D, None, ALU.mult)
                v.tensor_scalar(m.mean_sq[:], m.sq4[:, past], 1.0 / D, LN_EPS, ALU.mult, ALU.add
                                ).then_inc(stat_step, 1)
                dve.wait_ge(stat_step, 3 * turn + 1)
                v.tensor_tensor(m.var[:], m.neg_mean[:], m.neg_mean[:], ALU.mult).then_inc(stat_step, 1)
                dve.wait_ge(stat_step, 3 * turn + 2)
                v.tensor_tensor(m.var[:], m.mean_sq[:], m.var[:], ALU.subtract).then_inc(var_ready, 1)

            def step(at):
                first, second = at.back(3), at.back(5)
                stats = norm and (first.within(steps) or (kind == 0 and second.within(steps)))
                turn = first.index()
                if stats and kind:
                    moments(at)
                now = at.back(2)
                if now.within(steps):
                    slot, n, t = now.slot(2), tiles(now), now.slot(3)
                    if now.is_step(0):
                        all_edges_stored(dve)
                    dve.wait_ge(multiplied, now.count(1, 2))
                    dve.wait_ge(edges_in[now.slot(g_ring)], gathered(now))
                    edge_rows = edge_sums(now.slot(g_ring))
                    product_of, sums = m.product(slot), m.t[:, t]
                    if kind == 0:
                        if at.back(5).within(steps):
                            dve.wait_ge(rows_free, at.back(5).count(1, n_ring))
                        for c in range(n):
                            done = v.scalar_tensor_tensor(
                                out=sums[:, c, :], in0=edge_rows[:, 0, c, :],
                                scalar=m.per_edge[:, bass.ds(now.index(2, c), 1)], in1=product_of[:, c, :],
                                op0=ALU.mult, op1=ALU.add, accum_out=m.sum4[:, at.slot(2), c:c + 1])
                        done.then_inc(added, 1)
                    else:
                        dve.wait_ge(stored[t], now.uses(3, 16))
                        v.tensor_tensor(sums[:, 0:n], product_of[:, 0:n], edge_rows[:, 0, 0:n], ALU.add
                                        ).then_inc(part_added, 1)
                        dve.wait_ge(part_added, now.count(2, -1))
                        v.tensor_tensor(sums[:, 0:n], sums[:, 0:n], edge_rows[:, 1, 0:n], ALU.add
                                        ).then_inc(part_added, 1)
                        dve.wait_ge(part_added, now.count(2))
                        if kind == 1:
                            v.tensor_tensor(sums[:, 0:n], sums[:, 0:n], deep(m.bias_b[:], n), ALU.add
                                            ).then_inc(added, 1)
                        else:
                            dve.wait_ge(extra_in[slot], now.uses(2, 16))
                            for c in range(n):
                                done = v.scalar_tensor_tensor(
                                    out=sums[:, c, :], in0=sums[:, c, :], scalar=1.0, in1=m.y[:, slot, c, :],
                                    op0=ALU.mult, op1=ALU.add, accum_out=m.sum4[:, at.slot(2), c:c + 1])
                            done.then_inc(added, 1)
                if stats and kind == 0:
                    moments(at)
                if stats:
                    dve.wait_ge(std_ready, first.count())
                    v.reciprocal(m.rstd[:, at.slot(2)], m.std[:]).then_inc(stat_step, 1)
                    dve.wait_ge(stat_step, 3 * turn + 3)
                    v.tensor_tensor(m.shift[:, at.slot(2)], m.neg_mean[:], m.rstd[:, at.slot(2)], ALU.mult
                                    ).then_inc(norm_ready, 1)
                now = at.back(4)
                if kind == 0 and now.within(steps):
                    slot, n = now.slot(3), tiles(now)
                    dve.wait_ge(gained, now.count())
                    v.tensor_tensor(m.t[:, slot, 0:n], m.t[:, slot, 0:n], deep(m.beta_b[:], n), ALU.add
                                    ).then_inc(shifted, 1)
                    dve.wait_ge(shifted, now.count())
                    dve.wait_ge(stored[now.slot(2)], now.uses(2, 16))
                    for c in range(n):
                        done = v.scalar_tensor_tensor(
                            out=m.y[:, now.slot(2), c, :], in0=m.t[:, slot, c, :], scalar=0.0,
                            in1=m.x[:, now.slot(n_ring), c, :], op0=ALU.max, op1=ALU.add,
                            accum_out=m.sum4[:, at.slot(2), 2 + c:3 + c])
                    done.then_inc(rows_free, 1)
                if at.early:
                    copy_made(at, EDGE_CHUNKS)
                now = at
                if now.within(steps):
                    slot, n = now.slot(2), tiles(now)
                    dve.wait_ge(hi_ready, now.count())
                    v.tensor_tensor(m.x_lo[:, slot, :, 0:n * P], m.turned(slot)[:, :, 0:n * P],
                                    m.x_hi[:, slot, :, 0:n * P].bitcast(F32), ALU.subtract).then_inc(lo_ready, 1)
                if next_edge and any(at.is_step(n) for n in NEXT_STEPS):
                    part = NEXT_STEPS.index(at.o)
                    k = slice(part_chunks * part, part_chunks * (part + 1))
                    dve.wait_ge(edge_hi, part + 1 + len(edge_weights or ()))
                    v.tensor_tensor(we_lo[:, k], we_in[:, k], we_hi[:, k].bitcast(F32), ALU.subtract
                                    ).then_inc(edge_lo, 1)

            sweep(dve, n_ring, full, steps, 5 if kind == 0 else 3, step, n_early)

        @block.scalar
        def _(act):
            act.sem_inc(e_copied, 2)
            for slot in range(e_ring):
                act.sem_inc(e_stored[slot], 16)
            if edge_weights:
                act.wait_ge(edge_w_in, 16)
                nc.scalar.copy(we_hi[:, 0:KC], we_in[:, 0:KC]).then_inc(edge_hi, 1)

            def edge_step(at):
                now = at.back(2)
                if now.within(e_steps):
                    slot = now.slot(2)
                    act.wait_ge(e_summed, now.count(1, 2))
                    act.wait_ge(e_multiplied, now.count())
                    nc.scalar.copy(m.x_hi[:, slot], m.sums[:, slot]).then_inc(e_hi_ready, 1)
                now = at
                if gated and now.within(e_steps):
                    slot = now.slot(e_ring)
                    act.wait_ge(e_logits_ready, now.count())
                    nc.scalar.activation(m.gates[:, slot, :], m.logits[:, slot, :], ACT.Sigmoid
                                         ).then_inc(e_gates_ready, 1)
                    act.wait_ge(e_gates_ready, now.count())
                    for c in range(2):
                        done = nc.scalar.activation(m.x[:, slot, c, :], m.x[:, slot, c, :], ACT.Copy,
                                                    scale=m.gates[:, slot, c:c + 1])
                    done.then_inc(e_scaled, 1)
                now = at.back(4)
                if now.within(e_steps):
                    slot = now.slot(e_ring)
                    act.wait_ge(e_multiplied, now.count(1, 2))
                    act.wait_ge(e_stored[slot], now.uses(e_ring, 16))
                    nc.scalar.copy(m.t[:, slot], m.product(now.slot(2))).then_inc(e_copied, 1)
                    act.wait_ge(e_copied, now.count(1, 2))
                    act.dma_start(table_rows[bass.ds(now.index(), 1)].rearrange("a p c o -> (a p) c o"),
                                  m.t[:, slot]).then_inc(e_stored[slot], 16)
                if at.is_step(3):
                    act.wait_ge(node_w_in, 16)
                    nc.scalar.copy(m.w_node_hi[:], m.w_node_stage[:]).then_inc(node_hi, 1)

            sweep(act, e_ring, e_steps, e_steps, 4, edge_step)
            act.wait_ge(e_multiplied, e_steps + 2)

            def step(at):
                now = at
                if now.within(steps):
                    slot, n = now.slot(2), tiles(now)
                    act.wait_ge(turned, now.count(1, x_ring))
                    act.wait_ge(multiplied, now.count())
                    nc.scalar.copy(m.x_hi[:, slot, :, 0:n * P], m.turned(slot)[:, :, 0:n * P]).then_inc(hi_ready, 1)
                if next_edge and any(at.is_step(n) for n in NEXT_STEPS):
                    part = NEXT_STEPS.index(at.o)
                    k = slice(part_chunks * part, part_chunks * (part + 1))
                    if part == 0:
                        act.wait_ge(edge_w_in, 16 * (RELATIONS + len(edge_weights or ())))
                        act.wait_ge(edge_lo, 1)
                    nc.scalar.copy(we_hi[:, k], we_in[:, k]).then_inc(edge_hi, 1)
                first, second = at.back(3), at.back(5)
                if norm and (first.within(steps) or (kind == 0 and second.within(steps))):
                    act.wait_ge(var_ready, first.count())
                    nc.scalar.activation(m.std[:], m.var[:], ACT.Sqrt).then_inc(std_ready, 1)
                if kind and at.within(steps):
                    if at.is_step(0):
                        act.wait_ge(node_lo, 1)
                    else:
                        act.wait_ge(added, at.index(1, 2 + 1 - g_ring))
                    nc.scalar.copy(edge_sums(at.slot(g_ring)), m.zeros[:].unsqueeze(2).unsqueeze(3).to_broadcast(
                        [P, RELATIONS, 2, D])).then_inc(cleared, 1)
                now = at.back(2)
                if now.within(steps):
                    slot, n = now.slot(3), tiles(now)
                    act.wait_ge(added, now.count(1, 2))
                    if now.is_step(0):
                        act.wait_ge(zeroed, 1)
                    if kind == 1:
                        nc.scalar.activation(m.t[:, slot, 0:n], m.t[:, slot, 0:n], ACT.Relu).then_inc(ready, 1)
                    else:
                        for c in range(n):
                            done = nc.scalar.activation(m.junk[:, c, :], m.t[:, slot, c, :], ACT.Square,
                                                        accum_out=m.sq4[:, at.slot(2), c:c + 1])
                        done.then_inc(squared, 1)
                now = at.back(3)
                if norm and now.within(steps):
                    slot, n = now.slot(3), tiles(now)
                    act.wait_ge(norm_ready, first.count(1, 1))
                    for c in range(n):
                        done = nc.scalar.activation(m.t[:, slot, c, :], m.t[:, slot, c, :], ACT.Identity,
                                                    bias=m.shift[:, at.slot(2), c:c + 1],
                                                    scale=m.rstd[:, at.slot(2), c:c + 1])
                    done.then_inc(normed if kind == 0 else ready, 1)
                now = at.back(5)
                if kind == 0 and now.within(steps):
                    slot, n = now.slot(2), tiles(now)
                    act.wait_ge(norm_ready, first.count(1, 1))
                    for c in range(n):
                        done = nc.scalar.activation(m.y[:, slot, c, :], m.y[:, slot, c, :], ACT.Identity,
                                                    bias=m.shift[:, at.slot(2), 2 + c:3 + c],
                                                    scale=m.rstd[:, at.slot(2), 2 + c:3 + c])
                    done.then_inc(ready, 1)
                now = at.back(4)
                if kind == 0 and now.within(steps):
                    slot, n = now.slot(2), tiles(now)
                    act.wait_ge(rows_free, now.count(1, n_ring))
                    for c in range(n):
                        done = nc.scalar.activation(m.junk[:, 2 + c, :], m.y[:, slot, c, :], ACT.Square,
                                                    accum_out=m.sq4[:, at.slot(2), 2 + c:3 + c])
                    done.then_inc(resid_squared, 1)

            sweep(act, n_ring, full, steps, 5 if kind == 0 else 3, step)

        inner.close()
        clear(nc, mine)


def main_buffers(nc, ctx, m):
    def sb(name, shape, dt):
        return ctx.enter_context(nc.sbuf_tensor(name, shape, dt))

    m.x = sb("x_rows", [P, 6, 2, D], F32)
    m.x_hi = sb("x_hi", [P, 2, KC, PAIR], F32R)
    m.x_lo = sb("x_lo", [P, 2, KC, PAIR], F32R)
    m.sums = sb("sums", [P, 2, KC, PAIR], F32)
    m.y = m.sums[:].rearrange("p s k r -> p (s k r)").rearrange("p (s c o) -> p s c o", s=2, c=2)
    m.t = sb("t_rows", [P, 4, 2, D], F32)
    m.g = sb("edge_rows", [P, RELATIONS, 2, 2, D], F32)
    m.index = sb("index", [P, 12], I32)
    m.w_edge_stage = sb("w_edge_stage", [P, RELATIONS * KC, D], F32)
    m.w_node_stage = m.g[:, 1].rearrange("p s c o -> p (s c) o")
    m.w_edge_hi = sb("w_edge_hi", [P, RELATIONS * KC, D], F32R)
    m.w_edge_lo = sb("w_edge_lo", [P, RELATIONS * KC, D], F32R)
    m.w_node_hi = sb("w_node_hi", [P, KC, D], F32R)
    m.w_node_lo = sb("w_node_lo", [P, KC, D], F32R)
    m.logits = sb("logits", [P, 4, 2], F32)
    m.gates = sb("gates", [P, 4, 2], F32)
    m.junk = sb("junk_squares", [P, 4, D], BF16)
    m.sum4, m.sq4, m.rstd, m.shift = (sb(f"stats{i}", [P, 2, 4], F32) for i in range(4))
    m.neg_mean, m.mean_sq, m.var, m.std = (sb(f"moments{i}", [P, 4], F32) for i in range(4))
    m.turned = lambda slot: m.psum[:, 2 * slot:2 * slot + 2, :].rearrange("p b (k r) -> p (b k) r", r=PAIR)
    m.product = lambda slot: m.psum[:, 4 + 2 * slot:6 + 2 * slot, :]


def gnn_kernel(nc, x, src, dst, edge_type, w_self_T, w_neigh_T, bias, gamma, beta, basis1, att1, gate_w1, root1, bias1,
               basis2, att2, gate_w2, root2, bias2, out):
    m = Shared()
    with ExitStack() as ctx:
        m.ctx = ctx
        shared(nc, ctx, m)
        m.src, m.dst, m.edge_type = src, dst, edge_type
        m.att, m.basis, m.gate_w = [att1, att2], [basis1, basis2], [gate_w1, gate_w2]
        m.biases, m.gamma, m.beta = [bias, bias1, bias2], gamma, beta
        m.w_made = [nc.dram_tensor(f"w_made{i}", [RELATIONS, D, D], F32).ap() for i in range(2)]
        m.x1 = nc.dram_tensor("x1", [NODES, D], F32).ap()
        m.h = nc.dram_tensor("h", [NODES, D], F32).ap()
        table = nc.dram_tensor("edge_table", [POSITIONS, D], F32).ap()
        prologue(nc, m)
        main_buffers(nc, ctx, m)
        m.node_weights = [w_self_T, root1, root2]
        m.made_weights = [[w[0], w[1]] for w in m.w_made]
        layer(nc, m, 0, x, m.x1, table, [w_neigh_T])
        layer(nc, m, 1, m.x1, m.h, table)
        layer(nc, m, 2, m.h, out, table)


def kernel(x, src, dst, edge_type_2, L0_gnn_w_self, L0_gnn_w_neigh, L0_gnn_bias, L0_gnn_gamma, L0_gnn_beta,
           L1_gnn_basis1, L1_gnn_att1, L1_gnn_gate_w1, L1_gnn_root1, L1_gnn_bias1,
           L1_gnn_basis2, L1_gnn_att2, L1_gnn_gate_w2, L1_gnn_root2, L1_gnn_bias2):
    import concourse.bacc as bacc
    from concourse.bass_utils import run_bass_kernel_spmd

    def spread(att):
        return np.repeat(np.asarray(att).T, QUARTERS, axis=0)

    arrays = {
        "x": x, "src": src, "dst": dst, "edge_type": edge_type_2,
        "w_self_T": np.asarray(L0_gnn_w_self).T, "w_neigh_T": np.asarray(L0_gnn_w_neigh).T,
        "bias": L0_gnn_bias, "gamma": L0_gnn_gamma, "beta": L0_gnn_beta,
        "basis1": L1_gnn_basis1, "att1": spread(L1_gnn_att1), "gate_w1": L1_gnn_gate_w1, "root1": L1_gnn_root1,
        "bias1": L1_gnn_bias1,
        "basis2": L1_gnn_basis2, "att2": spread(L1_gnn_att2), "gate_w2": L1_gnn_gate_w2, "root2": L1_gnn_root2,
        "bias2": L1_gnn_bias2,
    }
    nc = bacc.Bacc("TRN2", target_bir_lowering=False, num_devices=1)
    launch, args = {}, {}
    for name, array in arrays.items():
        array = np.ascontiguousarray(array)
        launch[f"in_{name}"] = array
        args[name] = nc.dram_tensor(f"in_{name}", array.shape, mybir.dt.from_np(array.dtype), kind="ExternalInput").ap()
    out = nc.dram_tensor("out_rows", (NODES, D), F32, kind="ExternalOutput").ap()
    gnn_kernel(nc, out=out, **args)
    result = run_bass_kernel_spmd(nc, [launch], core_ids=[0])
    return result.results[0]["out_rows"]
```
